# Optimizing a Trainium2 kernel written in Bass

```python
import numpy as np
import jax
import jax.numpy as jnp

def _softmax(x, axis=-1):
    return jax.nn.softmax(x, axis=axis)

def _gelu(x):
    return jax.nn.gelu(x, approximate=True)

def _silu(x):
    return jax.nn.silu(x)

def _sigmoid(x):
    return jax.nn.sigmoid(x)

def _layernorm(x, axis=-1, eps=1e-05):
    m = jnp.mean(x, axis=axis, keepdims=True)
    v = jnp.var(x, axis=axis, keepdims=True)
    return (x - m) / jnp.sqrt(v + eps)

def _scatter_add(tgt, idx, src, axis=0):
    return tgt.at[idx].add(src)

def _segment_sum(src, seg, n):
    return jax.ops.segment_sum(src, seg, n)
kernel_name = 'mk_macaron_d1_jaxref_r8_848dd0'

def setup_inputs(seed: int=0):
    np.random.seed(seed)
    _w = jnp.asarray

    def _L0_attn_setup():
        import jax, jax.numpy as jnp
        import numpy as np
        D_MODEL = 128
        N_HEADS = 16
        N_GROUPS = 4
        D_HEAD = D_MODEL // N_HEADS
        HPG = N_HEADS // N_GROUPS
        B, T = (2, 256)

        def _rope(x):
            t, d = (x.shape[2], x.shape[3])
            pos = jnp.arange(t, dtype=jnp.float32)[:, None]
            freq = jnp.exp(-(jnp.arange(0, d, 2, dtype=jnp.float32) / d) * jnp.log(jnp.float32(10000.0)))
            angle = pos * freq
            cos, sin = (jnp.cos(angle), jnp.sin(angle))
            xe, xo = (x[..., ::2], x[..., 1::2])
            re = xe * cos - xo * sin
            ro = xe * sin + xo * cos
            return jnp.stack([re, ro], axis=-1).reshape(x.shape)
        key = jax.random.key(seed)
        ks = jax.random.split(key, 10)
        s = 0.02
        return {'x': jax.random.normal(ks[0], (B, T, D_MODEL), dtype=jnp.float32), 'Wq': jax.random.normal(ks[1], (D_MODEL, D_MODEL), dtype=jnp.float32) * s, 'bq': jax.random.normal(ks[2], (D_MODEL,), dtype=jnp.float32) * s, 'Wk': jax.random.normal(ks[3], (D_MODEL, N_GROUPS * D_HEAD), dtype=jnp.float32) * s, 'bk': jax.random.normal(ks[4], (N_GROUPS * D_HEAD,), dtype=jnp.float32) * s, 'Wv': jax.random.normal(ks[5], (D_MODEL, N_GROUPS * D_HEAD), dtype=jnp.float32) * s, 'bv': jax.random.normal(ks[6], (N_GROUPS * D_HEAD,), dtype=jnp.float32) * s, 'Wo': jax.random.normal(ks[7], (D_MODEL, D_MODEL), dtype=jnp.float32) * s, 'bo': jax.random.normal(ks[8], (D_MODEL,), dtype=jnp.float32) * s}
    _L0_attn_in = _L0_attn_setup()

    def _L0_ffn_setup():
        import jax, jax.numpy as jnp
        import numpy as np
        DIM = 128
        DEPTH = 6
        HEADS = 16
        DIM_HEAD = 64
        WINDOW = 32
        INNER = HEADS * DIM_HEAD
        DIM_INNER = int(DIM * 4 * 2 / 3)
        QK_SCALE = 8.0

        def shift_tokens(t):
            a, s = jnp.split(t, 2, -1)
            s = jnp.pad(s, ((0, 0), (1, 0), (0, 0)))[:, :-1]
            return jnp.concatenate([a, s], -1)

        def l2norm(t):
            return t / jnp.maximum(jnp.linalg.norm(t, axis=-1, keepdims=True), 1e-12)

        def rotate_half(x):
            x1, x2 = jnp.split(x, 2, -1)
            return jnp.concatenate([-x2, x1], -1)

        def rotary_tables(n):
            half = jnp.arange(0, DIM_HEAD, 2, dtype=jnp.float32)
            inv_freq = 1.0 / 10000.0 ** (half / DIM_HEAD)
            t = jnp.arange(n, dtype=jnp.float32)
            freqs = t[:, None] * inv_freq[None, :]
            freqs = jnp.concatenate([freqs, freqs], -1)
            base_scale = (half + 0.4 * DIM_HEAD) / (1.4 * DIM_HEAD)
            power = (t - n // 2) / (WINDOW // 2)
            scale = base_scale[None, :] ** power[:, None]
            scale = jnp.concatenate([scale, scale], -1)
            return (freqs, scale)

        def local_attention(q, k, v):
            b, h, n, d = q.shape
            w = WINDOW
            nw = n // w
            bq = q.reshape(b, h, nw, w, d)
            bk = k.reshape(b, h, nw, w, d)
            bv = v.reshape(b, h, nw, w, d)

            def look(t):
                p = jnp.pad(t, ((0, 0), (0, 0), (1, 0), (0, 0), (0, 0)))
                return jnp.concatenate([p[:, :, :nw], p[:, :, 1:]], axis=3)
            bk2, bv2 = (look(bk), look(bv))
            seq = jnp.arange(n).reshape(nw, w)
            seq_p = jnp.pad(seq, ((1, 0), (0, 0)), constant_values=-1)
            jt = jnp.concatenate([seq_p[:nw], seq_p[1:]], axis=1)
            it = seq[:, :, None]
            jb = jt[:, None, :]
            mask = (it < jb) | (it > jb + w) | (jb == -1)
            sim = jnp.einsum('bhwie,bhwje->bhwij', bq, bk2) * QK_SCALE
            sim = jnp.where(mask, -jnp.finfo(sim.dtype).max, sim)
            attn = jax.nn.softmax(sim, -1)
            out = jnp.einsum('bhwij,bhwje->bhwie', attn, bv2)
            return out.reshape(b, h, n, d)

        def attn_layer(x, Wqkv, qs, ksc, Wo):
            b, n, _ = x.shape
            qkv = x @ Wqkv
            q, k, v = jnp.split(qkv, 3, -1)
            sh = lambda t: t.reshape(b, n, HEADS, DIM_HEAD).transpose(0, 2, 1, 3)
            q, k, v = (sh(q), sh(k), sh(v))
            q = l2norm(q) * qs
            k = l2norm(k) * ksc
            freqs, scale = rotary_tables(n)
            cos, sin = (jnp.cos(freqs), jnp.sin(freqs))
            q = q * cos * scale + rotate_half(q) * sin * scale
            inv = 1.0 / scale
            k = k * cos * inv + rotate_half(k) * sin * inv
            out = local_attention(q, k, v)
            out = out.transpose(0, 2, 1, 3).reshape(b, n, INNER)
            return out @ Wo

        def ffn_layer(x, g, bln, W1, b1, W2, b2):
            mu = x.mean(-1, keepdims=True)
            var = ((x - mu) ** 2).mean(-1, keepdims=True)
            xn = (x - mu) / jnp.sqrt(var + 1e-05) * g + bln
            hg = xn @ W1 + b1
            a, gate = jnp.split(hg, 2, -1)
            return a * jax.nn.gelu(gate, approximate=False) @ W2 + b2
        key = jax.random.key(seed)
        ks = jax.random.split(key, 8)
        B, N = (2, 256)
        init = lambda k, shape: jax.random.normal(k, shape, jnp.float32) * 0.02
        return {'x': jax.random.normal(ks[0], (B, N, DIM), jnp.float32), 'Wqkv': init(ks[1], (DEPTH, DIM, 3 * INNER)), 'q_scale': jnp.ones((DEPTH, DIM_HEAD), jnp.float32), 'k_scale': jnp.ones((DEPTH, DIM_HEAD), jnp.float32), 'Wo': init(ks[2], (DEPTH, INNER, DIM)), 'ln_g': jnp.ones((DEPTH, DIM), jnp.float32), 'ln_b': jnp.zeros((DEPTH, DIM), jnp.float32), 'W1': init(ks[3], (DEPTH, DIM, 2 * DIM_INNER)), 'b1': jnp.zeros((DEPTH, 2 * DIM_INNER), jnp.float32), 'W2': init(ks[4], (DEPTH, DIM_INNER, DIM)), 'b2': jnp.zeros((DEPTH, DIM), jnp.float32)}
    _L0_ffn_in = _L0_ffn_setup()
    _d = {'L0_attn_x': _L0_attn_in['x'], 'L0_attn_Wq': _L0_attn_in['Wq'], 'L0_attn_bq': _L0_attn_in['bq'], 'L0_attn_Wk': _L0_attn_in['Wk'], 'L0_attn_bk': _L0_attn_in['bk'], 'L0_attn_Wv': _L0_attn_in['Wv'], 'L0_attn_bv': _L0_attn_in['bv'], 'L0_attn_Wo': _L0_attn_in['Wo'], 'L0_attn_bo': _L0_attn_in['bo'], 'L0_ffn_Wqkv': _L0_ffn_in['Wqkv'], 'L0_ffn_q_scale': _L0_ffn_in['q_scale'], 'L0_ffn_k_scale': _L0_ffn_in['k_scale'], 'L0_ffn_Wo': _L0_ffn_in['Wo'], 'L0_ffn_ln_g': _L0_ffn_in['ln_g'], 'L0_ffn_ln_b': _L0_ffn_in['ln_b'], 'L0_ffn_W1': _L0_ffn_in['W1'], 'L0_ffn_b1': _L0_ffn_in['b1'], 'L0_ffn_W2': _L0_ffn_in['W2'], 'L0_ffn_b2': _L0_ffn_in['b2']}
    _x0 = _d['L0_attn_x']
    _d['L0_attn_x'] = jax.random.normal(jax.random.fold_in(jax.random.key(seed), 1), (8, 256, 128), dtype=_x0.dtype)
    del _x0
    return _d

def reference(L0_attn_x, L0_attn_Wq, L0_attn_bq, L0_attn_Wk, L0_attn_bk, L0_attn_Wv, L0_attn_bv, L0_attn_Wo, L0_attn_bo, L0_ffn_Wqkv, L0_ffn_q_scale, L0_ffn_k_scale, L0_ffn_Wo, L0_ffn_ln_g, L0_ffn_ln_b, L0_ffn_W1, L0_ffn_b1, L0_ffn_W2, L0_ffn_b2):

    def _L0_attn_ref(x, Wq, bq, Wk, bk, Wv, bv, Wo, bo):
        import jax, jax.numpy as jnp
        import numpy as np
        D_MODEL = 128
        N_HEADS = 16
        N_GROUPS = 4
        D_HEAD = D_MODEL // N_HEADS
        HPG = N_HEADS // N_GROUPS
        B, T = (2, 256)

        def _rope(x):
            t, d = (x.shape[2], x.shape[3])
            pos = jnp.arange(t, dtype=jnp.float32)[:, None]
            freq = jnp.exp(-(jnp.arange(0, d, 2, dtype=jnp.float32) / d) * jnp.log(jnp.float32(10000.0)))
            angle = pos * freq
            cos, sin = (jnp.cos(angle), jnp.sin(angle))
            xe, xo = (x[..., ::2], x[..., 1::2])
            re = xe * cos - xo * sin
            ro = xe * sin + xo * cos
            return jnp.stack([re, ro], axis=-1).reshape(x.shape)
        b, t, _ = x.shape
        q = (x @ Wq + bq).reshape(b, t, N_HEADS, D_HEAD).transpose(0, 2, 1, 3)
        k = (x @ Wk + bk).reshape(b, t, N_GROUPS, D_HEAD).transpose(0, 2, 1, 3)
        v = (x @ Wv + bv).reshape(b, t, N_GROUPS, D_HEAD).transpose(0, 2, 1, 3)
        k = jnp.repeat(k, HPG, axis=1)
        v = jnp.repeat(v, HPG, axis=1)
        q = _rope(q)
        k = _rope(k)
        scale = jnp.float32(np.sqrt(D_HEAD))
        scores = jnp.einsum('bhtd,bhsd->bhts', q, k) / scale
        causal = jnp.tril(jnp.ones((t, t), dtype=bool))
        scores = jnp.where(causal, scores, -jnp.inf)
        probs = jax.nn.softmax(scores, axis=-1)
        attn = jnp.einsum('bhts,bhsd->bhtd', probs, v)
        out = attn.transpose(0, 2, 1, 3).reshape(b, t, N_HEADS * D_HEAD)
        return out @ Wo + bo

    def _L0_ffn_ref(x, Wqkv, q_scale, k_scale, Wo, ln_g, ln_b, W1, b1, W2, b2):
        import jax, jax.numpy as jnp
        import numpy as np
        DIM = 128
        DEPTH = 6
        HEADS = 16
        DIM_HEAD = 64
        WINDOW = 32
        INNER = HEADS * DIM_HEAD
        DIM_INNER = int(DIM * 4 * 2 / 3)
        QK_SCALE = 8.0

        def shift_tokens(t):
            a, s = jnp.split(t, 2, -1)
            s = jnp.pad(s, ((0, 0), (1, 0), (0, 0)))[:, :-1]
            return jnp.concatenate([a, s], -1)

        def l2norm(t):
            return t / jnp.maximum(jnp.linalg.norm(t, axis=-1, keepdims=True), 1e-12)

        def rotate_half(x):
            x1, x2 = jnp.split(x, 2, -1)
            return jnp.concatenate([-x2, x1], -1)

        def rotary_tables(n):
            half = jnp.arange(0, DIM_HEAD, 2, dtype=jnp.float32)
            inv_freq = 1.0 / 10000.0 ** (half / DIM_HEAD)
            t = jnp.arange(n, dtype=jnp.float32)
            freqs = t[:, None] * inv_freq[None, :]
            freqs = jnp.concatenate([freqs, freqs], -1)
            base_scale = (half + 0.4 * DIM_HEAD) / (1.4 * DIM_HEAD)
            power = (t - n // 2) / (WINDOW // 2)
            scale = base_scale[None, :] ** power[:, None]
            scale = jnp.concatenate([scale, scale], -1)
            return (freqs, scale)

        def local_attention(q, k, v):
            b, h, n, d = q.shape
            w = WINDOW
            nw = n // w
            bq = q.reshape(b, h, nw, w, d)
            bk = k.reshape(b, h, nw, w, d)
            bv = v.reshape(b, h, nw, w, d)

            def look(t):
                p = jnp.pad(t, ((0, 0), (0, 0), (1, 0), (0, 0), (0, 0)))
                return jnp.concatenate([p[:, :, :nw], p[:, :, 1:]], axis=3)
            bk2, bv2 = (look(bk), look(bv))
            seq = jnp.arange(n).reshape(nw, w)
            seq_p = jnp.pad(seq, ((1, 0), (0, 0)), constant_values=-1)
            jt = jnp.concatenate([seq_p[:nw], seq_p[1:]], axis=1)
            it = seq[:, :, None]
            jb = jt[:, None, :]
            mask = (it < jb) | (it > jb + w) | (jb == -1)
            sim = jnp.einsum('bhwie,bhwje->bhwij', bq, bk2) * QK_SCALE
            sim = jnp.where(mask, -jnp.finfo(sim.dtype).max, sim)
            attn = jax.nn.softmax(sim, -1)
            out = jnp.einsum('bhwij,bhwje->bhwie', attn, bv2)
            return out.reshape(b, h, n, d)

        def attn_layer(x, Wqkv, qs, ksc, Wo):
            b, n, _ = x.shape
            qkv = x @ Wqkv
            q, k, v = jnp.split(qkv, 3, -1)
            sh = lambda t: t.reshape(b, n, HEADS, DIM_HEAD).transpose(0, 2, 1, 3)
            q, k, v = (sh(q), sh(k), sh(v))
            q = l2norm(q) * qs
            k = l2norm(k) * ksc
            freqs, scale = rotary_tables(n)
            cos, sin = (jnp.cos(freqs), jnp.sin(freqs))
            q = q * cos * scale + rotate_half(q) * sin * scale
            inv = 1.0 / scale
            k = k * cos * inv + rotate_half(k) * sin * inv
            out = local_attention(q, k, v)
            out = out.transpose(0, 2, 1, 3).reshape(b, n, INNER)
            return out @ Wo

        def ffn_layer(x, g, bln, W1, b1, W2, b2):
            mu = x.mean(-1, keepdims=True)
            var = ((x - mu) ** 2).mean(-1, keepdims=True)
            xn = (x - mu) / jnp.sqrt(var + 1e-05) * g + bln
            hg = xn @ W1 + b1
            a, gate = jnp.split(hg, 2, -1)
            return a * jax.nn.gelu(gate, approximate=False) @ W2 + b2
        for i in range(DEPTH):
            x = attn_layer(shift_tokens(x), Wqkv[i], q_scale[i], k_scale[i], Wo[i]) + x
            x = ffn_layer(shift_tokens(x), ln_g[i], ln_b[i], W1[i], b1[i], W2[i], b2[i]) + x
        return x
    x = L0_attn_x
    x = x + 0.5 * _L0_ffn_ref(_layernorm(x, axis=-1), L0_ffn_Wqkv, L0_ffn_q_scale, L0_ffn_k_scale, L0_ffn_Wo, L0_ffn_ln_g, L0_ffn_ln_b, L0_ffn_W1, L0_ffn_b1, L0_ffn_W2, L0_ffn_b2)
    x = x + _L0_attn_ref(_layernorm(x, axis=-1), L0_attn_Wq, L0_attn_bq, L0_attn_Wk, L0_attn_bk, L0_attn_Wv, L0_attn_bv, L0_attn_Wo, L0_attn_bo)
    x = x + 0.5 * _L0_ffn_ref(_layernorm(x, axis=-1), L0_ffn_Wqkv, L0_ffn_q_scale, L0_ffn_k_scale, L0_ffn_Wo, L0_ffn_ln_g, L0_ffn_ln_b, L0_ffn_W1, L0_ffn_b1, L0_ffn_W2, L0_ffn_b2)
    return x

_drawn_inputs = setup_inputs


def setup_inputs(seed=0):
    import zlib

    import numpy as np

    out = dict(_drawn_inputs(seed))
    spreads = {'L0_ffn_q_scale': (1.0, 0.6),
     'L0_ffn_k_scale': (1.0, 0.6),
     'L0_ffn_ln_g': (1.0, 0.6),
     'L0_ffn_ln_b': (0.0, 0.8),
     'L0_ffn_b1': (0.0, 0.8),
     'L0_ffn_b2': (0.0, 0.1)}
    factors = {'L0_attn_Wq': 8.0,
     'L0_attn_bq': 8.0,
     'L0_attn_Wk': 8.0,
     'L0_attn_bk': 8.0,
     'L0_attn_Wv': 8.0,
     'L0_attn_bv': 8.0,
     'L0_attn_Wo': 8.0,
     'L0_attn_bo': 4.099,
     'L0_ffn_W1': 3.133,
     'L0_ffn_W2': 3.075}
    for name, (base, spread) in spreads.items():
        noise = np.random.default_rng([zlib.crc32(name.encode()), seed]).standard_normal(out[name].shape)
        drawn = base * np.exp(spread * noise) if base else spread * noise
        out[name] = jnp.asarray(drawn.astype(out[name].dtype))
    for name, factor in factors.items():
        out[name] = (out[name] * factor).astype(out[name].dtype)
    return out
```

```python
from contextlib import ExitStack

import numpy as np

import concourse.bass as bass
from concourse import mybir

F32 = mybir.dt.float32
BF16 = mybir.dt.bfloat16
ALU = mybir.AluOpType
ACT = mybir.ActivationFunctionType
AX_X = mybir.AxisListType.X

P = 128
DIM = 128
DEPTH = 6
HEADS = 16
DIM_HEAD = 64
HALF = DIM_HEAD // 2
WINDOW = 32
INNER = HEADS * DIM_HEAD
DIM_INNER = int(DIM * 4 * 2 / 3)
QK_SCALE = 8.0
M_HEADS = 16
M_GROUPS = 4
M_DIM = DIM // M_HEADS
M_REP = M_HEADS // M_GROUPS
B = 8
T = 256
TOKENS = B * T
GH = P // HALF
GROUPS = HEADS // GH
STEPS = B * GROUPS
KEYS = 2 * WINDOW
BAND = P + WINDOW
KPAD = T + WINDOW
CHUNK = 512
CHUNKS = TOKENS // CHUNK
SEQ_PER_CHUNK = CHUNK // T
FFN_ROWS = [128, 128, DIM_INNER - 256]
FFN_BLOCKS = len(FFN_ROWS)
MASKED = -1.0e30
LN_EPS = 1e-5
INV_NORM_MAX = 1e12
SQ_SCALE = 2.0**16
LN2 = 0.6931471805599453
M_CHUNK_HEADS = 4
M_CHUNKS = M_HEADS // M_CHUNK_HEADS


def rotary_constants():
    f = np.float32
    half = np.arange(0, DIM_HEAD, 2, dtype=f)
    inv_freq = f(1.0) / np.power(f(10000.0), half / f(DIM_HEAD))
    t = np.arange(T, dtype=f)
    angle = (t[:, None] * inv_freq[None, :]).astype(f)
    base = ((half + f(0.4 * DIM_HEAD)) / f(1.4 * DIM_HEAD)).astype(f)
    power = ((t - f(T // 2)) / f(WINDOW // 2)).astype(f)
    scale = np.power(base[None, :], power[:, None]).astype(f)
    cos, sin = np.cos(angle), np.sin(angle)
    cq, sq = cos * scale * f(QK_SCALE), sin * scale * f(QK_SCALE)
    ck, sk = cos * (f(1.0) / scale), sin * (f(1.0) / scale)
    rows = np.stack([cq, sq, -sq, ck, sk, -sk]).transpose(2, 0, 1)
    return np.ascontiguousarray(np.tile(rows, (GH, 1, 1)).astype(f))


def window_mask():
    a = np.arange(P)[:, None, None] % WINDOW
    window = np.arange(2)[None, :, None] * (P // WINDOW) + np.arange(P)[:, None, None] // WINDOW
    k = np.arange(KEYS)[None, None, :]
    seen = (k >= a) & (k <= a + WINDOW) & ((window > 0) | (k >= WINDOW))
    return np.where(seen, 0.0, MASKED).astype(np.float32)


def middle_rotary():
    f = np.float32
    freq = np.exp(-(np.arange(0, M_DIM, 2, dtype=f) / f(M_DIM)) * np.log(f(10000.0))).astype(f)
    angle = (np.arange(T, dtype=f)[:, None] * freq).astype(f)
    d = np.arange(P) % M_DIM
    cos, sin = np.cos(angle)[:, d // 2].T, np.sin(angle)[:, d // 2].T
    return np.ascontiguousarray(np.stack([cos, np.where(d % 2 == 0, -1.0, 1.0)[:, None] * sin], 1).astype(f))


def constants():
    f = np.float32
    own_head = (np.arange(P)[:, None] // M_DIM == np.arange(M_HEADS)[None, :]).astype(f)
    causal = np.where(np.arange(P)[None, :] <= np.arange(P)[:, None], 0.0, MASKED).astype(f)
    block = (np.arange(P)[:, None] // HALF == np.arange(P)[None, :] // HALF).astype(f)
    return {
        "identity": np.eye(P, dtype=f),
        "centre": (np.eye(P) - 1.0 / P).astype(f),
        "average": np.full((P, P), 1.0 / P, f),
        "same_head": block,
        "rotary": rotary_constants().reshape(P, -1),
        "mask": window_mask().reshape(P, -1),
        "m_rotary": middle_rotary().reshape(P, -1),
        "own_head": own_head,
        "causal": causal,
    }


def build_macaron(nc, io):
    out = io["out"]
    values = constants()
    const_dram = {n: nc.inline_tensor(v, name="const_" + n).ap() for n, v in values.items()}

    with ExitStack() as ctx:
        def sb(name, shape, dt=F32):
            return ctx.enter_context(nc.sbuf_tensor(name, shape, dt))

        def sem(name):
            return ctx.enter_context(nc.semaphore(name))

        ps_pair = [ctx.enter_context(nc.psum_tensor(f"ps_pair{i}", [P, 2, 512], F32)) for i in range(4)]
        bank = [ps_pair[i // 2][:, i % 2, :] for i in range(8)]

        cst = {n: sb("c_" + n, list(v.shape)) for n, v in values.items()}
        ident = cst["identity"]
        rot = cst["rotary"][:, :].rearrange("p (r t) -> p r t", r=6)
        ident_bf = sb("ident_bf", [P, P], BF16)
        mask_bf = sb("mask_bf", [P, 2, KEYS], BF16)
        causal_bf = sb("causal_bf", [P, P], BF16)
        eps_col = sb("eps_col", [P, 1])
        rnorm_col = sb("rnorm_col", [P, 1])

        xT = sb("xT", [P, TOKENS + T])
        baseT = sb("baseT", [P, TOKENS])
        shifted = sb("shifted", [P, TOKENS])
        normed = sb("normed", [P, TOKENS])

        wqkv = sb("wqkv", [P, 3 * INNER])
        wo = sb("wo", [P, INNER // P, DIM])
        w1 = sb("w1", [P, 2 * DIM_INNER])
        w2 = sb("w2", [P, FFN_BLOCKS, DIM])
        ffn_cols = sb("ffn_cols", [P, 3 + 2 * FFN_BLOCKS])
        b1 = ffn_cols[:, 3:].rearrange("p (a m) -> p a m", a=2)
        qk_cols = sb("qk_cols", [P, 4])

        xs = sb("xs", [P, T])
        tab_a = sb("tab_a", [P, 2, 2, T])
        tab_b = sb("tab_b", [P, 2, 2, T])
        squares = sb("squares", [P, 2, 2, T])
        sqsum = sb("sqsum", [P, 2, T])
        rot_a = sb("rot_a", [P, 2, 2, T])
        rot_b = sb("rot_b", [P, 2, 2, T])
        rotated = sb("rotated", [P, 2, 2, T])
        rnorm = sb("rnorm", [P, 2, T])
        qfin = sb("qfin", [P, 2, T])
        kblock = sb("kblock", [P, 2, GH, KPAD])
        nmax = sb("nmax", [P, 2 * GH])
        probs = sb("probs", [P, 2 * GH, KEYS])
        psum_row = sb("psum_row", [P, 2 * GH])
        prec = sb("prec", [P, 2 * GH])
        band = sb("band", [P, 2 * GH, BAND])
        bandT = sb("bandT", [P, GH, P + WINDOW + P])
        vals = sb("vals", [P, 4, 2, GH * DIM_HEAD])
        outT = sb("outT", [P, INNER // P, T])

        f_sq = sb("f_sq", [P, 2, CHUNK])
        f_rstd = sb("f_rstd", [P, 2, CHUNK])
        f_gelu = sb("f_gelu", [P, FFN_BLOCKS, CHUNK])
        f_h = sb("f_h", [P, 2, FFN_BLOCKS, CHUNK])

        m_w = sb("m_w", [P, 4, P])
        m_wk = sb("m_wk", [P, 2 * M_GROUPS * M_DIM])
        m_wo = sb("m_wo", [P, DIM])
        m_bo = sb("m_bo", [P, 1])
        m_brow = sb("m_brow", [1, 4, P])
        m_bin = sb("m_bin", [1, P + 2 * M_GROUPS * M_DIM])
        ones_row = sb("ones_row", [1, T])
        m_h = xs
        m_rot = rot_a[:, :, :, :].rearrange("p a b t -> p (a b t)")
        m_rope = sb("m_rope", [P, 2, T])
        m_kz = kblock[:, :, :, :].rearrange("p a b t -> p (a b t)")
        m_kblock = sb("m_kblock", [P, M_HEADS, T])
        m_v = sb("m_v", [P, 2, M_GROUPS * M_DIM])
        m_nmax = sb("m_nmax", [P, M_CHUNK_HEADS])
        m_sum = sb("m_sum", [P, M_CHUNK_HEADS])
        m_rec = sb("m_rec", [P, M_CHUNK_HEADS])
        m_e = rot_b[:, :, :, :].rearrange("p a b t -> p (a b) t")
        m_pT = rotated[:, :, :, :].rearrange("p a b t -> p (a b t)").rearrange("p (k h q) -> p k h q", k=2, h=M_CHUNK_HEADS)
        m_o = sb("m_o", [P, 2, DIM])
        m_oT = sb("m_oT", [P, T])

        s = {n: sem(n) for n in (
            "consts_loaded", "x_loaded", "consts_ready", "m_loaded",
            "w_qkv_loaded", "w_o_loaded", "w_scale_loaded", "w_ffn_loaded",
            "x_turned", "x_kept", "out_summed", "out_turned", "out_kept", "out_stored",
            "xs_ready", "tables_ready",
            "qk_ready", "v_ready", "s_ready", "pt_ready", "ss_ready", "pv_ready", "y_ready",
            "squared", "v_saved", "exped", "pt_saved", "ss_logged", "rnorm_ready", "out_saved",
            "rotated_parts", "x_updated", "max_ready", "shifted_scores", "sum_ready", "prec_ready", "qk_final",
            "sqsum_ready", "rotated_ready", "band_ready",
            "f_gate", "f_a", "f_gelued", "f_mixed", "f_y", "f_x",
            "m_copied", "m_qk", "m_parts", "m_roped", "m_kblocked", "m_vdone", "m_vsaved",
            "m_scores", "m_maxed", "m_shifted", "m_exped", "m_summed", "m_recd", "m_probs",
            "m_turned", "m_tsaved", "m_pv", "m_osaved", "m_oturned", "m_otsaved", "m_y", "m_x", "m_prepared",
        )}
        ln_sems = {f: {n: sem(f"{f}_{n}") for n in ("copied", "centred", "squared", "var", "logged", "rstd", "scaled", "normed")}
                   for f in ("ln_in", "ln_mid", "ln_out", "ln_ffn")}

        def chunks_before(stack, layer):
            return CHUNKS * (stack * (DEPTH + 1) + 1) + layer * CHUNKS

        def ln_tensor(pe, q, base, src, started):
            def centre(c):
                if started is not None:
                    pe.wait_ge(started[0], started[1] + (c + 1 if started[2] else 0))
                if c >= 2:
                    pe.wait_ge(q["scaled"], base + c - 1)
                pe.matmul(bank[c % 2], cst["centre"][:, :], src[:, c * CHUNK:(c + 1) * CHUNK],
                          start=True, stop=True).then_inc(q["centred"], 1)

            def variance(c):
                pe.wait_ge(q["squared"], base + c + 1)
                if c >= 2:
                    pe.wait_ge(q["logged"], base + c - 1)
                pe.matmul(bank[2 + c % 2], cst["average"][:, :], f_sq[:, c % 2, :],
                          start=True, stop=True).then_inc(q["var"], 1)

            for c in range(CHUNKS + 1):
                if c < CHUNKS:
                    centre(c)
                if c >= 1:
                    variance(c - 1)

        def ln_scalar(act, q, base):
            def square(c):
                act.wait_ge(q["centred"], base + c + 1)
                if c >= 2:
                    act.wait_ge(q["var"], base + c - 1)
                act.activation(f_sq[:, c % 2, :], bank[c % 2], ACT.Square).then_inc(q["squared"], 1)

            def rstd(c):
                act.wait_ge(q["var"], base + c + 1)
                if c >= 2:
                    act.wait_ge(q["scaled"], base + c - 1)
                act.activation(f_rstd[:, c % 2, :], bank[2 + c % 2], ACT.Ln, bias=eps_col[:, 0:1]).then_inc(q["logged"], 1)
                act.wait_ge(q["logged"], base + c + 1)
                act.activation(f_rstd[:, c % 2, :], f_rstd[:, c % 2, :], ACT.Exp, scale=-0.5).then_inc(q["rstd"], 1)

            for c in range(CHUNKS + 1):
                if c < CHUNKS:
                    square(c)
                if c >= 1:
                    rstd(c - 1)

        def ln_vector(dve, q, base, dst, affine, done=None):
            for c in range(CHUNKS):
                to = dst[:, c * CHUNK:(c + 1) * CHUNK]
                dve.wait_ge(q["rstd"], base + c + 1)
                if affine:
                    nc.vector.scalar_tensor_tensor(out=to, in0=bank[c % 2], scalar=ffn_cols[:, 0:1], in1=f_rstd[:, c % 2, :],
                                                   op0=ALU.mult, op1=ALU.mult).then_inc(q["scaled"], 1)
                    dve.wait_ge(q["scaled"], base + c + 1)
                    nc.vector.tensor_scalar(to, to, ffn_cols[:, 1:2], None, ALU.add).then_inc(q["normed"], 1)
                else:
                    nc.vector.tensor_tensor(to, bank[c % 2], f_rstd[:, c % 2, :], ALU.mult).then_inc(q["scaled"], 1)
                    if done is not None:
                        dve.sem_inc(done, 1)

        block = ctx.enter_context(nc.Block())

        @block.sync
        def _(sp):
            for n in values:
                sp.dma_start(cst[n][:, :], const_dram[n]).then_inc(s["consts_loaded"], 16)
            x_in = io["L0_attn_x"].rearrange("b (h p) d -> p (b h) d", p=P)
            sp.dma_start(normed[:, :].rearrange("p (n d) -> p n d", d=DIM), x_in).then_inc(s["x_loaded"], 16)

            def load_layer(layer, done, final):
                wqkv_l = io["wqkv"][bass.ds(layer, 1), :, :].rearrange("l p n -> p (l n)")
                wo_l = io["L0_ffn_Wo"][bass.ds(layer, 1), :, :].rearrange("l (c p) n -> p (l c) n", p=P)
                w1_l = io["L0_ffn_W1"][bass.ds(layer, 1), :, :].rearrange("l p n -> p (l n)")
                w2_l = io["L0_ffn_W2"][bass.ds(layer, 1), :, :].rearrange("l k n -> (l k) n")
                if done is not None:
                    sp.wait_ge(s["v_ready"], done * STEPS)
                sp.dma_start(wqkv[:, :], wqkv_l).then_inc(s["w_qkv_loaded"], 16)
                if done is not None:
                    sp.wait_ge(s["tables_ready"], done)
                sp.dma_start(qk_cols[:, :], io["qk_cols"][bass.ds(layer, 1), :, :].rearrange("l p n -> p (l n)")).then_inc(s["w_scale_loaded"], 16)
                if done is not None:
                    sp.wait_ge(s["y_ready"], done * B)
                sp.dma_start(wo[:, :, :], wo_l).then_inc(s["w_o_loaded"], 16)
                if final is not None:
                    sp.wait_ge(s["f_x"], final)
                sp.dma_start(w1[:, :], w1_l).then_inc(s["w_ffn_loaded"], 16)
                sp.dma_start(w2[:, 0:2, :], w2_l[0:2 * P, :].rearrange("(c p) n -> p c n", p=P)).then_inc(s["w_ffn_loaded"], 16)
                sp.dma_start(w2[0:FFN_ROWS[2], 2, :], w2_l[2 * P:DIM_INNER, :]).then_inc(s["w_ffn_loaded"], 16)
                sp.dma_start(ffn_cols[:, :], io["ffn_cols"][bass.ds(layer, 1), :, :].rearrange("l p n -> p (l n)")).then_inc(s["w_ffn_loaded"], 16)

            load_layer(0, None, None)
            sp.dma_start(m_w[:, 0, :], io["L0_attn_Wq"]).then_inc(s["m_loaded"], 16)
            sp.dma_start(m_wk[:, 0:32], io["L0_attn_Wk"]).then_inc(s["m_loaded"], 16)
            sp.dma_start(m_wk[:, 32:64], io["L0_attn_Wv"]).then_inc(s["m_loaded"], 16)
            sp.dma_start(m_wo[:, :], io["L0_attn_Wo"]).then_inc(s["m_loaded"], 16)
            sp.dma_start(m_bo[:, :], io["L0_attn_bo"].rearrange("(p a) -> p a", a=1), allow_slow_non_contiguous=True).then_inc(s["m_loaded"], 16)
            sp.dma_start(m_bin[:, 0:128], io["L0_attn_bq"].rearrange("(a p) -> a p", a=1)).then_inc(s["m_loaded"], 16)
            sp.dma_start(m_bin[:, 128:160], io["L0_attn_bk"].rearrange("(a p) -> a p", a=1)).then_inc(s["m_loaded"], 16)
            sp.dma_start(m_bin[:, 160:192], io["L0_attn_bv"].rearrange("(a p) -> a p", a=1)).then_inc(s["m_loaded"], 16)
            with sp.Fori(1, DEPTH) as layer:
                load_layer(layer, layer, chunks_before(0, layer))
            load_layer(0, DEPTH, chunks_before(0, DEPTH))
            with sp.Fori(1, DEPTH) as layer:
                load_layer(layer, layer + DEPTH, chunks_before(1, layer))
            sp.wait_ge(s["out_kept"], 4)
            sp.dma_start(out.rearrange("b (h p) d -> p (b h) d", p=P),
                         normed[:, :].rearrange("p (n d) -> p n d", d=DIM)).then_inc(s["out_stored"], 16)
            sp.wait_ge(s["out_stored"], 16)

        @block.tensor
        def _(pe):
            def proj_qk(S0, g, peeled):
                if not (peeled and g == 0):
                    pe.wait_ge(s["rotated_parts"], S0 + g)
                for i in range(2):
                    for p in range(2):
                        at = i * INNER + (2 * g + p) * P
                        mm = pe.matmul(bank[i][:, p * T:(p + 1) * T],
                                       wqkv[:, at:at + P], xs[:, :],
                                       start=True, stop=True)
                mm.then_inc(s["qk_ready"], 1)

            def proj_v(S0, g, peeled):
                if not (peeled and g < 3):
                    pe.wait_ge(s["out_saved"], S0 + g - 2)
                elif g >= 1:
                    pe.wait_ge(s["v_saved"], S0 + g)
                w = wqkv[:, 2 * INNER + g * GH * DIM_HEAD:2 * INNER + (g + 1) * GH * DIM_HEAD]
                for hf in range(2):
                    mm = pe.matmul(bank[6][:, hf * 256:(hf + 1) * 256], xs[:, hf * P:(hf + 1) * P], w, start=True, stop=True)
                mm.then_inc(s["v_ready"], 1)

            def scores(S0, g, n):
                pe.wait_ge(s["qk_final"], S0 + g)
                if n is None or n >= 2:
                    pe.wait_ge(s["shifted_scores"], S0 + g - 1)
                pe.matmul(bank[3].rearrange("p (f h k) -> p f h k", f=2, h=GH), ident_bf[:, :],
                          mask_bf[:, :, :].unsqueeze(2).broadcast_to((P, 2, GH, KEYS)), start=True, stop=False,
                          skip_group_check=True)
                for hf in range(2):
                    for p in range(2):
                        for j in range(P // WINDOW):
                            w = hf * (P // WINDOW) + j
                            mm = pe.matmul(bank[3][j * WINDOW:(j + 1) * WINDOW, hf * 256:(hf + 1) * 256],
                                           qfin[:, p, w * WINDOW:(w + 1) * WINDOW],
                                           kblock[:, p, :, w * WINDOW:w * WINDOW + KEYS],
                                           start=False, stop=(p == 1), skip_group_check=True)
                mm.then_inc(s["s_ready"], 1)

            def turn_probs(S0, U0, g, n, after_y):
                pe.wait_ge(s["band_ready"], S0 + g - 1)
                if n is None or n >= 3:
                    pe.wait_ge(s["pt_saved"], S0 + g - 2)
                if after_y:
                    pe.wait_ge(s["x_updated"], U0)
                for h in range(GH):
                    pe.transpose(bank[4][:, h * P:(h + 1) * P], band[:, h, WINDOW:BAND], ident[:, :])
                    pe.transpose(bank[5][:, h * P:(h + 1) * P], band[:, GH + h, WINDOW:BAND], ident[:, :])
                flat = band[:, :, :].rearrange("p i k -> p (i k)")
                for h in range(GH):
                    at = (GH + h) * BAND + WINDOW - P
                    mm = pe.transpose(bank[7][:, h * WINDOW:(h + 1) * WINDOW], flat[0:WINDOW, at:at + P], ident[0:WINDOW, 0:WINDOW])
                mm.then_inc(s["pt_ready"], 1)

            def norms(S0, g, peeled):
                pe.wait_ge(s["sqsum_ready"], S0 + g + 1)
                if not (peeled and g == 0):
                    pe.wait_ge(s["ss_logged"], S0 + g)
                pe.matmul(bank[2], cst["same_head"][:, :], sqsum[:, :, :].rearrange("p a t -> p (a t)"),
                          start=True, stop=True).then_inc(s["ss_ready"], 1)

            def attend(S0, g, n, cur):
                pe.wait_ge(s["pt_saved"], S0 + g - 1)
                pe.wait_ge(s["v_saved"], S0 + g + 1 if cur else S0 + g - 1)
                slot = (g - 2) % 4
                for pair in range(GH // 2):
                    for hf in range(2):
                        for odd in range(2):
                            h = 2 * pair + odd
                            to = bank[6][odd * 64:(odd + 1) * 64, pair * T:(pair + 1) * T]
                            v = vals[:, slot, hf, h * DIM_HEAD:(h + 1) * DIM_HEAD]
                            if hf == 0:
                                mm = pe.matmul(to[:, 0:BAND], v, bandT[:, h, 0:BAND], start=True, stop=False, skip_group_check=True)
                            else:
                                mm = pe.matmul(to[:, P:T], v, bandT[:, h, BAND:BAND + P], start=False, stop=True, skip_group_check=True)
                mm.then_inc(s["pv_ready"], 1)

            def project_out(S0, g):
                pe.wait_ge(s["out_saved"], S0 + g - 2)
                for c in range(INNER // P):
                    mm = pe.matmul(bank[7][:, T:2 * T], wo[:, c, :], outT[:, c, :], start=(c == 0), stop=(c == INNER // P - 1))
                mm.then_inc(s["y_ready"], 1)

            def feed_forward(C0):
                q = ln_sems["ln_ffn"]
                ln_tensor(pe, q, C0, shifted, (q["copied"], C0, True))

                def up(c):
                    pe.wait_ge(q["normed"], C0 + c + 1)
                    for part, sems in ((1, "f_gate"), (0, "f_a")):
                        for m, rows in enumerate(FFN_ROWS):
                            o = part * DIM_INNER + m * P
                            if c == 0:
                                pe.wait_ge(q["logged"], C0 + CHUNKS)
                            elif part == 1:
                                pe.wait_ge(s["f_gelued"], (C0 + c - 1) * FFN_BLOCKS + m + 1)
                            else:
                                pe.wait_ge(s["f_mixed"], (C0 + c - 1) * FFN_BLOCKS + m + 1)
                            pe.matmul(bank[(2 if part == 1 else 5) + m][0:rows, :], w1[:, o:o + rows],
                                      normed[:, c * CHUNK:(c + 1) * CHUNK], start=True, stop=True).then_inc(s[sems], 1)

                def down(c, first_x):
                    pe.wait_ge(s["f_mixed"], (C0 + c + 1) * FFN_BLOCKS)
                    if c < 2:
                        pe.wait_ge(q["scaled"], C0 + CHUNKS)
                    else:
                        pe.wait_ge(s["f_x"], first_x + c - 1)
                    for m, rows in enumerate(FFN_ROWS):
                        mm = pe.matmul(bank[c % 2], w2[0:rows, m, :], f_h[0:rows, c % 2, m, :], start=(m == 0), stop=(m == FFN_BLOCKS - 1))
                    mm.then_inc(s["f_y"], 1)

                return up, down

            def layer_body(stack, layer):
                S0 = stack * DEPTH * STEPS + layer * STEPS
                U0 = stack * DEPTH * (B + 1) + layer * (B + 1)
                Y0 = stack * DEPTH * B + layer * B
                C0 = stack * DEPTH * CHUNKS + layer * CHUNKS
                G0 = stack * DEPTH + layer
                pe.wait_ge(s["w_qkv_loaded"], G0 * 16 + 16)
                pe.wait_ge(s["f_x"], chunks_before(stack, layer))
                pe.wait_ge(s["w_o_loaded"], G0 * 16 + 16)
                attn_unit(S0, U0, Y0, True, False)
                with pe.Fori(1, B) as u:
                    attn_unit(S0 + u * GROUPS, U0 + u, Y0 + u, False, False)
                attn_unit(S0 + B * GROUPS, U0 + B, Y0 + B, False, True)
                pe.wait_ge(s["w_ffn_loaded"], G0 * 64 + 64)
                up, down = feed_forward(C0)
                X0 = chunks_before(stack, layer)
                for c in range(CHUNKS + 1):
                    if c < CHUNKS:
                        up(c)
                    if c >= 1:
                        down(c - 1, X0)

            def attn_unit(S0, U0, Y0, first, last):
                for g in range(GROUPS):
                    has1 = (not first or g >= 1) and not (last and g >= 1)
                    has2 = (not first or g >= 2) and not (last and g >= 2)
                    n = g if first else None
                    if not last:
                        if g == 0:
                            pe.wait_ge(s["xs_ready"], U0 + 1)
                        proj_qk(S0, g, first)
                        proj_v(S0, g, first)
                    if not first and g == 2:
                        project_out(S0, g)
                    if has1:
                        scores(S0, g, n)
                    if has2:
                        turn_probs(S0, Y0, g, n, not first and g == 2)
                    if not last:
                        norms(S0, g, first)
                    if has2:
                        attend(S0, g, n, not last)

            pe.wait_ge(s["consts_loaded"], 16 * len(values))
            pe.wait_ge(s["x_loaded"], 16)
            for c in range(CHUNKS):
                for i in range(4):
                    t = c * 4 + i
                    mm = pe.transpose(bank[4 + c][:, i * P:(i + 1) * P], normed[:, t * P:(t + 1) * P], ident[:, :])
                mm.then_inc(s["x_turned"], 1)
            ln_tensor(pe, ln_sems["ln_in"], 0, baseT, (s["x_kept"], 0, True))
            pe.wait_ge(s["consts_ready"], 1)

            with pe.Fori(0, DEPTH) as layer:
                layer_body(0, layer)

            ln_tensor(pe, ln_sems["ln_mid"], 0, baseT, (s["out_summed"], 0, True))
            pe.wait_ge(s["m_prepared"], 1)

            def mid_unit(u):
                C0 = u * 2 * M_CHUNKS
                pe.wait_ge(s["m_copied"], u + 1)
                for i in range(2):
                    for v in range(2):
                        to = bank[i][:, v * T:(v + 1) * T]
                        pe.matmul(to, m_w[:, 2 * i + v, :], m_h[:, :], start=True, stop=False)
                        mm = pe.matmul(to, m_brow[:, 2 * i + v, :], ones_row[:, :], start=False, stop=True)
                mm.then_inc(s["m_qk"], 1)
                pe.wait_ge(s["m_parts"], u * 2 + 2)
                for hf in range(2):
                    to = bank[1][:, hf * 32:(hf + 1) * 32]
                    pe.matmul(to, m_h[:, hf * P:(hf + 1) * P], m_wk[:, 32:64], start=True, stop=False)
                    mm = pe.matmul(to, ones_row[:, 0:P], m_bin[:, 160:192], start=False, stop=True)
                mm.then_inc(s["m_vdone"], 1)
                pe.wait_ge(s["m_kblocked"], u + 1)

                def m_scores(i):
                    hf, c = i // M_CHUNKS, i % M_CHUNKS
                    nk = (hf + 1) * P
                    t = ps_pair[1 + i % 2]
                    if i >= 2:
                        pe.wait_ge(s["m_shifted"], C0 + i - 1)
                    for b in range(2):
                        h = c * M_CHUNK_HEADS + 2 * b
                        to = t[:, b, :].rearrange("p (h k) -> p h k", h=2)
                        pe.matmul(to[:, :, 0:nk], m_rope[:, 0, hf * P:(hf + 1) * P], m_kblock[:, h:h + 2, 0:nk],
                                  start=True, stop=False, skip_group_check=True)
                        mm = pe.matmul(to[:, :, hf * P:nk], ident_bf[:, :], causal_bf[:, :].unsqueeze(1).broadcast_to((P, 2, P)),
                                       start=False, stop=True, skip_group_check=True)
                    mm.then_inc(s["m_scores"], 1)

                def m_turn(i):
                    hf, c = i // M_CHUNKS, i % M_CHUNKS
                    pe.wait_ge(s["m_probs"], C0 + i + 1)
                    if i >= 1:
                        pe.wait_ge(s["m_tsaved"], C0 + i)
                    for kb in range(hf + 1):
                        for h in range(M_CHUNK_HEADS):
                            mm = pe.transpose(ps_pair[3][:, kb, h * P:(h + 1) * P], m_e[:, h, kb * P:(kb + 1) * P], ident[:, :])
                    mm.then_inc(s["m_turned"], 1)

                def m_attend(i):
                    hf, c = i // M_CHUNKS, i % M_CHUNKS
                    pe.wait_ge(s["m_tsaved"], C0 + i + 1)
                    pe.wait_ge(s["m_vsaved"], u + 1)
                    for h in range(M_CHUNK_HEADS):
                        head = c * M_CHUNK_HEADS + h
                        gr = head // M_REP
                        for kb in range(hf + 1):
                            mm = pe.matmul(bank[0][:, hf * P + head * M_DIM:hf * P + (head + 1) * M_DIM], m_pT[:, kb, h, :],
                                           m_v[:, kb, gr * M_DIM:(gr + 1) * M_DIM], start=(kb == 0), stop=(kb == hf))
                    mm.then_inc(s["m_pv"], 1)

                for i in range(2 * M_CHUNKS + 2):
                    if i < 2 * M_CHUNKS:
                        m_scores(i)
                    if 1 <= i <= 2 * M_CHUNKS:
                        m_turn(i - 1)
                    if i >= 2:
                        m_attend(i - 2)
                pe.wait_ge(s["m_osaved"], u + 1)
                for hf in range(2):
                    mm = pe.transpose(bank[0][:, 256 + hf * P:256 + (hf + 1) * P], m_o[:, hf, :], ident[:, :])
                mm.then_inc(s["m_oturned"], 1)
                pe.wait_ge(s["m_otsaved"], u + 1)
                pe.matmul(bank[1][:, T:2 * T], m_wo[:, :], m_oT[:, :], start=True, stop=True).then_inc(s["m_y"], 1)

            mid_unit(0)
            with pe.Fori(1, B) as u:
                pe.wait_ge(s["m_x"], u)
                mid_unit(u)

            ln_tensor(pe, ln_sems["ln_out"], 0, baseT, (s["m_x"], B, False))
            with pe.Fori(0, DEPTH) as layer:
                layer_body(1, layer)

            for c in range(CHUNKS):
                pe.wait_ge(s["out_summed"], CHUNKS + c + 1)
                for i in range(4):
                    t = c * 4 + i
                    mm = pe.transpose(bank[4 + c][:, i * P:(i + 1) * P], baseT[:, t * P:(t + 1) * P], ident[:, :])
                mm.then_inc(s["out_turned"], 1)

        @block.scalar
        def _(act):
            def copy_shifted(u):
                nc.scalar.copy(xs[0:64, :], xT[0:64, bass.ds(u * T, T)])
                nc.scalar.copy(xs[64:P, 1:T], xT[64:P, bass.ds(u * T, T - 1)]).then_inc(s["xs_ready"], 1)

            def step(S0, Y0, u, g, first, last):
                has1 = (not first or g >= 1) and not (last and g >= 1)
                has2 = (not first or g >= 2) and not (last and g >= 2)
                if not last:
                    act.wait_ge(s["qk_ready"], S0 + g + 1)
                    if not (first and g == 0):
                        act.wait_ge(s["sqsum_ready"], S0 + g)
                    nc.scalar.activation(squares[:, :, :, :].rearrange("p a b t -> p a (b t)"), ps_pair[0][:, :, :],
                                         ACT.Square).then_inc(s["squared"], 1)
                    act.wait_ge(s["v_ready"], S0 + g + 1)
                    if not first:
                        act.wait_ge(s["pv_ready"], S0 + g - 3)
                    nc.scalar.copy(vals[:, g, :, :].rearrange("p a n -> p (a n)"), bank[6]).then_inc(s["v_saved"], 1)
                    if g == GROUPS - 1:
                        copy_shifted(u + 1)
                if has1:
                    act.wait_ge(s["shifted_scores"], S0 + g)
                    nc.scalar.activation(probs[:, :, :], probs[:, :, :], ACT.Exp).then_inc(s["exped"], 1)
                if has2:
                    act.wait_ge(s["pt_ready"], S0 + g - 1)
                    if not first or g >= 3:
                        act.wait_ge(s["pv_ready"], S0 + g - 2)
                    nc.scalar.copy(bandT[:, :, 0:P], bank[4].rearrange("p (h q) -> p h q", h=GH))
                    nc.scalar.copy(bandT[:, :, BAND:BAND + P], bank[5].rearrange("p (h q) -> p h q", h=GH))
                    nc.scalar.copy(bandT[:, :, P:BAND], bank[7][:, 0:P].rearrange("p (h q) -> p h q", h=GH)).then_inc(s["pt_saved"], 1)
                if not last:
                    act.wait_ge(s["ss_ready"], S0 + g + 1)
                    if not (first and g == 0):
                        act.wait_ge(s["qk_final"], S0 + g)
                    nc.scalar.activation(rnorm[:, :, :].rearrange("p a t -> p (a t)"), bank[2], ACT.Ln, scale=SQ_SCALE).then_inc(s["ss_logged"], 1)
                    act.wait_ge(s["ss_logged"], S0 + g + 1)
                    nc.scalar.activation(rnorm[:, :, :], rnorm[:, :, :], ACT.Exp, scale=-0.5,
                                         bias=rnorm_col[:, 0:1]).then_inc(s["rnorm_ready"], 1)
                if has2:
                    act.wait_ge(s["pv_ready"], S0 + g - 1)
                    if not first and g == 2:
                        act.wait_ge(s["y_ready"], Y0)
                    gp = (g - 2) % GROUPS
                    nc.scalar.copy(outT[:, 2 * gp:2 * gp + 2, :].rearrange("p a t -> p (a t)"), bank[6]).then_inc(s["out_saved"], 1)

            def layer_body(stack, layer):
                S0 = stack * DEPTH * STEPS + layer * STEPS
                Y0 = stack * DEPTH * B + layer * B
                C0 = stack * DEPTH * CHUNKS + layer * CHUNKS
                G0 = stack * DEPTH + layer
                act.wait_ge(s["f_x"], chunks_before(stack, layer))
                copy_shifted(0)
                for g in range(GROUPS):
                    step(S0, Y0, 0, g, True, False)
                with act.Fori(1, B) as u:
                    for g in range(GROUPS):
                        step(S0 + u * GROUPS, Y0 + u, u, g, False, False)
                for g in range(2):
                    step(S0 + B * GROUPS, Y0 + B, B, g, False, True)
                ln_scalar(act, ln_sems["ln_ffn"], C0)
                act.wait_ge(s["w_ffn_loaded"], G0 * 64 + 64)
                for c in range(CHUNKS):
                    for m, rows in enumerate(FFN_ROWS):
                        act.wait_ge(s["f_gate"], (C0 + c) * FFN_BLOCKS + m + 1)
                        if c >= 1:
                            act.wait_ge(s["f_mixed"], (C0 + c - 1) * FFN_BLOCKS + m + 1)
                        nc.scalar.activation(f_gelu[0:rows, m, :], bank[2 + m][0:rows, :], ACT.Gelu,
                                             bias=b1[0:rows, 1, m:m + 1]).then_inc(s["f_gelued"], 1)

            act.wait_ge(s["consts_ready"], 1)
            ln_scalar(act, ln_sems["ln_in"], 0)
            with act.Fori(0, DEPTH) as layer:
                layer_body(0, layer)

            ln_scalar(act, ln_sems["ln_mid"], 0)

            def mid_unit(u):
                C0 = u * 2 * M_CHUNKS
                act.wait_ge(ln_sems["ln_mid"]["scaled"], CHUNKS)
                nc.scalar.copy(m_h[:, :], xT[:, bass.ds(u * T, T)]).then_inc(s["m_copied"], 1)
                act.wait_ge(s["m_vdone"], u + 1)
                nc.scalar.copy(m_v[:, :, :].rearrange("p a n -> p (a n)"), bank[1][:, 0:64]).then_inc(s["m_vsaved"], 1)
                for i in range(2 * M_CHUNKS):
                    hf = i // M_CHUNKS
                    nk = (hf + 1) * P
                    act.wait_ge(s["m_shifted"], C0 + i + 1)
                    nc.scalar.activation(m_e[:, :, 0:nk], m_e[:, :, 0:nk], ACT.Exp, scale=float(1.0 / np.sqrt(M_DIM))).then_inc(s["m_exped"], 1)
                    act.wait_ge(s["m_turned"], C0 + i + 1)
                    if i >= 1:
                        act.wait_ge(s["m_pv"], C0 + i)
                    nc.scalar.copy(m_pT[:, 0:hf + 1, :, :].rearrange("p k h q -> p k (h q)"),
                                   ps_pair[3][:, 0:hf + 1, :]).then_inc(s["m_tsaved"], 1)
                act.wait_ge(s["m_pv"], C0 + 2 * M_CHUNKS)
                nc.scalar.copy(m_o[:, :, :].rearrange("p a n -> p (a n)"), bank[0][:, 0:256]).then_inc(s["m_osaved"], 1)
                act.wait_ge(s["m_oturned"], u + 1)
                nc.scalar.copy(m_oT[:, :], bank[0][:, 256:512]).then_inc(s["m_otsaved"], 1)

            mid_unit(0)
            with act.Fori(1, B) as u:
                act.wait_ge(s["m_x"], u)
                mid_unit(u)

            ln_scalar(act, ln_sems["ln_out"], 0)
            with act.Fori(0, DEPTH) as layer:
                layer_body(1, layer)

        @block.vector
        def _(dve):
            def tables(G0):
                dve.wait_ge(s["w_scale_loaded"], G0 * 16 + 16)
                for i in range(2):
                    for p in range(2):
                        c = qk_cols[:, 2 * i + p:2 * i + p + 1]
                        nc.vector.tensor_scalar(tab_a[:, i, p, :], rot[:, 3 * i, :], c, None, ALU.mult)
                        last = nc.vector.tensor_scalar(tab_b[:, i, p, :], rot[:, 3 * i + 1 + p, :], c, None, ALU.mult)
                last.then_inc(s["tables_ready"], 1)
                dve.wait_ge(s["tables_ready"], G0 + 1)

            def step(S0, Y0, u, g, first, last):
                has1 = (not first or g >= 1) and not (last and g >= 1)
                if not last:
                    dve.wait_ge(s["squared"], S0 + g + 1)
                    if not (first and g == 0):
                        dve.wait_ge(s["rotated_ready"], S0 + g)
                    qk = ps_pair[0][:, :, :].rearrange("p a n -> p (a n)")
                    nc.vector.tensor_tensor(rot_a[:, :, :, :].rearrange("p a b t -> p (a b t)"), qk,
                                            tab_a[:, :, :, :].rearrange("p a b t -> p (a b t)"), ALU.mult)
                    nc.vector.tensor_tensor(rot_b[:, :, :, :].rearrange("p a b t -> p (a b t)"), qk,
                                            tab_b[:, :, :, :].rearrange("p a b t -> p (a b t)"), ALU.mult).then_inc(s["rotated_parts"], 1)
                if not first and g == 2:
                    dve.wait_ge(s["y_ready"], Y0)
                    at = xT[:, bass.ds((u - 1) * T, T)]
                    nc.vector.tensor_tensor(at, bank[7][:, T:2 * T], at, ALU.add).then_inc(s["x_updated"], 1)
                if has1:
                    dve.wait_ge(s["s_ready"], S0 + g)
                    sc = bank[3].rearrange("p (i k) -> p i k", k=KEYS)
                    nc.vector.tensor_reduce(nmax[:, :], sc, AX_X, ALU.max, negate=True).then_inc(s["max_ready"], 1)
                    dve.wait_ge(s["max_ready"], S0 + g)
                    if not first or g >= 2:
                        dve.wait_ge(s["band_ready"], S0 + g - 1)
                    nc.vector.tensor_tensor(probs[:, :, :], sc, nmax[:, :].unsqueeze(2).broadcast_to((P, 2 * GH, KEYS)),
                                            ALU.add).then_inc(s["shifted_scores"], 1)
                    dve.wait_ge(s["exped"], S0 + g)
                    nc.vector.tensor_reduce(psum_row[:, :], probs[:, :, :], AX_X, ALU.add).then_inc(s["sum_ready"], 1)
                    dve.wait_ge(s["sum_ready"], S0 + g)
                    nc.vector.reciprocal(prec[:, :], psum_row[:, :]).then_inc(s["prec_ready"], 1)
                if not last:
                    dve.wait_ge(s["rotated_ready"], S0 + g + 1)
                    dve.wait_ge(s["rnorm_ready"], S0 + g + 1)
                    if not (first and g == 0):
                        dve.wait_ge(s["s_ready"], S0 + g)
                    nc.vector.scalar_tensor_tensor(out=qfin[:, :, :], in0=rnorm[:, 0:1, :].broadcast_to((P, 2, T)), scalar=INV_NORM_MAX,
                                                   in1=rotated[:, 0, :, :], op0=ALU.min, op1=ALU.mult)
                    for j in range(GH):
                        r = slice(j * HALF, (j + 1) * HALF)
                        fin = nc.vector.scalar_tensor_tensor(out=kblock[r, :, j, WINDOW:KPAD], in0=rnorm[r, 1:2, :].broadcast_to((HALF, 2, T)),
                                                             scalar=INV_NORM_MAX, in1=rotated[r, 1, :, :], op0=ALU.min, op1=ALU.mult)
                    fin.then_inc(s["qk_final"], 1)

            def layer_body(stack, layer):
                S0 = stack * DEPTH * STEPS + layer * STEPS
                Y0 = stack * DEPTH * B + layer * B
                C0 = stack * DEPTH * CHUNKS + layer * CHUNKS
                G0 = stack * DEPTH + layer
                tables(G0)
                for g in range(GROUPS):
                    step(S0, Y0, 0, g, True, False)
                with dve.Fori(1, B) as u:
                    for g in range(GROUPS):
                        step(S0 + u * GROUPS, Y0 + u, u, g, False, False)
                for g in range(3):
                    step(S0 + B * GROUPS, Y0 + B, B, g, False, True)
                dve.wait_ge(s["x_updated"], Y0 + B)
                q = ln_sems["ln_ffn"]
                for c in range(CHUNKS):
                    at = slice(c * CHUNK, (c + 1) * CHUNK)
                    nc.vector.tensor_copy(shifted[0:64, at], xT[0:64, at])
                    nc.vector.tensor_copy(shifted[64:P, at].rearrange("p (b t) -> p b t", t=T)[:, :, 1:T],
                                          xT[64:P, at].rearrange("p (b t) -> p b t", t=T)[:, :, 0:T - 1]).then_inc(q["copied"], 1)
                dve.wait_ge(s["w_ffn_loaded"], G0 * 64 + 64)
                ln_vector(dve, q, C0, normed, True)
                for c in range(CHUNKS + 1):
                    if c < CHUNKS:
                        if c >= 2:
                            dve.wait_ge(s["f_y"], C0 + c - 1)
                        for m, rows in enumerate(FFN_ROWS):
                            n = (C0 + c) * FFN_BLOCKS + m + 1
                            dve.wait_ge(s["f_gelued"], n)
                            dve.wait_ge(s["f_a"], n)
                            nc.vector.scalar_tensor_tensor(out=f_h[0:rows, c % 2, m, :], in0=bank[5 + m][0:rows, :], scalar=b1[0:rows, 0, m:m + 1],
                                                           in1=f_gelu[0:rows, m, :], op0=ALU.add, op1=ALU.mult).then_inc(s["f_mixed"], 1)
                    if c >= 1:
                        dve.wait_ge(s["f_y"], C0 + c)
                        at = xT[:, (c - 1) * CHUNK:c * CHUNK]
                        nc.vector.scalar_tensor_tensor(out=at, in0=bank[(c - 1) % 2], scalar=ffn_cols[:, 2:3], in1=at,
                                                       op0=ALU.add, op1=ALU.add).then_inc(s["f_x"], 1)

            def add_half(stack):
                dve.wait_ge(s["f_x"], chunks_before(stack, DEPTH))
                for c in range(CHUNKS):
                    at = slice(c * CHUNK, (c + 1) * CHUNK)
                    nc.vector.scalar_tensor_tensor(out=baseT[:, at], in0=xT[:, at], scalar=0.5, in1=baseT[:, at],
                                                   op0=ALU.mult, op1=ALU.add).then_inc(s["out_summed"], 1)

            dve.wait_ge(s["consts_loaded"], 16 * len(values))
            nc.vector.tensor_copy(ident_bf[:, :], ident[:, :])
            nc.vector.tensor_copy(mask_bf[:, :, :].rearrange("p f k -> p (f k)"), cst["mask"][:, :])
            nc.vector.tensor_copy(causal_bf[:, :], cst["causal"][:, :])
            nc.vector.memset(eps_col[:, :], LN_EPS)
            nc.vector.memset(rnorm_col[:, :], 0.5 * LN2 * float(np.log2(SQ_SCALE)))
            nc.vector.memset(kblock[:, :, :, :], 0.0)
            nc.vector.memset(band[:, :, :], 0.0)
            nc.vector.memset(xs[:, :], 0.0)
            nc.vector.memset(shifted[:, :], 0.0)
            nc.vector.memset(ones_row[:, :], 1.0)
            nc.vector.memset(xT[:, TOKENS:TOKENS + T], 0.0).then_inc(s["consts_ready"], 1)
            dve.wait_ge(s["consts_ready"], 1)
            for c in range(CHUNKS):
                dve.wait_ge(s["x_turned"], c + 1)
                nc.vector.tensor_copy(baseT[:, c * CHUNK:(c + 1) * CHUNK], bank[4 + c]).then_inc(s["x_kept"], 1)
            ln_vector_plain(dve, nc, ln_sems["ln_in"], bank, f_rstd, xT, s["f_x"])
            with dve.Fori(0, DEPTH) as layer:
                layer_body(0, layer)
            add_half(0)

            ln_vector(dve, ln_sems["ln_mid"], 0, xT, False)
            dve.wait_ge(s["m_loaded"], 16 * 8)
            pairs = "p (n two) -> p n two"
            for to, frm in ((m_w[:, 1, :], m_w[:, 0, :]), (m_brow[:, 1, :], m_bin[:, 0:128])):
                t2, f2 = to.rearrange(pairs, two=2), frm.rearrange(pairs, two=2)
                nc.vector.tensor_copy(t2[:, :, 0:1], f2[:, :, 1:2])
                nc.vector.tensor_copy(t2[:, :, 1:2], f2[:, :, 0:1])
            nc.vector.tensor_copy(m_brow[:, 0, :], m_bin[:, 0:128])
            for rows, to, frm in ((P, m_w, m_wk[:, 0:32]), (1, m_brow, m_bin[:, 128:160])):
                for rep in range(M_REP):
                    t3 = to[:, 2, :].rearrange("p (g r d) -> p g r d", r=M_REP, d=M_DIM)[:, :, rep, :]
                    s3 = to[:, 3, :].rearrange("p (g r d) -> p g r d", r=M_REP, d=M_DIM)[:, :, rep, :]
                    f3 = frm.rearrange("p (g d) -> p g d", d=M_DIM)
                    nc.vector.tensor_copy(t3, f3)
                    for a in range(2):
                        last = nc.vector.tensor_copy(s3.rearrange("p g (n two) -> p g n two", two=2)[:, :, :, a],
                                                     f3.rearrange("p g (n two) -> p g n two", two=2)[:, :, :, 1 - a])
            last.then_inc(s["m_prepared"], 1)

            def mid_unit(u):
                C0 = u * 2 * M_CHUNKS
                dve.wait_ge(s["m_qk"], u + 1)
                for i in range(2):
                    nc.vector.tensor_tensor(m_rot[:, i * 512:(i + 1) * 512], bank[i], cst["m_rotary"][:, :], ALU.mult).then_inc(s["m_parts"], 1)
                dve.wait_ge(s["m_parts"], u * 2 + 2)
                parts = m_rot.rearrange("p (i v t) -> p i v t", i=2, v=2)
                nc.vector.tensor_tensor(m_rope[:, :, :], parts[:, :, 0, :], parts[:, :, 1, :], ALU.add).then_inc(s["m_roped"], 1)
                dve.wait_ge(s["m_roped"], u + 1)
                nc.vector.tensor_tensor(m_kblock[:, :, :], m_rope[:, 1:2, :].broadcast_to((P, M_HEADS, T)),
                                        cst["own_head"][:, :].unsqueeze(2).broadcast_to((P, M_HEADS, T)), ALU.mult).then_inc(s["m_kblocked"], 1)
                for i in range(2 * M_CHUNKS):
                    hf = i // M_CHUNKS
                    nk = (hf + 1) * P
                    dve.wait_ge(s["m_scores"], C0 + i + 1)
                    sc = ps_pair[1 + i % 2][:, :, :].rearrange("p a (h k) -> p (a h) k", h=2)[:, :, 0:nk]
                    e = m_e[:, :, 0:nk]
                    nc.vector.tensor_reduce(m_nmax[:, :], sc, AX_X, ALU.max, negate=True).then_inc(s["m_maxed"], 1)
                    dve.wait_ge(s["m_maxed"], C0 + i + 1)
                    if i >= 1:
                        dve.wait_ge(s["m_turned"], C0 + i)
                    nc.vector.tensor_tensor(e, sc, m_nmax[:, :].unsqueeze(2).broadcast_to((P, M_CHUNK_HEADS, nk)), ALU.add).then_inc(s["m_shifted"], 1)
                    dve.wait_ge(s["m_exped"], C0 + i + 1)
                    nc.vector.tensor_reduce(m_sum[:, :], e, AX_X, ALU.add).then_inc(s["m_summed"], 1)
                    dve.wait_ge(s["m_summed"], C0 + i + 1)
                    nc.vector.reciprocal(m_rec[:, :], m_sum[:, :]).then_inc(s["m_recd"], 1)
                    dve.wait_ge(s["m_recd"], C0 + i + 1)
                    nc.vector.tensor_tensor(e, e, m_rec[:, :].unsqueeze(2).broadcast_to((P, M_CHUNK_HEADS, nk)), ALU.mult).then_inc(s["m_probs"], 1)
                dve.wait_ge(s["m_y"], u + 1)
                at = baseT[:, bass.ds(u * T, T)]
                nc.vector.scalar_tensor_tensor(out=at, in0=bank[1][:, T:2 * T], scalar=m_bo[:, 0:1], in1=at,
                                               op0=ALU.add, op1=ALU.add).then_inc(s["m_x"], 1)

            mid_unit(0)
            with dve.Fori(1, B) as u:
                mid_unit(u)

            nc.vector.memset(xs[:, :], 0.0)
            ln_vector_plain(dve, nc, ln_sems["ln_out"], bank, f_rstd, xT, s["f_x"])
            with dve.Fori(0, DEPTH) as layer:
                layer_body(1, layer)
            add_half(1)
            for c in range(CHUNKS):
                dve.wait_ge(s["out_turned"], c + 1)
                nc.vector.tensor_copy(normed[:, c * CHUNK:(c + 1) * CHUNK], bank[4 + c]).then_inc(s["out_kept"], 1)

        @block.gpsimd
        def _(pool):
            def step(S0, g, first, last):
                has1 = (not first or g >= 1) and not (last and g >= 1)
                if not last:
                    pool.wait_ge(s["squared"], S0 + g + 1)
                    if not first or g >= 2:
                        pool.wait_ge(s["band_ready"], S0 + g - 1)
                    if not (first and g == 0):
                        pool.wait_ge(s["ss_ready"], S0 + g)
                    nc.gpsimd.tensor_tensor(sqsum[:, :, :], squares[:, :, 0, :], squares[:, :, 1, :], ALU.add).then_inc(s["sqsum_ready"], 1)
                    pool.wait_ge(s["rotated_parts"], S0 + g + 1)
                    if not (first and g == 0):
                        pool.wait_ge(s["qk_final"], S0 + g)
                    nc.gpsimd.tensor_tensor(rotated[:, :, 0, :], rot_a[:, :, 0, :], rot_b[:, :, 1, :], ALU.add)
                    nc.gpsimd.tensor_tensor(rotated[:, :, 1, :], rot_a[:, :, 1, :], rot_b[:, :, 0, :], ALU.add).then_inc(s["rotated_ready"], 1)
                if has1:
                    if not last:
                        pool.wait_ge(s["rotated_ready"], S0 + g + 1)
                    pool.wait_ge(s["prec_ready"], S0 + g)
                    if not first or g >= 2:
                        pool.wait_ge(s["pt_ready"], S0 + g - 1)
                    for j in range(P // WINDOW):
                        r = slice(j * WINDOW, (j + 1) * WINDOW)
                        to = nc.gpsimd.tensor_tensor(band[r, :, j * WINDOW:j * WINDOW + KEYS], probs[r, :, :],
                                                     prec[r, :].unsqueeze(2).broadcast_to((WINDOW, 2 * GH, KEYS)), ALU.mult)
                    to.then_inc(s["band_ready"], 1)

            def layer_body(stack, layer):
                S0 = stack * DEPTH * STEPS + layer * STEPS
                pool.wait_ge(s["consts_ready"], 1)
                for g in range(GROUPS):
                    step(S0, g, True, False)
                with pool.Fori(1, B) as u:
                    for g in range(GROUPS):
                        step(S0 + u * GROUPS, g, False, False)
                step(S0 + B * GROUPS, 0, False, True)

            for stack in range(2):
                with pool.Fori(0, DEPTH) as layer:
                    layer_body(stack, layer)


def ln_vector_plain(dve, nc, q, bank, f_rstd, dst, done):
    for c in range(CHUNKS):
        dve.wait_ge(q["rstd"], c + 1)
        nc.vector.tensor_tensor(dst[:, c * CHUNK:(c + 1) * CHUNK], bank[c % 2], f_rstd[:, c % 2, :], ALU.mult).then_inc(q["scaled"], 1)
        dve.wait_ge(q["scaled"], c + 1)
        dve.sem_inc(done, 1)


_AS_THEY_ARE = ["L0_attn_x", "L0_attn_Wq", "L0_attn_bq", "L0_attn_Wk", "L0_attn_bk", "L0_attn_Wv", "L0_attn_bv", "L0_attn_Wo",
                "L0_attn_bo", "L0_ffn_Wo", "L0_ffn_W1", "L0_ffn_W2"]


def laid_out(inputs):
    arrays = {n: np.ascontiguousarray(inputs[n]) for n in _AS_THEY_ARE}
    w = np.asarray(inputs["L0_ffn_Wqkv"])
    qk = w[:, :, :2 * INNER].reshape(DEPTH, DIM, 2, GROUPS, GH, 2, HALF).transpose(0, 1, 2, 3, 5, 4, 6)
    arrays["wqkv"] = np.ascontiguousarray(np.concatenate([qk.reshape(DEPTH, DIM, 2 * INNER), w[:, :, 2 * INNER:]], axis=2))
    scales = [np.asarray(inputs[n]).reshape(DEPTH, 2, HALF).transpose(0, 2, 1) for n in ("L0_ffn_q_scale", "L0_ffn_k_scale")]
    arrays["qk_cols"] = np.ascontiguousarray(np.tile(np.concatenate(scales, axis=2), (1, GH, 1)))
    cols = [np.asarray(inputs[n]) for n in ("L0_ffn_ln_g", "L0_ffn_ln_b", "L0_ffn_b2")]
    b1 = np.asarray(inputs["L0_ffn_b1"])
    for part in range(2):
        for m, rows in enumerate(FFN_ROWS):
            o = part * DIM_INNER + m * P
            cols.append(np.pad(b1[:, o:o + rows], ((0, 0), (0, P - rows))))
    arrays["ffn_cols"] = np.ascontiguousarray(np.stack(cols, axis=2))
    return arrays


def kernel(**inputs):
    import concourse.bacc as _bacc
    from concourse.bass_utils import run_bass_kernel_spmd as _run

    nc = _bacc.Bacc("TRN2", target_bir_lowering=False, num_devices=1)
    arrays, io = {}, {}
    for name, a in laid_out(inputs).items():
        arrays[f"in_{name}"] = a
        io[name] = nc.dram_tensor(f"in_{name}", a.shape, mybir.dt.from_np(a.dtype), kind="ExternalInput").ap()
    io["out"] = nc.dram_tensor("out_0", (B, T, DIM), F32, kind="ExternalOutput").ap()
    build_macaron(nc, io)
    r = _run(nc, [arrays], core_ids=[0])
    return r.results[0]["out_0"]
```

```python
from contextlib import ExitStack

import numpy as np

import concourse.bass as bass
from concourse import mybir

F32 = mybir.dt.float32
F32R = mybir.dt.float32r
BF16 = mybir.dt.bfloat16
ALU = mybir.AluOpType
ACT = mybir.ActivationFunctionType
AX_X = mybir.AxisListType.X

P = 128
DIM = 128
DEPTH = 6
HEADS = 16
DIM_HEAD = 64
HALF = DIM_HEAD // 2
WINDOW = 32
INNER = HEADS * DIM_HEAD
DIM_INNER = int(DIM * 4 * 2 / 3)
QK_SCALE = 8.0
M_HEADS = 16
M_GROUPS = 4
M_DIM = DIM // M_HEADS
M_REP = M_HEADS // M_GROUPS
B = 8
T = 256
TOKENS = B * T
TILES = T // P
GH = 4
PAIRS = GH * DIM_HEAD // P
GCOLS = GH * DIM_HEAD
GROUPS = HEADS // GH
STEPS = B * GROUPS
KEYS = 2 * WINDOW
BAND = P + WINDOW
KPAD = T + WINDOW
CHUNK = 512
CHUNKS = TOKENS // CHUNK
SEQ_PER_CHUNK = CHUNK // T
FFN_ROWS = [128, 128, DIM_INNER - 256]
FFN_BLOCKS = len(FFN_ROWS)
MASKED = -1.0e30
LN_EPS = 1e-5
INV_NORM_MAX = 1e12
SQ_SCALE = 2.0**16
ACT_SET = "natural_log_exp_and_others"
LN2 = 0.6931471805599453
M_CHUNK_HEADS = 4
M_CHUNKS = M_HEADS // M_CHUNK_HEADS


def rotary_constants():
    f = np.float32
    half = np.arange(0, DIM_HEAD, 2, dtype=f)
    inv_freq = f(1.0) / np.power(f(10000.0), half / f(DIM_HEAD))
    t = np.arange(T, dtype=f)
    angle = (t[:, None] * inv_freq[None, :]).astype(f)
    base = ((half + f(0.4 * DIM_HEAD)) / f(1.4 * DIM_HEAD)).astype(f)
    power = ((t - f(T // 2)) / f(WINDOW // 2)).astype(f)
    scale = np.power(base[None, :], power[:, None]).astype(f)
    cos, sin = np.cos(angle), np.sin(angle)
    for_qk = (scale * f(QK_SCALE), f(1.0) / scale)
    own = np.stack([np.concatenate([cos * s, cos * s], 1) for s in for_qk], 1)
    partner = np.stack([np.concatenate([-sin * s, sin * s], 1) for s in for_qk], 1)
    rows = np.stack([own, partner], 1).reshape(TILES, P, 2, 2, DIM_HEAD).transpose(1, 2, 0, 3, 4)
    return np.ascontiguousarray(rows.astype(f))


def window_mask():
    a = np.arange(P)[:, None, None] % WINDOW
    window = np.arange(2)[None, :, None] * (P // WINDOW) + np.arange(P)[:, None, None] // WINDOW
    k = np.arange(KEYS)[None, None, :]
    seen = (k >= a) & (k <= a + WINDOW) & ((window > 0) | (k >= WINDOW))
    return np.where(seen, 0.0, MASKED).astype(np.float32)


def middle_rotary():
    f = np.float32
    freq = np.exp(-(np.arange(0, M_DIM, 2, dtype=f) / f(M_DIM)) * np.log(f(10000.0))).astype(f)
    angle = (np.arange(T, dtype=f)[:, None] * freq).astype(f)
    d = np.arange(P) % M_DIM
    cos, sin = np.cos(angle)[:, d // 2].T, np.sin(angle)[:, d // 2].T
    return np.ascontiguousarray(np.stack([cos, np.where(d % 2 == 0, -1.0, 1.0)[:, None] * sin], 1).astype(f))


def constants():
    f = np.float32
    own_head = (np.arange(P)[:, None] // M_DIM == np.arange(M_HEADS)[None, :]).astype(f)
    causal = np.where(np.arange(P)[None, :] <= np.arange(P)[:, None], 0.0, MASKED).astype(f)
    return {
        "identity": np.eye(P, dtype=f),
        "centre": (np.eye(P) - 1.0 / P).astype(f),
        "average": np.full((P, P), 1.0 / P, f),
        "rotary": rotary_constants().reshape(P, -1),
        "mask": window_mask().reshape(P, -1),
        "m_rotary": middle_rotary().reshape(P, -1),
        "own_head": own_head,
        "causal": causal,
    }


def stages(g, first):
    return [not first or g >= k for k in range(4)]


def build_macaron(nc, io):
    out = io["out"]
    values = constants()
    const_dram = {n: nc.inline_tensor(v, name="const_" + n).ap() for n, v in values.items()}

    with ExitStack() as ctx:
        def sb(name, shape, dt=F32):
            return ctx.enter_context(nc.sbuf_tensor(name, shape, dt))

        def sem(name):
            return ctx.enter_context(nc.semaphore(name))

        ps_pair = [ctx.enter_context(nc.psum_tensor(f"ps_pair{i}", [P, 2, 512], F32)) for i in range(4)]
        bank = [ps_pair[i // 2][:, i % 2, :] for i in range(8)]

        m_out = bank[0].rearrange("p (a n) -> p a n", a=2)[:, :, 0:M_HEADS * (M_DIM + 1)].rearrange("p a (h d) -> p a h d", d=M_DIM + 1)

        cst = {n: sb("c_" + n, list(v.shape)) for n, v in values.items()}
        ident = cst["identity"]
        rot = cst["rotary"][:, :].rearrange("p (r a n) -> p r a n", r=2, a=TILES)
        ident_bf = sb("ident_bf", [P, P], BF16)
        mask_bf = sb("mask_bf", [P, 2, KEYS], BF16)
        causal_bf = sb("causal_bf", [P, P], BF16)
        eps_col = sb("eps_col", [P, 1])
        rnorm_col = sb("rnorm_col", [P, 1])

        xT = sb("xT", [P, TOKENS + T])
        baseT = sb("baseT", [P, TOKENS])
        shifted = sb("shifted", [P, TOKENS])
        normed = sb("normed", [P, TOKENS])

        wqkv = sb("wqkv", [P, 3 * INNER])
        w_hi = sb("w_hi", [P, 3 * INNER], F32R)
        w_lo = sb("w_lo", [P, 3 * INNER], F32R)
        wo = sb("wo", [P, INNER // P, DIM])
        w1 = sb("w1", [P, 2 * DIM_INNER])
        w2 = sb("w2", [P, FFN_BLOCKS, DIM])
        ffn_cols = sb("ffn_cols", [P, 3 + 2 * FFN_BLOCKS])
        b1 = ffn_cols[:, 3:].rearrange("p (a m) -> p a m", a=2)
        qk_rows = sb("qk_rows", [P, 2, 2 * DIM_HEAD])

        xs_hi = sb("xs_hi", [P, T], F32R)
        xs_lo = sb("xs_lo", [P, T], F32R)
        tab_a = sb("tab_a", [P, TILES, 2 * DIM_HEAD])
        tab_b = sb("tab_b", [P, TILES, 2 * DIM_HEAD])
        squares = sb("squares", [P, TILES * 2 * GCOLS])
        rot_a = sb("rot_a", [P, TILES * 2 * GCOLS])
        rot_b = sb("rot_b", [P, TILES * 2 * GCOLS])
        rotated = sb("rotated", [P, TILES * 2 * GCOLS])
        qk_norm = sb("qk_norm", [P, TILES * 2 * GCOLS])
        sqsum = sb("sqsum", [P, TILES * 2 * GH])
        rnorm = sb("rnorm", [P, TILES * 2 * GH])
        qfin = sb("qfin", [P, PAIRS, T])
        kblock = sb("kblock", [P, PAIRS, 2, KPAD])
        nmax = sb("nmax", [P, 2 * GH])
        probs = sb("probs", [P, 2 * GH, KEYS])
        psum_row = sb("psum_row", [P, 2 * GH])
        prec = sb("prec", [P, 2 * GH])
        band = sb("band", [P, 2 * GH, BAND])
        bandT = sb("bandT", [P, GH, P + WINDOW + P])
        vals = sb("vals", [P, 4, 2, GH * DIM_HEAD])
        outT = sb("outT", [P, INNER // P, T])

        f_sq = sb("f_sq", [P, 2, CHUNK])
        f_rstd = sb("f_rstd", [P, 2, CHUNK])
        f_mid = sb("f_mid", [P, 3 * FFN_BLOCKS * CHUNK])
        f_gelu = f_mid[:, 0:FFN_BLOCKS * CHUNK].rearrange("p (m n) -> p m n", m=FFN_BLOCKS)
        f_h = f_mid[:, FFN_BLOCKS * CHUNK:].rearrange("p (c m n) -> p c m n", c=2, m=FFN_BLOCKS)

        m_w = sb("m_w", [P, 4, P])
        m_wk = sb("m_wk", [P, 2 * M_GROUPS * M_DIM])
        m_wo = sb("m_wo", [P, DIM])
        m_bo = sb("m_bo", [P, 1])
        m_brow = sb("m_brow", [1, 4, P])
        m_bin = sb("m_bin", [1, P + 2 * M_GROUPS * M_DIM])
        ones_row = sb("ones_row", [1, T])
        m_h = sb("m_h", [P, T])
        m_rot = rot_a[:, :]
        m_rope = sb("m_rope", [P, 2, T])
        m_kblock = f_mid[:, 0:M_HEADS * T].rearrange("p (h t) -> p h t", h=M_HEADS)
        m_v = sb("m_v", [P, 2, M_GROUPS, M_DIM + 1])
        m_bcol = sb("m_bcol", [P, 4])
        m_nmax = sb("m_nmax", [P, M_CHUNK_HEADS])
        m_rec = sb("m_rec", [P, 2 * M_HEADS])
        m_e = [x[:, :].rearrange("p (h t) -> p h t", h=M_CHUNK_HEADS) for x in (rot_b, squares)]
        m_pT = rotated[:, :].rearrange("p (k h q) -> p k h q", k=2, h=M_CHUNK_HEADS)
        m_o = sb("m_o", [P, 2, DIM])
        m_oT = sb("m_oT", [P, T])

        s = {n: sem(n) for n in (
            "consts_loaded", "x_loaded", "consts_ready", "m_loaded",
            "w_qkv_loaded", "w_o_loaded", "w_scale_loaded", "w_ffn_loaded",
            "x_turned", "x_kept", "out_summed", "out_turned", "out_kept", "out_stored",
            "w_rounded", "w_split", "xs_ready", "xs_split", "tables_ready",
            "qk_ready", "v_ready", "qk_turned", "s_ready", "pt_ready", "pv_ready", "y_ready",
            "squared", "v_saved", "qk_kept", "exped", "pt_saved", "sqsum_logged", "rnorm_ready", "out_saved",
            "rotated_parts", "sqsum_ready", "qk_normed", "x_updated", "max_ready", "shifted_scores", "sum_ready", "prec_ready",
            "rotated_ready", "band_ready",
            "f_gate", "f_a", "f_gelued", "f_mixed", "f_y", "f_x",
            "m_copied", "m_qk", "m_parts", "m_roped", "m_kblocked", "m_vdone", "m_vsaved",
            "m_bturned", "m_bsaved", "m_scores", "m_maxed", "m_shifted", "m_exped", "m_recd",
            "m_turned", "m_tsaved", "m_pv", "m_osaved", "m_oturned", "m_otsaved", "m_y", "m_x", "m_prepared",
        )}
        ln_sems = {f: {n: sem(f"{f}_{n}") for n in ("copied", "centred", "squared", "var", "logged", "rstd", "scaled", "normed")}
                   for f in ("ln_in", "ln_mid", "ln_out", "ln_ffn")}

        def chunks_before(stack, layer):
            return CHUNKS * (stack * (DEPTH + 1) + 1) + layer * CHUNKS

        def ln_tensor(pe, q, base, src, started):
            def centre(c):
                pe.wait_ge(started[0], started[1] + (c + 1 if started[2] else 0))
                if c >= 2:
                    pe.wait_ge(q["scaled"], base + c - 1)
                pe.matmul(bank[c % 2], cst["centre"][:, :], src[:, c * CHUNK:(c + 1) * CHUNK],
                          start=True, stop=True).then_inc(q["centred"], 1)

            def variance(c):
                pe.wait_ge(q["squared"], base + c + 1)
                if c >= 1:
                    pe.wait_ge(q["logged"], base + c)
                pe.matmul(bank[2], cst["average"][:, :], f_sq[:, c % 2, :],
                          start=True, stop=True).then_inc(q["var"], 1)

            return centre, variance

        def ln_scalar(act, q, base):
            def square(c):
                act.wait_ge(q["centred"], base + c + 1)
                if c >= 2:
                    act.wait_ge(q["var"], base + c - 1)
                act.activation(f_sq[:, c % 2, :], bank[c % 2], ACT.Square).then_inc(q["squared"], 1)

            def rstd(c):
                act.wait_ge(q["var"], base + c + 1)
                if c >= 2:
                    act.wait_ge(q["scaled"], base + c - 1)
                act.activation(f_rstd[:, c % 2, :], bank[2], ACT.Ln, bias=eps_col[:, 0:1]).then_inc(q["logged"], 1)
                act.wait_ge(q["logged"], base + c + 1)
                act.activation(f_rstd[:, c % 2, :], f_rstd[:, c % 2, :], ACT.Exp, scale=-0.5).then_inc(q["rstd"], 1)

            return square, rstd

        def ln_vector(dve, q, base, dst, affine):
            def scale(c):
                to = dst[:, c * CHUNK:(c + 1) * CHUNK]
                dve.wait_ge(q["rstd"], base + c + 1)
                if affine:
                    nc.vector.scalar_tensor_tensor(out=to, in0=bank[c % 2], scalar=ffn_cols[:, 0:1], in1=f_rstd[:, c % 2, :],
                                                   op0=ALU.mult, op1=ALU.mult).then_inc(q["scaled"], 1)
                    dve.wait_ge(q["scaled"], base + c + 1)
                    nc.vector.tensor_scalar(to, to, ffn_cols[:, 1:2], None, ALU.add).then_inc(q["normed"], 1)
                else:
                    nc.vector.tensor_tensor(to, bank[c % 2], f_rstd[:, c % 2, :], ALU.mult).then_inc(q["scaled"], 1)

            return scale

        def one_behind(first, second):
            for c in range(CHUNKS + 1):
                if c < CHUNKS:
                    first(c)
                if c >= 1:
                    second(c - 1)

        block = ctx.enter_context(nc.Block())

        @block.sync
        def _(sp):
            for n in values:
                sp.dma_start(cst[n][:, :], const_dram[n]).then_inc(s["consts_loaded"], 16)
            x_in = io["L0_attn_x"].rearrange("b (h p) d -> p (b h) d", p=P)
            sp.dma_start(normed[:, :].rearrange("p (n d) -> p n d", d=DIM), x_in).then_inc(s["x_loaded"], 16)

            def load_layer(layer, done, final):
                wqkv_l = io["wqkv"][bass.ds(layer, 1), :, :].rearrange("l p n -> p (l n)")
                wo_l = io["L0_ffn_Wo"][bass.ds(layer, 1), :, :].rearrange("l (c p) n -> p (l c) n", p=P)
                w1_l = io["L0_ffn_W1"][bass.ds(layer, 1), :, :].rearrange("l p n -> p (l n)")
                w2_l = io["L0_ffn_W2"][bass.ds(layer, 1), :, :].rearrange("l k n -> (l k) n")
                if done is not None:
                    sp.wait_ge(s["w_split"], done * GROUPS)
                sp.dma_start(wqkv[:, :], wqkv_l).then_inc(s["w_qkv_loaded"], 16)
                if done is not None:
                    sp.wait_ge(s["tables_ready"], done)
                sp.dma_start(qk_rows[:, :, :], io["qk_rows"][bass.ds(layer, 1), :, :, :].rearrange("l p a n -> p (l a) n")).then_inc(s["w_scale_loaded"], 16)
                if done is not None:
                    sp.wait_ge(s["y_ready"], done * B)
                sp.dma_start(wo[:, :, :], wo_l).then_inc(s["w_o_loaded"], 16)
                if final is not None:
                    sp.wait_ge(s["f_x"], final)
                sp.dma_start(w1[:, :], w1_l).then_inc(s["w_ffn_loaded"], 16)
                sp.dma_start(w2[:, 0:2, :], w2_l[0:2 * P, :].rearrange("(c p) n -> p c n", p=P)).then_inc(s["w_ffn_loaded"], 16)
                sp.dma_start(w2[0:FFN_ROWS[2], 2, :], w2_l[2 * P:DIM_INNER, :]).then_inc(s["w_ffn_loaded"], 16)
                sp.dma_start(ffn_cols[:, :], io["ffn_cols"][bass.ds(layer, 1), :, :].rearrange("l p n -> p (l n)")).then_inc(s["w_ffn_loaded"], 16)

            load_layer(0, None, None)
            sp.dma_start(m_w[:, 0, :], io["L0_attn_Wq"]).then_inc(s["m_loaded"], 16)
            sp.dma_start(m_wk[:, 0:32], io["L0_attn_Wk"]).then_inc(s["m_loaded"], 16)
            sp.dma_start(m_wk[:, 32:64], io["L0_attn_Wv"]).then_inc(s["m_loaded"], 16)
            sp.dma_start(m_wo[:, :], io["L0_attn_Wo"]).then_inc(s["m_loaded"], 16)
            sp.dma_start(m_bo[:, :], io["L0_attn_bo"].rearrange("(p a) -> p a", a=1), allow_slow_non_contiguous=True).then_inc(s["m_loaded"], 16)
            sp.dma_start(m_bin[:, 0:128], io["L0_attn_bq"].rearrange("(a p) -> a p", a=1)).then_inc(s["m_loaded"], 16)
            sp.dma_start(m_bin[:, 128:160], io["L0_attn_bk"].rearrange("(a p) -> a p", a=1)).then_inc(s["m_loaded"], 16)
            sp.dma_start(m_bin[:, 160:192], io["L0_attn_bv"].rearrange("(a p) -> a p", a=1)).then_inc(s["m_loaded"], 16)
            with sp.Fori(1, DEPTH) as layer:
                load_layer(layer, layer, chunks_before(0, layer))
            load_layer(0, DEPTH, chunks_before(0, DEPTH))
            with sp.Fori(1, DEPTH) as layer:
                load_layer(layer, layer + DEPTH, chunks_before(1, layer))
            sp.wait_ge(s["out_kept"], 4)
            sp.dma_start(out.rearrange("b (h p) d -> p (b h) d", p=P),
                         normed[:, :].rearrange("p (n d) -> p n d", d=DIM)).then_inc(s["out_stored"], 16)
            sp.wait_ge(s["out_stored"], 16)

        @block.tensor
        def _(pe):
            def split_product(to, tile, cols):
                at = slice(tile * P, (tile + 1) * P)
                pe.matmul(to, xs_hi[:, at], w_hi[:, cols], start=True, stop=False)
                pe.matmul(to, xs_hi[:, at], w_lo[:, cols], start=False, stop=False)
                return pe.matmul(to, xs_lo[:, at], w_hi[:, cols], start=False, stop=True)

            def proj_qk(N, g, first):
                if not (first and g == 0):
                    pe.wait_ge(s["rotated_parts"], N)
                for tile in range(TILES):
                    mm = split_product(bank[tile], tile, slice(g * 3 * GCOLS, g * 3 * GCOLS + 2 * GCOLS))
                mm.then_inc(s["qk_ready"], 1)

            def proj_v(N, g, first):
                if not first or g >= 3:
                    pe.wait_ge(s["out_saved"], N - 2)
                elif g >= 1:
                    pe.wait_ge(s["v_saved"], N)
                for tile in range(TILES):
                    mm = split_product(bank[6][:, tile * GCOLS:(tile + 1) * GCOLS], tile,
                                       slice(g * 3 * GCOLS + 2 * GCOLS, (g + 1) * 3 * GCOLS))
                mm.then_inc(s["v_ready"], 1)

            def turn_qk(N, g, first, pair):
                if pair == 0:
                    pe.wait_ge(s["qk_normed"], N)
                if not (first and g == 1 and pair == 0):
                    pe.wait_ge(s["qk_kept"], 2 * (N - 1) + pair)
                for i in range(2):
                    for tile in range(TILES):
                        at = ((tile * 2 + i) * PAIRS + pair) * P
                        mm = pe.transpose(bank[2][:, (i * TILES + tile) * P:(i * TILES + tile + 1) * P], qk_norm[:, at:at + P], ident[:, :])
                mm.then_inc(s["qk_turned"], 1)

            def scores(N, g, first, pair):
                pe.wait_ge(s["qk_kept"], 2 * (N - 1) + pair + 1)
                if pair == 0:
                    if not (first and g == 1):
                        pe.wait_ge(s["shifted_scores"], N - 1)
                    pe.matmul(bank[3].rearrange("p (f h k) -> p f h k", f=2, h=GH), ident_bf[:, :],
                              mask_bf[:, :, :].unsqueeze(2).broadcast_to((P, 2, GH, KEYS)), start=True, stop=False,
                              skip_group_check=True)
                for hf in range(2):
                    for j in range(P // WINDOW):
                        w = hf * (P // WINDOW) + j
                        at = (hf * GH + 2 * pair) * KEYS
                        mm = pe.matmul(bank[3][j * WINDOW:(j + 1) * WINDOW, at:at + 2 * KEYS],
                                       qfin[:, pair, w * WINDOW:(w + 1) * WINDOW],
                                       kblock[:, pair, :, w * WINDOW:w * WINDOW + KEYS],
                                       start=False, stop=True, skip_group_check=True)
                if pair == PAIRS - 1:
                    mm.then_inc(s["s_ready"], 1)

            def turn_probs(N, Y0, g, first):
                pe.wait_ge(s["band_ready"], N - 1)
                if not (first and g == 2):
                    pe.wait_ge(s["pt_saved"], N - 2)
                if not first and g == 3:
                    pe.wait_ge(s["x_updated"], Y0)
                for h in range(GH):
                    pe.transpose(bank[4][:, h * P:(h + 1) * P], band[:, h, WINDOW:BAND], ident[:, :])
                    pe.transpose(bank[5][:, h * P:(h + 1) * P], band[:, GH + h, WINDOW:BAND], ident[:, :])
                flat = band[:, :, :].rearrange("p i k -> p (i k)")
                for h in range(GH):
                    at = (GH + h) * BAND + WINDOW - P
                    mm = pe.transpose(bank[7][:, h * WINDOW:(h + 1) * WINDOW], flat[0:WINDOW, at:at + P], ident[0:WINDOW, 0:WINDOW])
                mm.then_inc(s["pt_ready"], 1)

            def attend(N, g, values):
                pe.wait_ge(s["pt_saved"], N - 2)
                pe.wait_ge(s["v_saved"], values)
                slot = (g - 3) % 4
                for pair in range(PAIRS):
                    for hf in range(2):
                        for odd in range(2):
                            h = 2 * pair + odd
                            to = bank[6][odd * 64:(odd + 1) * 64, pair * T:(pair + 1) * T]
                            v = vals[:, slot, hf, h * DIM_HEAD:(h + 1) * DIM_HEAD]
                            if hf == 0:
                                mm = pe.matmul(to[:, 0:BAND], v, bandT[:, h, 0:BAND], start=True, stop=False, skip_group_check=True)
                            else:
                                mm = pe.matmul(to[:, P:T], v, bandT[:, h, BAND:BAND + P], start=False, stop=True, skip_group_check=True)
                mm.then_inc(s["pv_ready"], 1)

            def project_out(saved, turned, pieces):
                pe.wait_ge(s["out_saved"], saved)
                if pieces[0] == 0:
                    pe.wait_ge(s["pt_saved"], turned)
                for c in pieces:
                    mm = pe.matmul(bank[7][:, T:2 * T], wo[:, c, :], outT[:, c, :], start=(c == 0), stop=(c == INNER // P - 1))
                if c == INNER // P - 1:
                    mm.then_inc(s["y_ready"], 1)

            def feed_forward(C0, X0):
                q = ln_sems["ln_ffn"]
                value_bank = (6, 7, 2)

                def gates(c):
                    pe.wait_ge(q["normed"], C0 + c + 1)
                    for m, rows in enumerate(FFN_ROWS):
                        if c >= 1:
                            pe.wait_ge(s["f_gelued"], (C0 + c - 1) * FFN_BLOCKS + m + 1)
                        o = DIM_INNER + m * P
                        pe.matmul(bank[3 + m][0:rows, :], w1[:, o:o + rows],
                                  normed[:, c * CHUNK:(c + 1) * CHUNK], start=True, stop=True).then_inc(s["f_gate"], 1)

                def values(c):
                    for m, rows in enumerate(FFN_ROWS):
                        if c >= 1:
                            pe.wait_ge(s["f_mixed"], (C0 + c - 1) * FFN_BLOCKS + m + 1)
                        elif value_bank[m] == 2:
                            pe.wait_ge(q["logged"], C0 + CHUNKS)
                        pe.matmul(bank[value_bank[m]][0:rows, :], w1[:, m * P:m * P + rows],
                                  normed[:, c * CHUNK:(c + 1) * CHUNK], start=True, stop=True).then_inc(s["f_a"], 1)

                def down(c):
                    pe.wait_ge(s["f_mixed"], (C0 + c + 1) * FFN_BLOCKS)
                    if c < 2:
                        pe.wait_ge(q["scaled"], C0 + CHUNKS)
                    else:
                        pe.wait_ge(s["f_x"], X0 + c - 1)
                    for m, rows in enumerate(FFN_ROWS):
                        mm = pe.matmul(bank[c % 2], w2[0:rows, m, :], f_h[0:rows, c % 2, m, :], start=(m == 0), stop=(m == FFN_BLOCKS - 1))
                    mm.then_inc(s["f_y"], 1)

                return gates, values, down

            def layer_body(stack, layer):
                S0 = stack * DEPTH * STEPS + layer * STEPS
                U0 = stack * DEPTH * (B + 1) + layer * (B + 1)
                Y0 = stack * DEPTH * B + layer * B
                C0 = stack * DEPTH * CHUNKS + layer * CHUNKS
                G0 = stack * DEPTH + layer
                X0 = chunks_before(stack, layer)
                pe.wait_ge(s["f_x"], X0)
                pe.wait_ge(s["w_o_loaded"], G0 * 16 + 16)
                attn_unit(S0, U0, Y0, G0, True)
                with pe.Fori(1, B) as u:
                    attn_unit(S0 + u * GROUPS, U0 + u, Y0 + u, G0, False)

                centre, variance = ln_tensor(pe, ln_sems["ln_ffn"], C0, shifted, (ln_sems["ln_ffn"]["copied"], C0, True))
                gates, values, down = feed_forward(C0, X0)
                N = S0 + STEPS
                attend(N, 0, N)
                turn_qk(N, 0, False, 0)
                turn_qk(N, 0, False, 1)
                scores(N, 0, False, 0)
                scores(N, 0, False, 1)
                turn_probs(N, Y0, 0, False)
                pe.wait_ge(s["rotated_parts"], N)
                centre(0)
                centre(1)
                attend(N + 1, 1, N)
                pe.wait_ge(s["qk_kept"], 2 * N)
                variance(0)
                variance(1)
                centre(2)
                turn_probs(N + 1, Y0, 1, False)
                project_out(N - 1, N, range(0, INNER // P - 2))
                variance(2)
                pe.wait_ge(s["w_ffn_loaded"], G0 * 64 + 64)
                pe.wait_ge(s["shifted_scores"], N)
                gates(0)
                attend(N + 2, 2, N)
                project_out(N, None, range(INNER // P - 2, INNER // P))
                centre(3)
                variance(3)
                pe.wait_ge(s["x_updated"], Y0 + B)
                values(0)
                for c in range(1, CHUNKS + 1):
                    if c < CHUNKS:
                        gates(c)
                        values(c)
                    down(c - 1)

            def attn_unit(S0, U0, Y0, G0, first):
                for g in range(GROUPS):
                    N = S0 + g
                    stage = stages(g, first)
                    if g == 0:
                        pe.wait_ge(s["xs_split"], U0 + 1)
                    if first:
                        pe.wait_ge(s["w_split"], G0 * GROUPS + g + 1)
                    proj_qk(N, g, first)
                    if not first and g == 3:
                        project_out(N - 3, N - 2, range(INNER // P))
                    if stage[3]:
                        attend(N, g, N)
                    if stage[1]:
                        turn_qk(N, g, first, 0)
                    proj_v(N, g, first)
                    if stage[1]:
                        turn_qk(N, g, first, 1)
                        scores(N, g, first, 0)
                        scores(N, g, first, 1)
                    if stage[2]:
                        turn_probs(N, Y0, g, first)

            pe.wait_ge(s["consts_loaded"], 16 * len(values))
            pe.wait_ge(s["x_loaded"], 16)
            for c in range(CHUNKS):
                for i in range(4):
                    t = c * 4 + i
                    mm = pe.transpose(bank[4 + c][:, i * P:(i + 1) * P], normed[:, t * P:(t + 1) * P], ident[:, :])
                mm.then_inc(s["x_turned"], 1)
            one_behind(*ln_tensor(pe, ln_sems["ln_in"], 0, baseT, (s["x_kept"], 0, True)))
            pe.wait_ge(s["consts_ready"], 1)

            with pe.Fori(0, DEPTH) as layer:
                layer_body(0, layer)

            one_behind(*ln_tensor(pe, ln_sems["ln_mid"], 0, baseT, (s["out_summed"], 0, True)))
            pe.wait_ge(s["m_prepared"], 1)
            for i in range(4):
                mm = pe.matmul(bank[3][:, i:i + 1], m_brow[:, i, :], ones_row[:, 0:1], start=True, stop=True)
            mm.then_inc(s["m_bturned"], 1)
            pe.wait_ge(s["m_bsaved"], 1)
            pe.wait_ge(ln_sems["ln_mid"]["scaled"], CHUNKS)

            def mid_unit(u):
                C0 = u * 2 * M_CHUNKS
                pe.wait_ge(s["m_copied"], u + 1)
                for i in range(2):
                    for v in range(2):
                        mm = pe.matmul(bank[i][:, v * T:(v + 1) * T], m_w[:, 2 * i + v, :], m_h[:, :], start=True, stop=True)
                mm.then_inc(s["m_qk"], 1)
                pe.wait_ge(s["m_parts"], u + 1)
                for hf in range(2):
                    to = bank[1][:, hf * 32:(hf + 1) * 32]
                    pe.matmul(to, m_h[:, hf * P:(hf + 1) * P], m_wk[:, 32:64], start=True, stop=False)
                    mm = pe.matmul(to, ones_row[:, 0:P], m_bin[:, 160:192], start=False, stop=True)
                mm.then_inc(s["m_vdone"], 1)
                def m_scores(i):
                    hf, c = i // M_CHUNKS, i % M_CHUNKS
                    nk = (hf + 1) * P
                    t = ps_pair[1 + i % 2]
                    if hf == 0:
                        pe.wait_ge(s["m_kblocked"], u * M_CHUNKS + c + 1)
                    if i >= 2:
                        pe.wait_ge(s["m_shifted"], C0 + i - 1)
                    for b in range(2):
                        h = c * M_CHUNK_HEADS + 2 * b
                        to = t[:, b, :].rearrange("p (h k) -> p h k", h=2)
                        pe.matmul(to[:, :, 0:nk], m_rope[:, 0, hf * P:(hf + 1) * P], m_kblock[:, h:h + 2, 0:nk],
                                  start=True, stop=False, skip_group_check=True)
                        mm = pe.matmul(to[:, :, hf * P:nk], ident_bf[:, :], causal_bf[:, :].unsqueeze(1).broadcast_to((P, 2, P)),
                                       start=False, stop=True, skip_group_check=True)
                    mm.then_inc(s["m_scores"], 1)

                def m_turn(i):
                    hf, c = i // M_CHUNKS, i % M_CHUNKS
                    pe.wait_ge(s["m_exped"], C0 + i + 1)
                    if i >= 1:
                        pe.wait_ge(s["m_tsaved"], C0 + i)
                    for kb in range(hf + 1):
                        for h in range(M_CHUNK_HEADS):
                            mm = pe.transpose(ps_pair[3][:, kb, h * P:(h + 1) * P], m_e[i % 2][:, h, kb * P:(kb + 1) * P], ident[:, :])
                    mm.then_inc(s["m_turned"], 1)

                def m_attend(i):
                    hf, c = i // M_CHUNKS, i % M_CHUNKS
                    pe.wait_ge(s["m_tsaved"], C0 + i + 1)
                    pe.wait_ge(s["m_vsaved"], u + 1)
                    for h in range(M_CHUNK_HEADS):
                        head = c * M_CHUNK_HEADS + h
                        gr = head // M_REP
                        for kb in range(hf + 1):
                            mm = pe.matmul(m_out[:, hf, head, :], m_pT[:, kb, h, :], m_v[:, kb, gr, :], start=(kb == 0), stop=(kb == hf))
                    mm.then_inc(s["m_pv"], 1)

                for i in range(2 * M_CHUNKS + 2):
                    if i < 2 * M_CHUNKS:
                        m_scores(i)
                    if 1 <= i <= 2 * M_CHUNKS:
                        m_turn(i - 1)
                    if i >= 2:
                        m_attend(i - 2)
                pe.wait_ge(s["m_osaved"], u + 1)
                for hf in range(2):
                    mm = pe.transpose(bank[1][:, hf * P:(hf + 1) * P], m_o[:, hf, :], ident[:, :])
                mm.then_inc(s["m_oturned"], 1)
                pe.wait_ge(s["m_otsaved"], u + 1)
                pe.matmul(bank[1][:, T:2 * T], m_wo[:, :], m_oT[:, :], start=True, stop=True).then_inc(s["m_y"], 1)

            mid_unit(0)
            with pe.Fori(1, B) as u:
                pe.wait_ge(s["m_x"], u)
                mid_unit(u)

            one_behind(*ln_tensor(pe, ln_sems["ln_out"], 0, baseT, (s["m_x"], B, False)))
            with pe.Fori(0, DEPTH) as layer:
                layer_body(1, layer)

            for c in range(CHUNKS):
                pe.wait_ge(s["out_summed"], CHUNKS + c + 1)
                for i in range(4):
                    t = c * 4 + i
                    mm = pe.transpose(bank[4 + c][:, i * P:(i + 1) * P], baseT[:, t * P:(t + 1) * P], ident[:, :])
                mm.then_inc(s["out_turned"], 1)

        @block.scalar
        def _(act):
            def copy_shifted(u):
                nc.scalar.copy(xs_hi[0:64, :], xT[0:64, bass.ds(u * T, T)])
                nc.scalar.copy(xs_hi[64:P, 1:T], xT[64:P, bass.ds(u * T, T - 1)]).then_inc(s["xs_ready"], 1)

            def keep_qk(N, g, first, pair):
                act.wait_ge(s["qk_turned"], 2 * (N - 1) + pair + 1)
                if pair == 0 and not (first and g == 1):
                    act.wait_ge(s["s_ready"], N - 1)
                nc.scalar.copy(qfin[:, pair, :], bank[2][:, 0:T])
                nc.scalar.copy(kblock[0:64, pair, 0, WINDOW:KPAD], bank[2][0:64, T:2 * T])
                nc.scalar.copy(kblock[64:P, pair, 1, WINDOW:KPAD], bank[2][64:P, T:2 * T]).then_inc(s["qk_kept"], 1)

            def save_out(N, g, projected):
                act.wait_ge(s["pv_ready"], N - 2)
                if projected is not None:
                    act.wait_ge(s["y_ready"], projected)
                gp = (g - 3) % GROUPS
                nc.scalar.copy(outT[:, 2 * gp:2 * gp + 2, :].rearrange("p a t -> p (a t)"), bank[6]).then_inc(s["out_saved"], 1)

            def save_turned(N, used):
                act.wait_ge(s["pt_ready"], N - 1)
                if used is not None:
                    act.wait_ge(s["pv_ready"], used)
                nc.scalar.copy(bandT[:, :, 0:P], bank[4].rearrange("p (h q) -> p h q", h=GH))
                nc.scalar.copy(bandT[:, :, BAND:BAND + P], bank[5].rearrange("p (h q) -> p h q", h=GH))
                nc.scalar.copy(bandT[:, :, P:BAND], bank[7][:, 0:P].rearrange("p (h q) -> p h q", h=GH)).then_inc(s["pt_saved"], 1)

            def exponentials(N):
                act.wait_ge(s["shifted_scores"], N)
                nc.scalar.activation(probs[:, :, :], probs[:, :, :], ACT.Exp).then_inc(s["exped"], 1)

            def step(S0, Y0, u, g, first):
                N = S0 + g
                stage = stages(g, first)
                act.wait_ge(s["qk_ready"], N + 1)
                if not (first and g == 0):
                    act.wait_ge(s["sqsum_ready"], N)
                nc.scalar.activation(squares[:, :].rearrange("p (a n) -> p a n", a=TILES), ps_pair[0][:, :, :],
                                     ACT.Square).then_inc(s["squared"], 1)
                if stage[3]:
                    save_out(N, g, Y0 if not first and g == 3 else None)
                if stage[1]:
                    keep_qk(N, g, first, 0)
                    keep_qk(N, g, first, 1)
                act.wait_ge(s["v_ready"], N + 1)
                if not first:
                    act.wait_ge(s["pv_ready"], N - 3)
                nc.scalar.copy(vals[:, g, :, :].rearrange("p a n -> p (a n)"), bank[6]).then_inc(s["v_saved"], 1)
                if g == GROUPS - 1:
                    copy_shifted(u + 1)
                act.wait_ge(s["sqsum_ready"], N + 1)
                if not (first and g == 0):
                    act.wait_ge(s["qk_normed"], N)
                nc.scalar.activation(rnorm[:, :], sqsum[:, :], ACT.Ln, scale=SQ_SCALE).then_inc(s["sqsum_logged"], 1)
                act.wait_ge(s["sqsum_logged"], N + 1)
                nc.scalar.activation(rnorm[:, :], rnorm[:, :], ACT.Exp, scale=-0.5,
                                     bias=rnorm_col[:, 0:1]).then_inc(s["rnorm_ready"], 1)
                if stage[1]:
                    exponentials(N)
                if stage[2]:
                    save_turned(N, N - 2 if stage[3] else None)

            def round_weights(G0):
                act.wait_ge(s["w_qkv_loaded"], G0 * 16 + 16)
                for g in range(GROUPS):
                    cols = slice(g * 3 * GCOLS, (g + 1) * 3 * GCOLS)
                    nc.scalar.copy(w_hi[:, cols], wqkv[:, cols]).then_inc(s["w_rounded"], 1)

            def layer_body(stack, layer, following):
                S0 = stack * DEPTH * STEPS + layer * STEPS
                Y0 = stack * DEPTH * B + layer * B
                C0 = stack * DEPTH * CHUNKS + layer * CHUNKS
                G0 = stack * DEPTH + layer
                nc.scalar.preload_act_table_set(ACT_SET)
                act.wait_ge(s["f_x"], chunks_before(stack, layer))
                copy_shifted(0)
                for g in range(GROUPS):
                    step(S0, Y0, 0, g, True)
                with act.Fori(1, B) as u:
                    for g in range(GROUPS):
                        step(S0 + u * GROUPS, Y0 + u, u, g, False)

                square, rstd = ln_scalar(act, ln_sems["ln_ffn"], C0)
                N = S0 + STEPS
                save_out(N, 0, None)
                keep_qk(N, 0, False, 0)
                keep_qk(N, 0, False, 1)
                exponentials(N)
                save_turned(N, N - 2)
                if following:
                    round_weights(G0 + 1)
                square(0)
                square(1)
                save_out(N + 1, 1, None)
                rstd(0)
                rstd(1)
                square(2)
                save_turned(N + 1, N - 1)
                rstd(2)
                save_out(N + 2, 2, None)
                square(3)
                rstd(3)
                act.wait_ge(s["w_ffn_loaded"], G0 * 64 + 64)
                for c in range(CHUNKS):
                    for m, rows in enumerate(FFN_ROWS):
                        act.wait_ge(s["f_gate"], (C0 + c) * FFN_BLOCKS + m + 1)
                        if c >= 1:
                            act.wait_ge(s["f_mixed"], (C0 + c - 1) * FFN_BLOCKS + m + 1)
                        nc.scalar.activation(f_gelu[0:rows, m, :], bank[3 + m][0:rows, :], ACT.Gelu,
                                             bias=b1[0:rows, 1, m:m + 1]).then_inc(s["f_gelued"], 1)

            act.wait_ge(s["consts_ready"], 1)
            one_behind(*ln_scalar(act, ln_sems["ln_in"], 0))
            round_weights(0)
            with act.Fori(0, DEPTH) as layer:
                layer_body(0, layer, True)

            nc.scalar.preload_act_table_set(ACT_SET)
            one_behind(*ln_scalar(act, ln_sems["ln_mid"], 0))

            def mid_unit(u):
                C0 = u * 2 * M_CHUNKS
                act.wait_ge(ln_sems["ln_mid"]["scaled"], CHUNKS)
                nc.scalar.copy(m_h[:, :], xT[:, bass.ds(u * T, T)]).then_inc(s["m_copied"], 1)
                act.wait_ge(s["m_vdone"], u + 1)
                nc.scalar.copy(m_v[:, :, :, 0:M_DIM].rearrange("p a g d -> p (a g) d"),
                               bank[1][:, 0:64].rearrange("p (n d) -> p n d", d=M_DIM)).then_inc(s["m_vsaved"], 1)

                def exponentials(i):
                    nk = (i // M_CHUNKS + 1) * P
                    act.wait_ge(s["m_shifted"], C0 + i + 1)
                    nc.scalar.activation(m_e[i % 2][:, :, 0:nk], m_e[i % 2][:, :, 0:nk], ACT.Exp,
                                         scale=float(1.0 / np.sqrt(M_DIM))).then_inc(s["m_exped"], 1)

                def save_turned(i):
                    hf = i // M_CHUNKS
                    act.wait_ge(s["m_turned"], C0 + i + 1)
                    if i >= 1:
                        act.wait_ge(s["m_pv"], C0 + i)
                    nc.scalar.copy(m_pT[:, 0:hf + 1, :, :].rearrange("p k h q -> p k (h q)"),
                                   ps_pair[3][:, 0:hf + 1, :]).then_inc(s["m_tsaved"], 1)

                for i in range(2 * M_CHUNKS + 1):
                    if i < 2 * M_CHUNKS:
                        exponentials(i)
                    if i >= 1:
                        save_turned(i - 1)
                act.wait_ge(s["m_oturned"], u + 1)
                nc.scalar.copy(m_oT[:, :], bank[1][:, 0:T]).then_inc(s["m_otsaved"], 1)

            mid_unit(0)
            with act.Fori(1, B) as u:
                act.wait_ge(s["m_x"], u)
                mid_unit(u)

            one_behind(*ln_scalar(act, ln_sems["ln_out"], 0))
            with act.Fori(0, DEPTH - 1) as layer:
                layer_body(1, layer, True)
            layer_body(1, DEPTH - 1, False)

        @block.vector
        def _(dve):
            def tables(G0):
                dve.wait_ge(s["w_scale_loaded"], G0 * 16 + 16)
                for n, tab in enumerate((tab_a, tab_b)):
                    last = nc.vector.tensor_tensor(tab[:, :, :], rot[:, n, :, :], qk_rows[:, n:n + 1, :].broadcast_to((P, TILES, 2 * DIM_HEAD)), ALU.mult)
                last.then_inc(s["tables_ready"], 1)
                dve.wait_ge(s["tables_ready"], G0 + 1)

            def split_shifted(U0, u):
                dve.wait_ge(s["xs_ready"], U0 + 1)
                nc.vector.tensor_tensor(xs_lo[0:64, :], xT[0:64, bass.ds(u * T, T)], xs_hi[0:64, :].bitcast(F32), ALU.subtract)
                nc.vector.tensor_tensor(xs_lo[64:P, 1:T], xT[64:P, bass.ds(u * T, T - 1)], xs_hi[64:P, 1:T].bitcast(F32),
                                        ALU.subtract).then_inc(s["xs_split"], 1)

            heads = "p (n h d) -> p n h d"

            def sum_exponentials(N, used):
                dve.wait_ge(s["exped"], N - 1)
                nc.vector.tensor_reduce(psum_row[:, :], probs[:, :, :], AX_X, ALU.add).then_inc(s["sum_ready"], 1)
                dve.wait_ge(s["sum_ready"], N - 1)
                if used is not None:
                    dve.wait_ge(s["band_ready"], used)
                nc.vector.reciprocal(prec[:, :], psum_row[:, :]).then_inc(s["prec_ready"], 1)

            def norm_qk(N, turned):
                dve.wait_ge(s["rotated_ready"], N)
                dve.wait_ge(s["rnorm_ready"], N)
                if turned is not None:
                    dve.wait_ge(s["qk_turned"], turned)
                by_head = "p (n d) -> p n d"
                nc.vector.scalar_tensor_tensor(out=qk_norm[:, :].rearrange(by_head, d=DIM_HEAD),
                                               in0=rnorm[:, :].unsqueeze(2).broadcast_to((P, TILES * 2 * GH, DIM_HEAD)), scalar=INV_NORM_MAX,
                                               in1=rotated[:, :].rearrange(by_head, d=DIM_HEAD),
                                               op0=ALU.min, op1=ALU.mult).then_inc(s["qk_normed"], 1)

            def shift_scores(N, placed):
                dve.wait_ge(s["s_ready"], N)
                sc = bank[3].rearrange("p (i k) -> p i k", k=KEYS)
                nc.vector.tensor_reduce(nmax[:, :], sc, AX_X, ALU.max, negate=True).then_inc(s["max_ready"], 1)
                dve.wait_ge(s["max_ready"], N)
                if placed is not None:
                    dve.wait_ge(s["band_ready"], placed)
                nc.vector.tensor_tensor(probs[:, :, :], sc, nmax[:, :].unsqueeze(2).broadcast_to((P, 2 * GH, KEYS)),
                                        ALU.add).then_inc(s["shifted_scores"], 1)

            def update_x(Y0, u):
                dve.wait_ge(s["y_ready"], Y0)
                at = xT[:, bass.ds((u - 1) * T, T)]
                nc.vector.tensor_tensor(at, bank[7][:, T:2 * T], at, ALU.add).then_inc(s["x_updated"], 1)

            def step(S0, U0, Y0, u, g, first):
                N = S0 + g
                stage = stages(g, first)
                if stage[2]:
                    sum_exponentials(N, N - 2 if stage[3] else None)
                if stage[1]:
                    norm_qk(N, 2 * (N - 1) if stage[2] else None)
                dve.wait_ge(s["squared"], N + 1)
                if not (first and g == 0):
                    dve.wait_ge(s["rotated_ready"], N)
                qk = ps_pair[0][:, :, :].rearrange("p a n -> p (a n)").rearrange(heads, h=GH, d=DIM_HEAD)
                a4, b4 = (r[:, :].rearrange(heads, h=GH, d=DIM_HEAD) for r in (rot_a, rot_b))
                ta, tb = (r[:, :, :].rearrange("p a (i d) -> p (a i) d", d=DIM_HEAD).unsqueeze(2) for r in (tab_a, tab_b))
                nc.vector.tensor_tensor(a4, qk, ta.broadcast_to((P, TILES * 2, GH, DIM_HEAD)), ALU.mult)
                for half in range(2):
                    own, partner = (slice(x * HALF, (x + 1) * HALF) for x in (half, 1 - half))
                    part = nc.vector.tensor_tensor(b4[:, :, :, own], qk[:, :, :, partner],
                                                   tb[:, :, :, own].broadcast_to((P, TILES * 2, GH, HALF)), ALU.mult)
                part.then_inc(s["rotated_parts"], 1)
                if not (first and g == 0):
                    dve.wait_ge(s["sqsum_logged"], N)
                nc.vector.tensor_reduce(sqsum[:, :], squares[:, :].rearrange("p (n d) -> p n d", d=DIM_HEAD), AX_X,
                                        ALU.add).then_inc(s["sqsum_ready"], 1)
                if not first and g == 3:
                    update_x(Y0, u)
                if g == 3:
                    split_shifted(U0 + 1, u + 1)
                if stage[1]:
                    shift_scores(N, N - 1 if stage[2] else None)

            def layer_body(stack, layer):
                S0 = stack * DEPTH * STEPS + layer * STEPS
                U0 = stack * DEPTH * (B + 1) + layer * (B + 1)
                Y0 = stack * DEPTH * B + layer * B
                C0 = stack * DEPTH * CHUNKS + layer * CHUNKS
                G0 = stack * DEPTH + layer
                tables(G0)
                split_shifted(U0, 0)
                for g in range(GROUPS):
                    step(S0, U0, Y0, 0, g, True)
                with dve.Fori(1, B) as u:
                    for g in range(GROUPS):
                        step(S0 + u * GROUPS, U0 + u, Y0 + u, u, g, False)

                q = ln_sems["ln_ffn"]
                scale = ln_vector(dve, q, C0, normed, True)

                def shift_tokens(c):
                    dve.wait_ge(s["x_updated"], Y0 + (c + 1) * SEQ_PER_CHUNK)
                    at = slice(c * CHUNK, (c + 1) * CHUNK)
                    nc.vector.tensor_copy(shifted[0:64, at], xT[0:64, at])
                    nc.vector.tensor_copy(shifted[64:P, at].rearrange("p (b t) -> p b t", t=T)[:, :, 1:T],
                                          xT[64:P, at].rearrange("p (b t) -> p b t", t=T)[:, :, 0:T - 1]).then_inc(q["copied"], 1)

                N = S0 + STEPS
                sum_exponentials(N, N - 2)
                norm_qk(N, 2 * (N - 1))
                for c in range(CHUNKS - 1):
                    shift_tokens(c)
                shift_scores(N, N - 1)
                sum_exponentials(N + 1, N - 1)
                dve.wait_ge(s["w_ffn_loaded"], G0 * 64 + 64)
                for c in range(CHUNKS - 1):
                    scale(c)
                update_x(Y0 + B, B)
                shift_tokens(CHUNKS - 1)
                scale(CHUNKS - 1)
                for c in range(CHUNKS + 1):
                    if c < CHUNKS:
                        if c >= 2:
                            dve.wait_ge(s["f_y"], C0 + c - 1)
                        for m, rows in enumerate(FFN_ROWS):
                            n = (C0 + c) * FFN_BLOCKS + m + 1
                            dve.wait_ge(s["f_gelued"], n)
                            dve.wait_ge(s["f_a"], n)
                            nc.vector.scalar_tensor_tensor(out=f_h[0:rows, c % 2, m, :], in0=bank[(6, 7, 2)[m]][0:rows, :], scalar=b1[0:rows, 0, m:m + 1],
                                                           in1=f_gelu[0:rows, m, :], op0=ALU.add, op1=ALU.mult).then_inc(s["f_mixed"], 1)
                    if c >= 1:
                        dve.wait_ge(s["f_y"], C0 + c)
                        at = xT[:, (c - 1) * CHUNK:c * CHUNK]
                        nc.vector.scalar_tensor_tensor(out=at, in0=bank[(c - 1) % 2], scalar=ffn_cols[:, 2:3], in1=at,
                                                       op0=ALU.add, op1=ALU.add).then_inc(s["f_x"], 1)

            def add_half(stack):
                dve.wait_ge(s["f_x"], chunks_before(stack, DEPTH))
                for c in range(CHUNKS):
                    at = slice(c * CHUNK, (c + 1) * CHUNK)
                    nc.vector.scalar_tensor_tensor(out=baseT[:, at], in0=xT[:, at], scalar=0.5, in1=baseT[:, at],
                                                   op0=ALU.mult, op1=ALU.add).then_inc(s["out_summed"], 1)

            dve.wait_ge(s["consts_loaded"], 16 * len(values))
            nc.vector.tensor_copy(ident_bf[:, :], ident[:, :])
            nc.vector.tensor_copy(mask_bf[:, :, :].rearrange("p f k -> p (f k)"), cst["mask"][:, :])
            nc.vector.tensor_copy(causal_bf[:, :], cst["causal"][:, :])
            nc.vector.memset(eps_col[:, :], LN_EPS)
            nc.vector.memset(rnorm_col[:, :], 0.5 * LN2 * float(np.log2(SQ_SCALE)))
            nc.vector.memset(kblock[:, :, :, :], 0.0)
            nc.vector.memset(band[:, :, :], 0.0)
            nc.vector.memset(xs_hi[:, :].bitcast(F32), 0.0)
            nc.vector.memset(xs_lo[:, :].bitcast(F32), 0.0)
            nc.vector.memset(shifted[:, :], 0.0)
            nc.vector.memset(ones_row[:, :], 1.0)
            nc.vector.memset(xT[:, TOKENS:TOKENS + T], 0.0).then_inc(s["consts_ready"], 1)
            dve.wait_ge(s["consts_ready"], 1)
            for c in range(CHUNKS):
                dve.wait_ge(s["x_turned"], c + 1)
                nc.vector.tensor_copy(baseT[:, c * CHUNK:(c + 1) * CHUNK], bank[4 + c]).then_inc(s["x_kept"], 1)
            ln_vector_plain(dve, nc, ln_sems["ln_in"], bank, f_rstd, xT, s["f_x"])
            with dve.Fori(0, DEPTH) as layer:
                layer_body(0, layer)
            add_half(0)

            scale = ln_vector(dve, ln_sems["ln_mid"], 0, xT, False)
            for c in range(CHUNKS):
                scale(c)
            dve.wait_ge(s["m_loaded"], 16 * 8)
            pairs = "p (n two) -> p n two"
            for to, frm in ((m_w[:, 1, :], m_w[:, 0, :]), (m_brow[:, 1, :], m_bin[:, 0:128])):
                t2, f2 = to.rearrange(pairs, two=2), frm.rearrange(pairs, two=2)
                nc.vector.tensor_copy(t2[:, :, 0:1], f2[:, :, 1:2])
                nc.vector.tensor_copy(t2[:, :, 1:2], f2[:, :, 0:1])
            nc.vector.tensor_copy(m_brow[:, 0, :], m_bin[:, 0:128])
            for rows, to, frm in ((P, m_w, m_wk[:, 0:32]), (1, m_brow, m_bin[:, 128:160])):
                for rep in range(M_REP):
                    t3 = to[:, 2, :].rearrange("p (g r d) -> p g r d", r=M_REP, d=M_DIM)[:, :, rep, :]
                    s3 = to[:, 3, :].rearrange("p (g r d) -> p g r d", r=M_REP, d=M_DIM)[:, :, rep, :]
                    f3 = frm.rearrange("p (g d) -> p g d", d=M_DIM)
                    nc.vector.tensor_copy(t3, f3)
                    for a in range(2):
                        last = nc.vector.tensor_copy(s3.rearrange("p g (n two) -> p g n two", two=2)[:, :, :, a],
                                                     f3.rearrange("p g (n two) -> p g n two", two=2)[:, :, :, 1 - a])
            nc.vector.memset(m_v[:, :, :, M_DIM:M_DIM + 1], 1.0)
            last.then_inc(s["m_prepared"], 1)
            dve.wait_ge(s["m_bturned"], 1)
            nc.vector.tensor_copy(m_bcol[:, :], bank[3][:, 0:4]).then_inc(s["m_bsaved"], 1)
            dve.wait_ge(s["m_bsaved"], 1)

            def mid_unit(u):
                C0 = u * 2 * M_CHUNKS
                dve.wait_ge(s["m_qk"], u + 1)
                for i in range(2):
                    for v in range(2):
                        n = 2 * i + v
                        part = nc.vector.scalar_tensor_tensor(out=m_rot[:, n * T:(n + 1) * T], in0=bank[i][:, v * T:(v + 1) * T],
                                                              scalar=m_bcol[:, n:n + 1], in1=cst["m_rotary"][:, v * T:(v + 1) * T],
                                                              op0=ALU.add, op1=ALU.mult)
                part.then_inc(s["m_parts"], 1)
                dve.wait_ge(s["m_parts"], u + 1)
                parts = m_rot.rearrange("p (i v t) -> p i v t", i=2, v=2)
                nc.vector.tensor_tensor(m_rope[:, :, :], parts[:, :, 0, :], parts[:, :, 1, :], ALU.add).then_inc(s["m_roped"], 1)
                dve.wait_ge(s["m_roped"], u + 1)

                def keys_by_head(c):
                    heads = slice(c * M_CHUNK_HEADS, (c + 1) * M_CHUNK_HEADS)
                    nc.vector.tensor_tensor(m_kblock[:, heads, :], m_rope[:, 1:2, :].broadcast_to((P, M_CHUNK_HEADS, T)),
                                            cst["own_head"][:, heads].unsqueeze(2).broadcast_to((P, M_CHUNK_HEADS, T)),
                                            ALU.mult).then_inc(s["m_kblocked"], 1)

                keys_by_head(0)
                for i in range(2 * M_CHUNKS):
                    nk = (i // M_CHUNKS + 1) * P
                    if i + 1 < M_CHUNKS:
                        keys_by_head(i + 1)
                    dve.wait_ge(s["m_scores"], C0 + i + 1)
                    sc = ps_pair[1 + i % 2][:, :, :].rearrange("p a (h k) -> p (a h) k", h=2)[:, :, 0:nk]
                    if i >= 1:
                        dve.wait_ge(s["m_shifted"], C0 + i)
                    nc.vector.tensor_reduce(m_nmax[:, :], sc, AX_X, ALU.max, negate=True).then_inc(s["m_maxed"], 1)
                    dve.wait_ge(s["m_maxed"], C0 + i + 1)
                    if i >= 2:
                        dve.wait_ge(s["m_turned"], C0 + i - 1)
                    nc.vector.tensor_tensor(m_e[i % 2][:, :, 0:nk], sc, m_nmax[:, :].unsqueeze(2).broadcast_to((P, M_CHUNK_HEADS, nk)),
                                            ALU.add).then_inc(s["m_shifted"], 1)
                dve.wait_ge(s["m_pv"], C0 + 2 * M_CHUNKS)
                nc.vector.reciprocal(m_rec[:, :].rearrange("p (a h) -> p a h", a=2), m_out[:, :, :, M_DIM]).then_inc(s["m_recd"], 1)
                dve.wait_ge(s["m_recd"], u + 1)
                for hf in range(2):
                    o = nc.vector.tensor_tensor(m_o[:, hf, :].rearrange("p (h d) -> p h d", d=M_DIM), m_out[:, hf, :, 0:M_DIM],
                                                m_rec[:, hf * M_HEADS:(hf + 1) * M_HEADS].unsqueeze(2).broadcast_to((P, M_HEADS, M_DIM)), ALU.mult)
                o.then_inc(s["m_osaved"], 1)
                dve.wait_ge(s["m_y"], u + 1)
                at = baseT[:, bass.ds(u * T, T)]
                nc.vector.scalar_tensor_tensor(out=at, in0=bank[1][:, T:2 * T], scalar=m_bo[:, 0:1], in1=at,
                                               op0=ALU.add, op1=ALU.add).then_inc(s["m_x"], 1)

            mid_unit(0)
            with dve.Fori(1, B) as u:
                mid_unit(u)

            ln_vector_plain(dve, nc, ln_sems["ln_out"], bank, f_rstd, xT, s["f_x"])
            with dve.Fori(0, DEPTH) as layer:
                layer_body(1, layer)
            add_half(1)
            for c in range(CHUNKS):
                dve.wait_ge(s["out_turned"], c + 1)
                nc.vector.tensor_copy(normed[:, c * CHUNK:(c + 1) * CHUNK], bank[4 + c]).then_inc(s["out_kept"], 1)

        @block.gpsimd
        def _(pool):
            def split_weights(G0, placed):
                if placed is not None:
                    pool.wait_ge(s["band_ready"], placed)
                for g in range(GROUPS):
                    cols = slice(g * 3 * GCOLS, (g + 1) * 3 * GCOLS)
                    pool.wait_ge(s["w_rounded"], G0 * GROUPS + g + 1)
                    nc.gpsimd.tensor_tensor(w_lo[:, cols], wqkv[:, cols], w_hi[:, cols].bitcast(F32), ALU.subtract).then_inc(s["w_split"], 1)

            def place_probs(N, summed, used):
                if summed is not None:
                    pool.wait_ge(s["rotated_ready"], summed)
                pool.wait_ge(s["prec_ready"], N - 1)
                if used is not None:
                    pool.wait_ge(s["pt_ready"], used)
                for j in range(P // WINDOW):
                    r = slice(j * WINDOW, (j + 1) * WINDOW)
                    to = nc.gpsimd.tensor_tensor(band[r, :, j * WINDOW:j * WINDOW + KEYS], probs[r, :, :],
                                                 prec[r, :].unsqueeze(2).broadcast_to((WINDOW, 2 * GH, KEYS)), ALU.mult)
                to.then_inc(s["band_ready"], 1)

            def step(S0, g, first):
                N = S0 + g
                stage = stages(g, first)
                if stage[2]:
                    place_probs(N, N, N - 2 if stage[3] else None)
                pool.wait_ge(s["rotated_parts"], N + 1)
                if stage[1]:
                    pool.wait_ge(s["qk_normed"], N)
                if stage[2]:
                    pool.wait_ge(s["band_ready"], N - 1)
                nc.gpsimd.tensor_tensor(rotated[:, :], rot_a[:, :], rot_b[:, :], ALU.add).then_inc(s["rotated_ready"], 1)

            def layer_body(stack, layer, following):
                S0 = stack * DEPTH * STEPS + layer * STEPS
                for g in range(GROUPS):
                    step(S0, g, True)
                with pool.Fori(1, B) as u:
                    for g in range(GROUPS):
                        step(S0 + u * GROUPS, g, False)
                N = S0 + STEPS
                place_probs(N, N, N - 2)
                place_probs(N + 1, None, N - 1)
                if following:
                    split_weights(stack * DEPTH + layer + 1, N)

            pool.wait_ge(s["consts_ready"], 1)
            split_weights(0, None)
            with pool.Fori(0, DEPTH) as layer:
                layer_body(0, layer, True)
            with pool.Fori(0, DEPTH - 1) as layer:
                layer_body(1, layer, True)
            layer_body(1, DEPTH - 1, False)


def ln_vector_plain(dve, nc, q, bank, f_rstd, dst, done):
    for c in range(CHUNKS):
        dve.wait_ge(q["rstd"], c + 1)
        nc.vector.tensor_tensor(dst[:, c * CHUNK:(c + 1) * CHUNK], bank[c % 2], f_rstd[:, c % 2, :], ALU.mult).then_inc(q["scaled"], 1)
        dve.wait_ge(q["scaled"], c + 1)
        dve.sem_inc(done, 1)


_AS_THEY_ARE = ["L0_attn_x", "L0_attn_Wq", "L0_attn_bq", "L0_attn_Wk", "L0_attn_bk", "L0_attn_Wv", "L0_attn_bv", "L0_attn_Wo",
                "L0_attn_bo", "L0_ffn_Wo", "L0_ffn_W1", "L0_ffn_W2"]


def laid_out(inputs):
    arrays = {n: np.ascontiguousarray(inputs[n]) for n in _AS_THEY_ARE}
    w = np.asarray(inputs["L0_ffn_Wqkv"])
    w = w.reshape(DEPTH, DIM, 3, GROUPS, GCOLS).transpose(0, 1, 3, 2, 4)
    arrays["wqkv"] = np.ascontiguousarray(w.reshape(DEPTH, DIM, 3 * INNER))
    scales = np.stack([np.asarray(inputs[n]) for n in ("L0_ffn_q_scale", "L0_ffn_k_scale")], axis=1)
    swapped = scales.reshape(DEPTH, 2, 2, HALF)[:, :, ::-1].reshape(DEPTH, 2, DIM_HEAD)
    rows = np.stack([scales, swapped], axis=1).reshape(DEPTH, 1, 2, 2 * DIM_HEAD)
    arrays["qk_rows"] = np.ascontiguousarray(np.tile(rows, (1, P, 1, 1)))
    cols = [np.asarray(inputs[n]) for n in ("L0_ffn_ln_g", "L0_ffn_ln_b", "L0_ffn_b2")]
    b1 = np.asarray(inputs["L0_ffn_b1"])
    for part in range(2):
        for m, rows in enumerate(FFN_ROWS):
            o = part * DIM_INNER + m * P
            cols.append(np.pad(b1[:, o:o + rows], ((0, 0), (0, P - rows))))
    arrays["ffn_cols"] = np.ascontiguousarray(np.stack(cols, axis=2))
    return arrays


def kernel(**inputs):
    import concourse.bacc as _bacc
    from concourse.bass_utils import run_bass_kernel_spmd as _run

    nc = _bacc.Bacc("TRN2", target_bir_lowering=False, num_devices=1)
    arrays, io = {}, {}
    for name, a in laid_out(inputs).items():
        arrays[f"in_{name}"] = a
        io[name] = nc.dram_tensor(f"in_{name}", a.shape, mybir.dt.from_np(a.dtype), kind="ExternalInput").ap()
    io["out"] = nc.dram_tensor("out_0", (B, T, DIM), F32, kind="ExternalOutput").ap()
    build_macaron(nc, io)
    r = _run(nc, [arrays], core_ids=[0])
    return r.results[0]["out_0"]
```

```python
from contextlib import ExitStack

import numpy as np

import concourse.bass as bass
from concourse import mybir

F32 = mybir.dt.float32
F32R = mybir.dt.float32r
BF16 = mybir.dt.bfloat16
ALU = mybir.AluOpType
ACT = mybir.ActivationFunctionType
AX_X = mybir.AxisListType.X

P = 128
DIM = 128
DEPTH = 6
HEADS = 16
DIM_HEAD = 64
HALF = DIM_HEAD // 2
WINDOW = 32
INNER = HEADS * DIM_HEAD
DIM_INNER = int(DIM * 4 * 2 / 3)
QK_SCALE = 8.0
M_HEADS = 16
M_GROUPS = 4
M_DIM = DIM // M_HEADS
M_REP = M_HEADS // M_GROUPS
B = 8
T = 256
TOKENS = B * T
TILES = T // P
GH = 4
PAIRS = GH * DIM_HEAD // P
GCOLS = GH * DIM_HEAD
GROUPS = HEADS // GH
LAYERS = 2 * DEPTH
UNITS = DEPTH * B
KEYS = 2 * WINDOW
BAND = P + WINDOW
KPAD = T + WINDOW
CHUNK = 512
CHUNKS = TOKENS // CHUNK
FFN_ROWS = [128, 128, DIM_INNER - 256]
FFN_BLOCKS = len(FFN_ROWS)
MASKED = -1.0e30
LN_EPS = 1e-5
INV_NORM_MAX = 1e12
SQ_SCALE = 2.0**16
ACT_SET = "natural_log_exp_and_others"
GELU_SET = "gelu_and_others"
LN2 = 0.6931471805599453
M_CHUNK_HEADS = 4
M_CHUNKS = M_HEADS // M_CHUNK_HEADS


def chunk_heads(c):
    first = c // 2 * 2
    return [(first + b, c % 2 * 2 + j) for b in range(2) for j in range(2)]


def rotary_constants():
    f = np.float32
    half = np.arange(0, DIM_HEAD, 2, dtype=f)
    inv_freq = f(1.0) / np.power(f(10000.0), half / f(DIM_HEAD))
    t = np.arange(T, dtype=f)
    angle = (t[:, None] * inv_freq[None, :]).astype(f)
    base = ((half + f(0.4 * DIM_HEAD)) / f(1.4 * DIM_HEAD)).astype(f)
    power = ((t - f(T // 2)) / f(WINDOW // 2)).astype(f)
    scale = np.power(base[None, :], power[:, None]).astype(f)
    cos, sin = np.cos(angle), np.sin(angle)
    for_qk = (scale * f(QK_SCALE), f(1.0) / scale)
    own = np.stack([np.concatenate([cos * s, cos * s], 1) for s in for_qk], 1)
    partner = np.stack([np.concatenate([-sin * s, sin * s], 1) for s in for_qk], 1)
    rows = np.stack([own, partner], 1).reshape(TILES, P, 2, 2, DIM_HEAD).transpose(1, 2, 0, 3, 4)
    return np.ascontiguousarray(rows.astype(f))


def window_mask():
    a = np.arange(P)[:, None, None] % WINDOW
    window = np.arange(2)[None, :, None] * (P // WINDOW) + np.arange(P)[:, None, None] // WINDOW
    k = np.arange(KEYS)[None, None, :]
    seen = (k >= a) & (k <= a + WINDOW) & ((window > 0) | (k >= WINDOW))
    return np.where(seen, 0.0, MASKED).astype(np.float32)


def middle_rotary():
    f = np.float32
    freq = np.exp(-(np.arange(0, M_DIM, 2, dtype=f) / f(M_DIM)) * np.log(f(10000.0))).astype(f)
    angle = (np.arange(T, dtype=f)[:, None] * freq).astype(f)
    d = np.arange(P) % M_DIM
    cos, sin = np.cos(angle)[:, d // 2].T, np.sin(angle)[:, d // 2].T
    return np.ascontiguousarray(np.stack([cos, np.where(d % 2 == 0, -1.0, 1.0)[:, None] * sin], 1).astype(f))


def constants():
    f = np.float32
    own_head = np.where(np.arange(P)[:, None] // M_DIM % M_REP == np.arange(M_REP)[None, :], M_DIM**-0.5, 0.0).astype(f)
    own_group = (np.arange(P)[:, None] // (M_REP * M_DIM) == np.arange(M_GROUPS)[None, :]).astype(f)
    causal = np.where(np.arange(P)[None, :] <= np.arange(P)[:, None], 0.0, MASKED).astype(f)
    return {
        "identity": np.eye(P, dtype=f),
        "centre": (np.eye(P) - 1.0 / P).astype(f),
        "average": np.full((P, P), 1.0 / P, f),
        "rotary": rotary_constants().reshape(P, -1),
        "mask": window_mask().reshape(P, -1),
        "m_rotary": middle_rotary().reshape(P, -1),
        "own_head": own_head,
        "own_group": own_group,
        "causal": causal,
    }


def build_macaron(nc, io):
    out = io["out"]
    values = constants()
    const_dram = {n: nc.inline_tensor(v, name="const_" + n).ap() for n, v in values.items()}

    with ExitStack() as ctx:
        def sb(name, shape, dt=F32):
            return ctx.enter_context(nc.sbuf_tensor(name, shape, dt))

        def sem(name):
            return ctx.enter_context(nc.semaphore(name))

        ps_pair = [ctx.enter_context(nc.psum_tensor(f"ps_pair{i}", [P, 2, 512], F32)) for i in range(4)]
        bank = [ps_pair[i // 2][:, i % 2, :] for i in range(8)]

        m_out = bank[0].rearrange("p (a n) -> p a n", a=2)[:, :, 0:M_HEADS * (M_DIM + 1)].rearrange("p a (h d) -> p a h d", d=M_DIM + 1)

        cst = {n: sb("c_" + n, list(v.shape)) for n, v in values.items()}
        ident = cst["identity"]
        rot = cst["rotary"][:, :].rearrange("p (r a n) -> p r a n", r=2, a=TILES)
        ident_bf = sb("ident_bf", [P, P], BF16)
        mask_bf = sb("mask_bf", [P, 2, KEYS], BF16)
        causal_bf = sb("causal_bf", [P, P], BF16)
        eps_col = sb("eps_col", [P, 1])
        rnorm_col = sb("rnorm_col", [P, 1])

        xT = sb("xT", [P, TOKENS])
        baseT = sb("baseT", [P, TOKENS])
        by_token = sb("by_token", [P, TOKENS])

        wqkv = sb("wqkv", [P, 3 * INNER])
        w_hi = sb("w_hi", [P, 3 * INNER], F32R)
        w_lo = sb("w_lo", [P, 3 * INNER], F32R)
        wo = sb("wo", [P, INNER // P, DIM])
        w1 = sb("w1", [P, 2 * DIM_INNER])
        w1_hi = sb("w1_hi", [P, 2 * DIM_INNER], F32R)
        w1_lo = sb("w1_lo", [P, 2 * DIM_INNER], F32R)
        w2 = sb("w2", [P, FFN_BLOCKS, DIM])
        ln_cols = sb("ln_cols", [P, 2])
        b1 = sb("b1", [P, 2, FFN_BLOCKS])
        b2 = sb("b2", [P, 1])
        qk_rows = sb("qk_rows", [P, 2, 2 * DIM_HEAD])

        xs_hi = sb("xs_hi", [P, T], F32R)
        xs_lo = sb("xs_lo", [P, T], F32R)
        tab_a = sb("tab_a", [P, TILES, 2 * DIM_HEAD])
        tab_b = sb("tab_b", [P, TILES, 2 * DIM_HEAD])
        squares = sb("squares", [P, TILES * 2 * GCOLS])
        rot_a = sb("rot_a", [P, TILES * 2 * GCOLS])
        rot_b = sb("rot_b", [P, TILES * 2 * GCOLS])
        rotated = sb("rotated", [P, TILES * 2 * GCOLS])
        qk_norm = sb("qk_norm", [P, TILES * 2 * GCOLS])
        sqsum = sb("sqsum", [P, TILES * 2 * GH])
        rnorm = sb("rnorm", [P, TILES * 2 * GH])
        qfin = sb("qfin", [P, PAIRS, T])
        kblock = sb("kblock", [P, PAIRS, 2, KPAD])
        nmax = sb("nmax", [P, 2 * GH])
        probs = sb("probs", [P, 2, 2 * GH, KEYS])
        psum_row = sb("psum_row", [P, 2 * GH])
        prec = sb("prec", [P, 2, 2 * GH])
        band = sb("band", [P, 2, 2 * GH, BAND])
        bandT = sb("bandT", [P, GH, P + WINDOW + P])
        vals = sb("vals", [P, 4, 2, GH * DIM_HEAD])
        outT = sb("outT", [P, INNER // P, T])

        f_in = sb("f_in", [P, T])
        f_sq = sb("f_sq", [P, T])
        f_rstd = sb("f_rstd", [P, T])
        f_scaled = sb("f_scaled", [P, T])
        f_hi = sb("f_hi", [P, T], F32R)
        f_lo = sb("f_lo", [P, T], F32R)
        f_gelu = sb("f_gelu", [P, FFN_BLOCKS, T])
        f_h = sb("f_h", [P, FFN_BLOCKS, T])
        ln_sq = sb("ln_sq", [P, 2, CHUNK])
        ln_rstd = sb("ln_rstd", [P, 2, CHUNK])

        m_w = sb("m_w", [P, 4, P])
        m_wk = sb("m_wk", [P, 2 * M_GROUPS * M_DIM])
        m_wo = sb("m_wo", [P, DIM])
        m_bo = sb("m_bo", [P, 1])
        m_brow = sb("m_brow", [1, 4, P])
        m_bin = sb("m_bin", [1, P + 2 * M_GROUPS * M_DIM])
        ones_row = sb("ones_row", [1, T])
        m_h = sb("m_h", [P, T])
        m_rot = rot_a[:, :]
        m_rope = sb("m_rope", [P, 2, 2, T])
        m_qblock = sb("m_qblock", [P, 2, M_GROUPS, T])
        m_kblock = sb("m_kblock", [P, 2, M_REP, T])
        m_v = sb("m_v", [P, 2, 2, M_GROUPS, M_DIM + 1])
        m_bcol = sb("m_bcol", [P, 4])
        m_nmax = sb("m_nmax", [P, 2, M_CHUNK_HEADS])
        m_rec = sb("m_rec", [P, 2 * M_HEADS])
        m_e = [x[:, :].rearrange("p (h t) -> p h t", h=M_CHUNK_HEADS) for x in (rot_b, squares)]
        m_pT = [x[:, :].rearrange("p (k h q) -> p k h q", k=2, h=M_CHUNK_HEADS) for x in (rotated, qk_norm)]
        m_o = sb("m_o", [P, 2, DIM])
        m_oT = sb("m_oT", [P, T])

        s = {n: sem(n) for n in (
            "consts_loaded", "x_loaded", "consts_ready", "m_loaded",
            "w_qkv_loaded", "w_o_loaded", "w_scale_loaded", "w_ln_loaded", "w_1_loaded", "w_b1_loaded", "w_2_loaded",
            "x_turned", "x_kept", "out_summed", "out_turned", "out_kept", "out_stored",
            "w_rounded", "w_split", "xs_ready", "xs_split", "tables_ready",
            "qk_ready", "v_ready", "qk_turned", "s_ready", "pt_ready", "pv_ready", "y_ready",
            "squared", "v_saved", "qk_kept", "exped", "lookback_saved", "pt_saved", "sqsum_logged", "rnorm_ready", "out_saved",
            "rotated_parts", "sqsum_ready", "qk_normed", "x_updated", "max_ready", "shifted_scores", "sum_ready", "prec_ready",
            "rotated_ready", "band_ready",
            "f_copied", "w_1_rounded", "w_1_split", "f_centred", "f_squared", "f_var", "f_logged", "f_rstd_ready", "f_scaled", "f_rounded", "f_normed",
            "f_gates", "f_gelued", "f_values", "f_mixed", "f_y", "f_x",
            "m_copied", "m_k", "m_q", "m_kparts", "m_qparts", "m_kroped", "m_qroped", "m_qblocked", "m_kblocked", "m_vdone", "m_vsaved",
            "m_bturned", "m_bsaved", "m_scores", "m_maxed", "m_exped", "m_recd",
            "m_turned", "m_tsaved", "m_pv", "m_osaved", "m_oturned", "m_otsaved", "m_y", "m_x", "m_prepared",
        )}
        ln_sems = {f: {n: sem(f"{f}_{n}") for n in ("centred", "squared", "var", "logged", "rstd", "scaled")}
                   for f in ("ln_in", "ln_mid", "ln_out")}

        def final_before(stack):
            return stack + 1

        def each_unit(engine, stack, unit):
            U0, G0 = stack * UNITS, stack * DEPTH

            def a_layer(layer, lag, more):
                for u in range(3):
                    unit(U0 + layer * B + u, u, G0 + layer, min(lag + u, 3), more)
                with engine.Fori(3, B - 1) as u:
                    unit(U0 + layer * B + u, u, G0 + layer, 3, more)
                unit(U0 + layer * B + B - 1, B - 1, G0 + layer, 3, more)

            a_layer(0, 0, True)
            if stack == 0:
                with engine.Fori(1, DEPTH) as layer:
                    a_layer(layer, 3, True)
            else:
                with engine.Fori(1, DEPTH - 1) as layer:
                    a_layer(layer, 3, True)
                a_layer(DEPTH - 1, 3, False)

        def each_sequence(engine, unit):
            for u in range(2):
                unit(u, u, u == 0, False)
            with engine.Fori(1, B // 2 - 1) as pair:
                for parity in range(2):
                    unit(pair * 2 + parity, parity, False, False)
            for u in range(B - 2, B):
                unit(u, u % 2, False, u == B - 1)

        def stages(g, lag):
            return [lag >= 1 or g >= k for k in range(5)]

        def old_weights(u, units):
            return isinstance(u, int) and u < units

        def prepared_weights(u, g, more):
            if isinstance(u, int) and u == B - 1 and more and g in (1, 2):
                return g - 1, 1
            if isinstance(u, int) and u == 0 and g in (0, 1):
                return g + 2, 0
            return None

        ln_banks = [bank[i] for i in (0, 1, 3, 4)]

        def ln_tensor(pe, q, src, started):
            def centre(c):
                pe.wait_ge(started[0], started[1] + (c + 1 if started[2] else 0))
                pe.matmul(ln_banks[c], cst["centre"][:, :], src[:, c * CHUNK:(c + 1) * CHUNK],
                          start=True, stop=True).then_inc(q["centred"], 1)

            def variance(c):
                pe.wait_ge(q["squared"], c + 1)
                if c >= 1:
                    pe.wait_ge(q["logged"], c)
                pe.matmul(bank[5], cst["average"][:, :], ln_sq[:, c % 2, :],
                          start=True, stop=True).then_inc(q["var"], 1)

            return centre, variance

        def ln_scalar(act, q):
            def square(c):
                act.wait_ge(q["centred"], c + 1)
                if c >= 2:
                    act.wait_ge(q["var"], c - 1)
                act.activation(ln_sq[:, c % 2, :], ln_banks[c], ACT.Square).then_inc(q["squared"], 1)

            def rstd(c):
                act.wait_ge(q["var"], c + 1)
                if c >= 2:
                    act.wait_ge(q["scaled"], c - 1)
                act.activation(ln_rstd[:, c % 2, :], bank[5], ACT.Ln, bias=eps_col[:, 0:1]).then_inc(q["logged"], 1)
                act.wait_ge(q["logged"], c + 1)
                act.activation(ln_rstd[:, c % 2, :], ln_rstd[:, c % 2, :], ACT.Exp, scale=-0.5).then_inc(q["rstd"], 1)

            return square, rstd

        def ln_vector(dve, q, dst):
            for c in range(CHUNKS):
                dve.wait_ge(q["rstd"], c + 1)
                nc.vector.tensor_tensor(dst[:, c * CHUNK:(c + 1) * CHUNK], ln_banks[c], ln_rstd[:, c % 2, :], ALU.mult).then_inc(q["scaled"], 1)

        def one_behind(first, second):
            for c in range(CHUNKS + 1):
                if c < CHUNKS:
                    first(c)
                if c >= 1:
                    second(c - 1)

        block = ctx.enter_context(nc.Block())

        @block.sync
        def _(sp):
            for n in values:
                sp.dma_start(cst[n][:, :], const_dram[n]).then_inc(s["consts_loaded"], 16)
            x_in = io["L0_attn_x"].rearrange("b (h p) d -> p (b h) d", p=P)
            sp.dma_start(by_token[:, :].rearrange("p (n d) -> p n d", d=DIM), x_in).then_inc(s["x_loaded"], 16)

            def load_layer(G, final):
                layer = G % DEPTH
                at = bass.ds(layer, 1)
                if final is not None:
                    sp.wait_ge(s["tables_ready"], G)
                sp.dma_start(qk_rows[:, :, :], io["qk_rows"][at, :, :, :].rearrange("l p a n -> p (l a) n")).then_inc(s["w_scale_loaded"], 16)
                if final is not None:
                    sp.wait_ge(s["w_split"], G * GROUPS)
                sp.dma_start(wqkv[:, :], io["wqkv"][at, :, :].rearrange("l p n -> p (l n)")).then_inc(s["w_qkv_loaded"], 16)
                if final is not None:
                    sp.wait_ge(s["y_ready"], 2 * G * B)
                sp.dma_start(wo[:, :, :], io["L0_ffn_Wo"][at, :, :].rearrange("l (c p) n -> p (l c) n", p=P)).then_inc(s["w_o_loaded"], 16)
                if final is not None:
                    sp.wait_ge(s["f_normed"], G * B)
                cols = io["ffn_cols"][at, :, :].rearrange("l p n -> p (l n)")
                sp.dma_start(ln_cols[:, :], cols[:, 0:2]).then_inc(s["w_ln_loaded"], 16)
                if final is not None:
                    sp.wait_ge(s["w_1_split"], G)
                sp.dma_start(w1[:, :], io["L0_ffn_W1"][at, :, :].rearrange("l p n -> p (l n)")).then_inc(s["w_1_loaded"], 16)
                if final is not None:
                    sp.wait_ge(s["f_mixed"], G * B)
                sp.dma_start(b1[:, :, :].rearrange("p a m -> p (a m)"), cols[:, 3:]).then_inc(s["w_b1_loaded"], 16)
                if final is not None:
                    sp.wait_ge(s["f_x"], final + G * B)
                w2_l = io["L0_ffn_W2"][at, :, :].rearrange("l k n -> (l k) n")
                sp.dma_start(w2[:, 0:2, :], w2_l[0:2 * P, :].rearrange("(c p) n -> p c n", p=P)).then_inc(s["w_2_loaded"], 16)
                sp.dma_start(w2[0:FFN_ROWS[2], 2, :], w2_l[2 * P:DIM_INNER, :]).then_inc(s["w_2_loaded"], 16)
                sp.dma_start(b2[:, :], cols[:, 2:3], allow_slow_non_contiguous=True).then_inc(s["w_2_loaded"], 16)

            load_layer(0, None)
            sp.dma_start(m_w[:, 0, :], io["L0_attn_Wq"]).then_inc(s["m_loaded"], 16)
            sp.dma_start(m_wk[:, 0:32], io["L0_attn_Wk"]).then_inc(s["m_loaded"], 16)
            sp.dma_start(m_wk[:, 32:64], io["L0_attn_Wv"]).then_inc(s["m_loaded"], 16)
            sp.dma_start(m_wo[:, :], io["L0_attn_Wo"]).then_inc(s["m_loaded"], 16)
            sp.dma_start(m_bo[:, :], io["L0_attn_bo"].rearrange("(p a) -> p a", a=1), allow_slow_non_contiguous=True).then_inc(s["m_loaded"], 16)
            sp.dma_start(m_bin[:, 0:128], io["L0_attn_bq"].rearrange("(a p) -> a p", a=1)).then_inc(s["m_loaded"], 16)
            sp.dma_start(m_bin[:, 128:160], io["L0_attn_bk"].rearrange("(a p) -> a p", a=1)).then_inc(s["m_loaded"], 16)
            sp.dma_start(m_bin[:, 160:192], io["L0_attn_bv"].rearrange("(a p) -> a p", a=1)).then_inc(s["m_loaded"], 16)
            with sp.Fori(1, DEPTH + 1) as G:
                load_layer(G, final_before(0))
            with sp.Fori(DEPTH + 1, LAYERS) as G:
                load_layer(G, final_before(1))
            to = out.rearrange("b (h p) d -> p (b h) d", p=P)
            n = CHUNK // P
            for c in range(CHUNKS):
                sp.wait_ge(s["out_kept"], c + 1)
                sp.dma_start(to[:, c * n:(c + 1) * n, :],
                             by_token[:, c * CHUNK:(c + 1) * CHUNK].rearrange("p (n d) -> p n d", d=DIM)).then_inc(s["out_stored"], 16)
            sp.wait_ge(s["out_stored"], CHUNKS * 16)

        @block.tensor
        def _(pe):
            def split_product(to, tile, cols):
                at = slice(tile * P, (tile + 1) * P)
                pe.matmul(to, xs_hi[:, at], w_hi[:, cols], start=True, stop=False)
                pe.matmul(to, xs_hi[:, at], w_lo[:, cols], start=False, stop=False)
                return pe.matmul(to, xs_lo[:, at], w_hi[:, cols], start=False, stop=True)

            def proj_qk(N, g, first):
                if not (first and g == 0):
                    pe.wait_ge(s["rotated_parts"], N)
                for tile in range(TILES):
                    mm = split_product(bank[tile], tile, slice(g * 3 * GCOLS, g * 3 * GCOLS + 2 * GCOLS))
                mm.then_inc(s["qk_ready"], 1)

            def proj_v(N, g, first):
                if not first:
                    pe.wait_ge(s["out_saved"], N - 3)
                elif g >= 1:
                    pe.wait_ge(s["v_saved"], N)
                for tile in range(TILES):
                    mm = split_product(bank[6][:, tile * GCOLS:(tile + 1) * GCOLS], tile,
                                       slice(g * 3 * GCOLS + 2 * GCOLS, (g + 1) * 3 * GCOLS))
                mm.then_inc(s["v_ready"], 1)

            def turn_qk(N, saved):
                if saved:
                    pe.wait_ge(s["pt_saved"], N - 3)
                pe.wait_ge(s["qk_normed"], N)
                for pair in range(PAIRS):
                    for i in range(2):
                        for tile in range(TILES):
                            at = ((tile * 2 + i) * PAIRS + pair) * P
                            mm = pe.transpose(bank[4 + pair][:, (i * TILES + tile) * P:(i * TILES + tile + 1) * P], qk_norm[:, at:at + P], ident[:, :])
                mm.then_inc(s["qk_turned"], 1)

            def scores(N, g, first):
                if not (first and g == 1):
                    pe.wait_ge(s["shifted_scores"], N - 1)
                pe.matmul(bank[3].rearrange("p (f h k) -> p f h k", f=2, h=GH), ident_bf[:, :],
                          mask_bf[:, :, :].unsqueeze(2).broadcast_to((P, 2, GH, KEYS)), start=True, stop=False,
                          skip_group_check=True)
                pe.wait_ge(s["qk_kept"], N)
                for pair in range(PAIRS):
                    for hf in range(2):
                        for j in range(P // WINDOW):
                            w = hf * (P // WINDOW) + j
                            at = (hf * GH + 2 * pair) * KEYS
                            mm = pe.matmul(bank[3][j * WINDOW:(j + 1) * WINDOW, at:at + 2 * KEYS],
                                           qfin[:, pair, w * WINDOW:(w + 1) * WINDOW],
                                           kblock[:, pair, :, w * WINDOW:w * WINDOW + KEYS],
                                           start=False, stop=True, skip_group_check=True)
                mm.then_inc(s["s_ready"], 1)

            def turn_probs(N, g, bank_read=None):
                pe.wait_ge(s["band_ready"], N - 2)
                if bank_read is not None:
                    pe.wait_ge(*bank_read)
                own = band[:, (g - 3) % 2, :, :]
                for h in range(GH):
                    pe.transpose(bank[4][:, h * P:(h + 1) * P], own[:, h, WINDOW:BAND], ident[:, :])
                    pe.transpose(bank[5][:, h * P:(h + 1) * P], own[:, GH + h, WINDOW:BAND], ident[:, :])
                flat = own.rearrange("p i k -> p (i k)")
                for h in range(GH):
                    at = (GH + h) * BAND + WINDOW - P
                    mm = pe.transpose(bank[7][:, h * WINDOW:(h + 1) * WINDOW], flat[0:WINDOW, at:at + P], ident[0:WINDOW, 0:WINDOW])
                mm.then_inc(s["pt_ready"], 1)

            def attend(N, g, values, turned):
                if turned is not None:
                    pe.wait_ge(s["pt_saved"], turned)
                pe.wait_ge(s["v_saved"], values)
                slot = g % 4
                for pair in range(PAIRS):
                    for hf in range(2):
                        for odd in range(2):
                            h = 2 * pair + odd
                            to = bank[6][odd * 64:(odd + 1) * 64, pair * T:(pair + 1) * T]
                            v = vals[:, slot, hf, h * DIM_HEAD:(h + 1) * DIM_HEAD]
                            if hf == 0:
                                mm = pe.matmul(to[:, 0:BAND], v, bandT[:, h, 0:BAND], start=True, stop=False, skip_group_check=True)
                            else:
                                mm = pe.matmul(to[:, P:T], v, bandT[:, h, BAND:BAND + P], start=False, stop=True, skip_group_check=True)
                mm.then_inc(s["pv_ready"], 1)

            def project_half(half, saved, turned):
                if saved is not None:
                    pe.wait_ge(s["out_saved"], saved)
                    pe.wait_ge(s["lookback_saved"], turned)
                n = INNER // P // 2
                for i in range(n):
                    c = half * n + i
                    mm = pe.matmul(bank[7][:, T:2 * T], wo[:, c, :], outT[:, c, :], start=(i == 0), stop=(i == n - 1))
                mm.then_inc(s["y_ready"], 1)

            f_at = (bank[2][:, 0:T], bank[2][:, T:2 * T], bank[7][:, T:2 * T])

            def feed_centre(U, final):
                pe.wait_ge(s["f_copied"], U - 1)
                pe.wait_ge(s["f_x"], final)
                pe.matmul(f_at[0], cst["centre"][:, :], f_in[:, :], start=True, stop=True).then_inc(s["f_centred"], 1)

            def feed_variance(U):
                pe.wait_ge(s["f_squared"], U - 1)
                pe.matmul(f_at[1], cst["average"][:, :], f_sq[:, :], start=True, stop=True).then_inc(s["f_var"], 1)

            def feed_product(m, o, rows):
                cols = slice(o, o + rows)
                pe.matmul(f_at[m][0:rows, :], w1_hi[:, cols], f_hi[:, :], start=True, stop=False)
                pe.matmul(f_at[m][0:rows, :], w1_lo[:, cols], f_hi[:, :], start=False, stop=False)
                return pe.matmul(f_at[m][0:rows, :], w1_hi[:, cols], f_lo[:, :], start=False, stop=True)

            def feed_gates(U, u, G, updated, turned):
                if not old_weights(u, 2):
                    pe.wait_ge(s["w_1_split"], G + 1)
                pe.wait_ge(s["f_normed"], U - 1)
                pe.wait_ge(s["x_updated"], updated)
                pe.wait_ge(s["lookback_saved"], turned)
                for m, rows in enumerate(FFN_ROWS):
                    mm = feed_product(m, DIM_INNER + m * P, rows)
                mm.then_inc(s["f_gates"], 1)

            def feed_values(U):
                pe.wait_ge(s["f_gelued"], U - 1)
                for m, rows in enumerate(FFN_ROWS):
                    mm = feed_product(m, m * P, rows)
                mm.then_inc(s["f_values"], 1)

            def feed_down(U, u, G):
                if not old_weights(u, 3):
                    pe.wait_ge(s["w_2_loaded"], (G + 1) * 48)
                pe.wait_ge(s["f_mixed"], U - 2)
                for m, rows in enumerate(FFN_ROWS):
                    mm = pe.matmul(f_at[0], w2[0:rows, m, :], f_h[0:rows, m, :], start=(m == 0), stop=(m == FFN_BLOCKS - 1))
                mm.then_inc(s["f_y"], 1)

            def stack_body(stack):
                def unit(U, u, G, lag, more):
                    feed = lag >= 2
                    first = lag == 0
                    for g in range(GROUPS):
                        N = U * GROUPS + g
                        stage = stages(g, lag)
                        if g == 0:
                            pe.wait_ge(s["xs_split"], U + stack + 1)
                        if old_weights(u, 1):
                            pe.wait_ge(s["w_split"], G * GROUPS + g + 1)
                        proj_qk(N, g, first)
                        if g == 3 and feed:
                            feed_gates(U, u, G, 2 * U - 1, N - 3)
                        if g == 2 and feed:
                            feed_variance(U)
                        if stage[1]:
                            turn_qk(N, stage[4])
                        if stage[4]:
                            attend(N, g, N, None)
                        if g == 0 and lag >= 2:
                            if not old_weights(u, 2):
                                pe.wait_ge(s["w_o_loaded"], (G + 1) * 16)
                            project_half(1, None, None)
                        if g == 1 and lag >= 3:
                            feed_down(U, u, G)
                        if g == 2 and lag >= 1:
                            if not old_weights(u, 1):
                                pe.wait_ge(s["w_o_loaded"], (G + 1) * 16)
                            project_half(0, None, None)
                        if g == 3 and feed:
                            feed_values(U)
                        proj_v(N, g, first)
                        if stage[1]:
                            scores(N, g, first)
                        if stage[3]:
                            read = None
                            if g == 0 and lag >= 2:
                                read = (s["x_updated"], 2 * U - 2)
                            elif g == 2 and lag >= 1:
                                read = (s["x_updated"], 2 * U - 1)
                            elif g == 3 and feed:
                                read = (s["f_mixed"], U - 1)
                            turn_probs(N, g, read)
                        if g == 1 and feed:
                            feed_centre(U, final_before(stack) + U - 2)

                pe.wait_ge(s["f_x"], final_before(stack) + stack * UNITS)
                each_unit(pe, stack, unit)

                U = (stack + 1) * UNITS
                G = stack * DEPTH + DEPTH
                N = U * GROUPS
                final = final_before(stack) + U
                turn_qk(N, True)
                attend(N, 0, N, None)
                feed_down(U, 0, G)
                project_half(1, N - 4, N - 3)
                scores(N, 0, False)
                feed_centre(U, final - 2)
                turn_probs(N, 0, (s["x_updated"], 2 * U - 2))
                feed_variance(U)
                attend(N + 1, 1, N, N - 2)
                turn_probs(N + 1, 1)
                project_half(0, N - 2, N - 1)
                attend(N + 2, 2, N, N - 1)
                feed_gates(U, 0, G, 2 * U - 1, N - 1)
                feed_values(U)
                turn_probs(N + 2, 2, (s["f_mixed"], U - 1))
                attend(N + 3, 3, N, N)
                project_half(1, N, N)
                feed_down(U + 1, 1, G)
                feed_centre(U + 1, final - 1)
                feed_variance(U + 1)
                if stack == 1:
                    turn_results(range(CHUNKS - 1))
                feed_gates(U + 1, 1, G, 2 * U, N)
                feed_values(U + 1)
                feed_down(U + 2, 2, G)

            def turn_results(chunks):
                for c in chunks:
                    pe.wait_ge(s["out_summed"], CHUNKS + c + 1)
                    for i in range(4):
                        t = c * 4 + i
                        mm = pe.transpose(bank[4 + c][:, i * P:(i + 1) * P], baseT[:, t * P:(t + 1) * P], ident[:, :])
                    mm.then_inc(s["out_turned"], 1)

            pe.wait_ge(s["consts_loaded"], 16 * len(values))
            pe.wait_ge(s["x_loaded"], 16)
            for c in range(CHUNKS):
                for i in range(4):
                    t = c * 4 + i
                    mm = pe.transpose(bank[4 + c][:, i * P:(i + 1) * P], by_token[:, t * P:(t + 1) * P], ident[:, :])
                mm.then_inc(s["x_turned"], 1)
            one_behind(*ln_tensor(pe, ln_sems["ln_in"], baseT, (s["x_kept"], 0, True)))
            pe.wait_ge(s["consts_ready"], 1)

            stack_body(0)

            one_behind(*ln_tensor(pe, ln_sems["ln_mid"], baseT, (s["out_summed"], 0, True)))
            pe.wait_ge(ln_sems["ln_mid"]["scaled"], CHUNKS)
            pe.wait_ge(s["m_prepared"], 1)
            for i in range(4):
                mm = pe.matmul(bank[3][:, i:i + 1], m_brow[:, i, :], ones_row[:, 0:1], start=True, stop=True)
            mm.then_inc(s["m_bturned"], 1)
            pe.wait_ge(s["m_bsaved"], 1)

            def m_project_k(u, first):
                pe.wait_ge(s["m_copied"], u + 1)
                if isinstance(u, int) and 1 <= u <= 2:
                    pe.wait_ge(s["m_qparts"], u)
                elif not first:
                    pe.wait_ge(s["m_x"], u - 2)
                for v in range(2):
                    mm = pe.matmul(bank[1][:, v * T:(v + 1) * T], m_w[:, 2 + v, :], m_h[:, :], start=True, stop=True)
                mm.then_inc(s["m_k"], 1)

            def m_project_v(u):
                pe.wait_ge(s["m_kparts"], u + 1)
                for hf in range(2):
                    to = bank[1][:, hf * 32:(hf + 1) * 32]
                    pe.matmul(to, m_h[:, hf * P:(hf + 1) * P], m_wk[:, 32:64], start=True, stop=False)
                    mm = pe.matmul(to, ones_row[:, 0:P], m_bin[:, 160:192], start=False, stop=True)
                mm.then_inc(s["m_vdone"], 1)

            def m_project_q(u):
                pe.wait_ge(s["m_vsaved"], u + 1)
                for v in range(2):
                    mm = pe.matmul(bank[1][:, v * T:(v + 1) * T], m_w[:, v, :], m_h[:, :], start=True, stop=True)
                mm.then_inc(s["m_q"], 1)

            def m_turn_out(u, q_read):
                pe.wait_ge(s["m_osaved"], u + 1)
                if q_read is not None:
                    pe.wait_ge(s["m_qparts"], q_read)
                for hf in range(2):
                    mm = pe.transpose(bank[1][:, hf * P:(hf + 1) * P], m_o[:, hf, :], ident[:, :])
                mm.then_inc(s["m_oturned"], 1)

            def m_project_out(u):
                pe.wait_ge(s["m_otsaved"], u + 1)
                pe.matmul(bank[1][:, T:2 * T], m_wo[:, :], m_oT[:, :], start=True, stop=True).then_inc(s["m_y"], 1)

            def m_attend_head(n, u, parity, i, first):
                blocks = i // M_CHUNKS + 1
                h, kb = n // blocks, n % blocks
                g, r = chunk_heads(i % M_CHUNKS)[h]
                mm = pe.matmul(m_out[:, blocks - 1, g * M_REP + r, :], m_pT[i % 2][:, kb, h, :], m_v[:, parity, kb, g, :],
                               start=(kb == 0), stop=(kb == blocks - 1), skip_group_check=True)
                if n == M_CHUNK_HEADS * blocks - 1:
                    mm.then_inc(s["m_pv"], 1)

            def m_scores(u, parity, i, first, between):
                K = u * 2 * M_CHUNKS + i
                hf, c = i // M_CHUNKS, i % M_CHUNKS
                nk = (hf + 1) * P
                t = ps_pair[1 + i % 2]
                if i == 0:
                    pe.wait_ge(s["m_qblocked"], u + 1)
                    pe.wait_ge(s["m_kblocked"], u + 1)
                if not first or i >= 2:
                    pe.wait_ge(s["m_exped"], K - 1)
                heads = chunk_heads(c)
                early = between is not None and between[2] >= M_CHUNKS
                if early:
                    pe.wait_ge(s["m_tsaved"], K - 2)
                for h, (g, r) in enumerate(heads):
                    to = t[:, h // 2, h % 2 * T:h % 2 * T + nk]
                    pe.matmul(to, m_qblock[:, parity, g, hf * P:(hf + 1) * P], m_kblock[:, parity, r, 0:nk],
                              start=True, stop=False, skip_group_check=True)
                    mm = pe.matmul(to[:, hf * P:nk], ident_bf[:, :], causal_bf[:, :], start=False, stop=True, skip_group_check=True)
                    if early:
                        m_attend_head(h, *between)
                mm.then_inc(s["m_scores"], 1)

            def m_turn(u, i, first, between):
                K = u * 2 * M_CHUNKS + i
                pe.wait_ge(s["m_exped"], K + 1)
                if not first or i >= 1:
                    pe.wait_ge(s["m_tsaved"], K)
                n = 0
                if between is not None:
                    early = between[2] >= M_CHUNKS
                    if between[2] == 0:
                        pe.wait_ge(s["m_vsaved"], between[0] + 1)
                        if not between[3]:
                            pe.wait_ge(s["m_osaved"], between[0])
                    n = M_CHUNK_HEADS if early else 0
                for kb in range(i // M_CHUNKS + 1):
                    for h in range(M_CHUNK_HEADS):
                        mm = pe.transpose(ps_pair[3][:, kb, h * P:(h + 1) * P], m_e[i % 2][:, h, kb * P:(kb + 1) * P], ident[:, :])
                        if between is not None and kb == 0:
                            m_attend_head(n + h, *between)
                mm.then_inc(s["m_turned"], 1)

            def mid_unit(u, parity, first, last):
                n = 2 * M_CHUNKS
                for i in range(n):
                    if i >= 3:
                        between = (u, parity, i - 3, first)
                    else:
                        between = None if first else (u - 1, 1 - parity, n - 3 + i, False)
                    m_scores(u, parity, i, first, between)
                    if i >= 1:
                        m_turn(u, i - 1, first, between)
                    elif not first:
                        m_turn(u - 1, n - 1, False, between)
                    if i == 1 and not last:
                        m_project_k(u + 1, False)
                    if i == 2 and not last:
                        m_project_v(u + 1)
                    if i == 3 and not last:
                        m_project_q(u + 1)
                    if i == 4 and not first:
                        m_turn_out(u - 1, None if last else u + 2)
                    if i == 5 and not first:
                        m_project_out(u - 1)

            m_project_k(0, True)
            m_project_v(0)
            m_project_q(0)
            each_sequence(pe, mid_unit)
            u, n = B - 1, 2 * M_CHUNKS
            pe.wait_ge(s["m_tsaved"], u * n + n - 2)
            for h in range(M_CHUNK_HEADS):
                m_attend_head(h, u, u % 2, n - 3, False)
            m_turn(u, n - 1, False, (u, u % 2, n - 3, False))
            for i in (n - 2, n - 1):
                pe.wait_ge(s["m_tsaved"], u * n + i + 1)
                for h in range(2 * M_CHUNK_HEADS):
                    m_attend_head(h, u, u % 2, i, False)
            m_turn_out(u, None)
            m_project_out(u)

            one_behind(*ln_tensor(pe, ln_sems["ln_out"], baseT, (s["m_x"], B, False)))
            stack_body(1)

            turn_results(range(CHUNKS - 1, CHUNKS))

        @block.scalar
        def _(act):
            def copy_shifted(u):
                nc.scalar.copy(xs_hi[0:64, :], xT[0:64, bass.ds(u * T, T)])
                nc.scalar.copy(xs_hi[64:P, 1:T], xT[64:P, bass.ds(u * T, T - 1)]).then_inc(s["xs_ready"], 1)

            def keep_qk(N, g, first):
                act.wait_ge(s["qk_turned"], N)
                if not (first and g == 1):
                    act.wait_ge(s["s_ready"], N - 1)
                turned = ps_pair[2]
                nc.scalar.copy(qfin[:, :, :], turned[:, :, 0:T])
                nc.scalar.copy(kblock[0:64, :, 0, WINDOW:KPAD], turned[0:64, :, T:2 * T])
                nc.scalar.copy(kblock[64:P, :, 1, WINDOW:KPAD], turned[64:P, :, T:2 * T]).then_inc(s["qk_kept"], 1)

            def save_out(N, g, projected):
                act.wait_ge(s["pv_ready"], N - 3)
                if projected is not None:
                    act.wait_ge(s["y_ready"], projected)
                gp = g % GROUPS
                nc.scalar.copy(outT[:, 2 * gp:2 * gp + 2, :].rearrange("p a t -> p (a t)"), bank[6]).then_inc(s["out_saved"], 1)

            def save_turned(N, used):
                act.wait_ge(s["pt_ready"], N - 2)
                if used is not None:
                    act.wait_ge(s["pv_ready"], used)
                nc.scalar.copy(bandT[:, :, P:BAND], bank[7][:, 0:P].rearrange("p (h q) -> p h q", h=GH)).then_inc(s["lookback_saved"], 1)
                nc.scalar.copy(bandT[:, :, 0:P], bank[4].rearrange("p (h q) -> p h q", h=GH))
                nc.scalar.copy(bandT[:, :, BAND:BAND + P], bank[5].rearrange("p (h q) -> p h q", h=GH)).then_inc(s["pt_saved"], 1)

            def exponentials(N, g):
                act.wait_ge(s["shifted_scores"], N - 1)
                own = probs[:, g % 2, :, :]
                nc.scalar.activation(own, own, ACT.Exp).then_inc(s["exped"], 1)

            def save_values(N, g):
                act.wait_ge(s["v_ready"], N + 1)
                nc.scalar.copy(vals[:, g, :, :].rearrange("p a n -> p (a n)"), bank[6]).then_inc(s["v_saved"], 1)

            def inverse_norms(N, first):
                act.wait_ge(s["sqsum_ready"], N + 1)
                if not first:
                    act.wait_ge(s["qk_normed"], N)
                nc.scalar.activation(rnorm[:, :], sqsum[:, :], ACT.Ln, scale=SQ_SCALE).then_inc(s["sqsum_logged"], 1)
                act.wait_ge(s["sqsum_logged"], N + 1)
                nc.scalar.activation(rnorm[:, :], rnorm[:, :], ACT.Exp, scale=-0.5,
                                     bias=rnorm_col[:, 0:1]).then_inc(s["rnorm_ready"], 1)

            def round_weights(G, g):
                if g == 0:
                    act.wait_ge(s["w_qkv_loaded"], G * 16 + 16)
                cols = slice(g * 3 * GCOLS, (g + 1) * 3 * GCOLS)
                nc.scalar.copy(w_hi[:, cols], wqkv[:, cols]).then_inc(s["w_rounded"], 1)

            def round_first_weights(G, used):
                act.wait_ge(s["w_1_loaded"], G * 16 + 16)
                if used is not None:
                    act.wait_ge(s["f_values"], used)
                nc.scalar.copy(w1_hi[:, :], w1[:, :]).then_inc(s["w_1_rounded"], 1)

            def feed_square(U):
                act.wait_ge(s["f_centred"], U - 1)
                nc.scalar.activation(f_sq[:, :], bank[2][:, 0:T], ACT.Square).then_inc(s["f_squared"], 1)

            def feed_rstd(U):
                act.wait_ge(s["f_var"], U - 1)
                nc.scalar.activation(f_rstd[:, :], bank[2][:, T:2 * T], ACT.Ln, bias=eps_col[:, 0:1]).then_inc(s["f_logged"], 1)
                act.wait_ge(s["f_logged"], U - 1)
                nc.scalar.activation(f_rstd[:, :], f_rstd[:, :], ACT.Exp, scale=-0.5).then_inc(s["f_rstd_ready"], 1)

            def feed_gelu(U, u, G):
                if not old_weights(u, 2):
                    act.wait_ge(s["w_b1_loaded"], (G + 1) * 16)
                act.wait_ge(s["f_gates"], U - 1)
                f_at = (bank[2][:, 0:T], bank[2][:, T:2 * T], bank[7][:, T:2 * T])
                for m, rows in enumerate(FFN_ROWS):
                    gelu = nc.scalar.activation(f_gelu[0:rows, m, :], f_at[m][0:rows, :], ACT.Gelu, bias=b1[0:rows, 1, m:m + 1])
                gelu.then_inc(s["f_gelued"], 1)

            def unit(U, u, G, lag, more):
                feed = lag >= 2
                first = lag == 0
                for g in range(GROUPS):
                    N = U * GROUPS + g
                    stage = stages(g, lag)
                    weights = prepared_weights(u, g, more)
                    act.wait_ge(s["qk_ready"], N + 1)
                    if not (first and g == 0):
                        act.wait_ge(s["sqsum_ready"], N)
                    nc.scalar.activation(squares[:, :].rearrange("p (a n) -> p a n", a=TILES), ps_pair[0][:, :, :],
                                         ACT.Square).then_inc(s["squared"], 1)
                    if weights:
                        round_weights(G + weights[1], weights[0])
                    if isinstance(u, int) and u == 2 and g == 1:
                        round_first_weights(G, U - 2 if lag >= 3 else None)
                    if feed and g == 3:
                        feed_gelu(U, u, G)
                    if stage[1]:
                        keep_qk(N, g, first)
                    if stage[4]:
                        save_out(N, g, {0: 2 * U - 3, 2: 2 * U - 2}.get(g) if lag >= 2 else None)
                    if stage[2] and not (feed and g == 3):
                        exponentials(N, g)
                    if feed and g == 2:
                        feed_rstd(U)
                    if g < 3:
                        inverse_norms(N, first and g == 0)
                        if feed and g == 2:
                            nc.scalar.preload_act_table_set(GELU_SET)
                        save_values(N, g)
                    else:
                        if feed:
                            nc.scalar.preload_act_table_set(ACT_SET)
                        act.wait_ge(s["v_ready"], N + 1)
                        copy_shifted((u + 1) % B)
                        inverse_norms(N, False)
                        if feed:
                            exponentials(N, g)
                    if stage[3]:
                        save_turned(N, N - 3 if stage[4] else None)
                    if feed and g == 1:
                        feed_square(U)

            def stack_body(stack):
                act.wait_ge(s["f_x"], final_before(stack) + stack * UNITS)
                copy_shifted(0)
                each_unit(act, stack, unit)

                U = (stack + 1) * UNITS
                G = stack * DEPTH + DEPTH
                N = U * GROUPS
                exponentials(N, 0)
                save_out(N, 0, 2 * U - 3)
                keep_qk(N, 0, False)
                exponentials(N + 1, 1)
                feed_square(U)
                save_turned(N, N - 3)
                feed_rstd(U)
                save_out(N + 1, 1, None)
                save_turned(N + 1, N - 2)
                save_out(N + 2, 2, 2 * U - 2)
                feed_gelu(U, 0, G)
                nc.scalar.preload_act_table_set(ACT_SET)
                save_turned(N + 2, N - 1)
                save_out(N + 3, 3, None)
                feed_square(U + 1)
                feed_rstd(U + 1)
                feed_gelu(U + 1, 1, G)

            nc.scalar.preload_act_table_set(ACT_SET)
            act.wait_ge(s["consts_ready"], 1)
            round_weights(0, 0)
            round_weights(0, 1)
            one_behind(*ln_scalar(act, ln_sems["ln_in"]))
            stack_body(0)

            nc.scalar.preload_act_table_set(ACT_SET)
            one_behind(*ln_scalar(act, ln_sems["ln_mid"]))

            def m_copy(u, first):
                if not first:
                    act.wait_ge(s["m_q"], u)
                nc.scalar.copy(m_h[:, :], xT[:, bass.ds(u * T, T)]).then_inc(s["m_copied"], 1)

            def m_save_values(u, parity):
                act.wait_ge(s["m_vdone"], u + 1)
                nc.scalar.copy(m_v[:, parity, :, :, 0:M_DIM].rearrange("p a g d -> p (a g) d"),
                               bank[1][:, 0:64].rearrange("p (n d) -> p n d", d=M_DIM)).then_inc(s["m_vsaved"], 1)

            def m_exponentials(u, i, first):
                K = u * 2 * M_CHUNKS + i
                nk = (i // M_CHUNKS + 1) * P
                act.wait_ge(s["m_maxed"], K + 1)
                if not first or i >= 2:
                    act.wait_ge(s["m_turned"], K - 1)
                for h in range(M_CHUNK_HEADS):
                    e = nc.scalar.activation(m_e[i % 2][:, h, 0:nk], ps_pair[1 + i % 2][:, h // 2, h % 2 * T:h % 2 * T + nk],
                                             ACT.Exp, bias=m_nmax[:, i % 2, h:h + 1])
                e.then_inc(s["m_exped"], 1)

            def m_save_turned(u, i, first):
                K = u * 2 * M_CHUNKS + i
                hf = i // M_CHUNKS
                act.wait_ge(s["m_turned"], K + 1)
                if not first or i >= 2:
                    act.wait_ge(s["m_pv"], K - 1)
                nc.scalar.copy(m_pT[i % 2][:, 0:hf + 1, :, :].rearrange("p k h q -> p k (h q)"),
                               ps_pair[3][:, 0:hf + 1, :]).then_inc(s["m_tsaved"], 1)

            def m_save_out(u):
                act.wait_ge(s["m_oturned"], u + 1)
                nc.scalar.copy(m_oT[:, :], bank[1][:, 0:T]).then_inc(s["m_otsaved"], 1)

            def mid_unit(u, parity, first, last):
                n = 2 * M_CHUNKS
                for i in range(n):
                    if i == 0 and not last:
                        m_copy(u + 1, False)
                    m_exponentials(u, i, first)
                    if i >= 1:
                        m_save_turned(u, i - 1, first)
                    elif not first:
                        m_save_turned(u - 1, n - 1, False)
                    if i == 2 and not last:
                        m_save_values(u + 1, 1 - parity)
                    if i == 4 and not first:
                        m_save_out(u - 1)

            act.wait_ge(ln_sems["ln_mid"]["scaled"], CHUNKS)
            act.wait_ge(s["m_prepared"], 1)
            m_copy(0, True)
            m_save_values(0, 0)
            each_sequence(act, mid_unit)
            u = B - 1
            m_save_turned(u, 2 * M_CHUNKS - 1, False)
            m_save_out(u)

            one_behind(*ln_scalar(act, ln_sems["ln_out"]))
            stack_body(1)

        @block.vector
        def _(dve):
            def tables(G0):
                dve.wait_ge(s["w_scale_loaded"], G0 * 16 + 16)
                for n, tab in enumerate((tab_a, tab_b)):
                    last = nc.vector.tensor_tensor(tab[:, :, :], rot[:, n, :, :], qk_rows[:, n:n + 1, :].broadcast_to((P, TILES, 2 * DIM_HEAD)), ALU.mult)
                last.then_inc(s["tables_ready"], 1)
                dve.wait_ge(s["tables_ready"], G0 + 1)

            heads = "p (n h d) -> p n h d"

            def sum_exponentials(N, g, used):
                dve.wait_ge(s["exped"], N - 1)
                if used is not None:
                    dve.wait_ge(s["prec_ready"], N - 2)
                nc.vector.tensor_reduce(psum_row[:, :], probs[:, g % 2, :, :], AX_X, ALU.add).then_inc(s["sum_ready"], 1)
                dve.wait_ge(s["sum_ready"], N - 1)
                if used is not None:
                    dve.wait_ge(s["band_ready"], used)
                nc.vector.reciprocal(prec[:, g % 2, :], psum_row[:, :]).then_inc(s["prec_ready"], 1)

            def norm_qk(N, turned):
                dve.wait_ge(s["rotated_ready"], N)
                dve.wait_ge(s["rnorm_ready"], N)
                if turned is not None:
                    dve.wait_ge(s["qk_turned"], turned)
                by_head = "p (n d) -> p n d"
                nc.vector.scalar_tensor_tensor(out=qk_norm[:, :].rearrange(by_head, d=DIM_HEAD),
                                               in0=rnorm[:, :].unsqueeze(2).broadcast_to((P, TILES * 2 * GH, DIM_HEAD)), scalar=INV_NORM_MAX,
                                               in1=rotated[:, :].rearrange(by_head, d=DIM_HEAD),
                                               op0=ALU.min, op1=ALU.mult).then_inc(s["qk_normed"], 1)

            def shift_scores(N, g, placed):
                dve.wait_ge(s["s_ready"], N)
                sc = bank[3].rearrange("p (i k) -> p i k", k=KEYS)
                nc.vector.tensor_reduce(nmax[:, :], sc, AX_X, ALU.max, negate=True).then_inc(s["max_ready"], 1)
                dve.wait_ge(s["max_ready"], N)
                if placed is not None:
                    dve.wait_ge(s["band_ready"], placed)
                nc.vector.tensor_tensor(probs[:, (g - 1) % 2, :, :], sc, nmax[:, :].unsqueeze(2).broadcast_to((P, 2 * GH, KEYS)),
                                        ALU.add).then_inc(s["shifted_scores"], 1)

            def update_x(count, u):
                dve.wait_ge(s["y_ready"], count)
                at = xT[:, bass.ds(u * T, T)]
                nc.vector.tensor_tensor(at, bank[7][:, T:2 * T], at, ALU.add).then_inc(s["x_updated"], 1)

            def shift_for_feed(u):
                nc.vector.tensor_copy(f_in[0:64, :], xT[0:64, bass.ds(u * T, T)])
                nc.vector.tensor_copy(f_in[64:P, 1:T], xT[64:P, bass.ds(u * T, T - 1)]).then_inc(s["f_copied"], 1)

            def feed_scale(U, u, G):
                if not old_weights(u, 2):
                    dve.wait_ge(s["w_ln_loaded"], (G + 1) * 16)
                dve.wait_ge(s["f_rstd_ready"], U - 1)
                nc.vector.scalar_tensor_tensor(out=f_scaled[:, :], in0=bank[2][:, 0:T], scalar=ln_cols[:, 0:1], in1=f_rstd[:, :],
                                               op0=ALU.mult, op1=ALU.mult).then_inc(s["f_scaled"], 1)
                dve.wait_ge(s["f_scaled"], U - 1)
                nc.vector.tensor_scalar(f_hi[:, :], f_scaled[:, :], ln_cols[:, 1:2], None, ALU.add).then_inc(s["f_rounded"], 1)
                dve.wait_ge(s["f_rounded"], U - 1)
                nc.vector.scalar_tensor_tensor(out=f_lo[:, :], in0=f_scaled[:, :], scalar=ln_cols[:, 1:2], in1=f_hi[:, :].bitcast(F32),
                                               op0=ALU.add, op1=ALU.subtract).then_inc(s["f_normed"], 1)

            f_at = (bank[2][:, 0:T], bank[2][:, T:2 * T], bank[7][:, T:2 * T])

            def feed_mix(U, u, G):
                if not old_weights(u, 2):
                    dve.wait_ge(s["w_b1_loaded"], (G + 1) * 16)
                dve.wait_ge(s["f_gelued"], U - 1)
                dve.wait_ge(s["f_values"], U - 1)
                for m, rows in enumerate(FFN_ROWS):
                    mix = nc.vector.scalar_tensor_tensor(out=f_h[0:rows, m, :], in0=f_at[m][0:rows, :], scalar=b1[0:rows, 0, m:m + 1],
                                                         in1=f_gelu[0:rows, m, :], op0=ALU.add, op1=ALU.mult)
                mix.then_inc(s["f_mixed"], 1)

            def feed_add(U, u, G):
                if not old_weights(u, 3):
                    dve.wait_ge(s["w_2_loaded"], (G + 1) * 48)
                dve.wait_ge(s["f_y"], U - 2)
                at = xT[:, bass.ds((u + B - 3) % B * T, T)]
                nc.vector.scalar_tensor_tensor(out=at, in0=f_at[0], scalar=b2[:, 0:1], in1=at, op0=ALU.add, op1=ALU.add).then_inc(s["f_x"], 1)

            def stack_body(stack):
                def unit(U, u, G, lag, more):
                    feed = lag >= 2
                    first = lag == 0
                    for g in range(GROUPS):
                        N = U * GROUPS + g
                        stage = stages(g, lag)
                        if g == 0 and lag >= 3:
                            sum_exponentials(N - 1, 3, N - 4)
                        if old_weights(u, 1) and g == 0:
                            tables(G)
                        dve.wait_ge(s["squared"], N + 1)
                        if not (first and g == 0):
                            dve.wait_ge(s["rotated_ready"], N)
                        qk = ps_pair[0][:, :, :].rearrange("p a n -> p (a n)").rearrange(heads, h=GH, d=DIM_HEAD)
                        a4, b4 = (r[:, :].rearrange(heads, h=GH, d=DIM_HEAD) for r in (rot_a, rot_b))
                        ta, tb = (r[:, :, :].rearrange("p a (i d) -> p (a i) d", d=DIM_HEAD).unsqueeze(2) for r in (tab_a, tab_b))
                        nc.vector.tensor_tensor(a4, qk, ta.broadcast_to((P, TILES * 2, GH, DIM_HEAD)), ALU.mult)
                        for half in range(2):
                            own, partner = (slice(x * HALF, (x + 1) * HALF) for x in (half, 1 - half))
                            part = nc.vector.tensor_tensor(b4[:, :, :, own], qk[:, :, :, partner],
                                                           tb[:, :, :, own].broadcast_to((P, TILES * 2, GH, HALF)), ALU.mult)
                        part.then_inc(s["rotated_parts"], 1)
                        if not (first and g == 0):
                            dve.wait_ge(s["sqsum_logged"], N)
                        nc.vector.tensor_reduce(sqsum[:, :], squares[:, :].rearrange("p (n d) -> p n d", d=DIM_HEAD), AX_X,
                                                ALU.add).then_inc(s["sqsum_ready"], 1)
                        if g == 1 and lag >= 3:
                            feed_add(U, u, G)
                        if stage[2] and not (feed and g == 3):
                            sum_exponentials(N, g, N - 3 if lag >= 1 else None)
                        if g == 0 and lag >= 2:
                            update_x(2 * U - 2, (u + B - 2) % B)
                            dve.wait_ge(s["x_updated"], 2 * U - 2)
                        if g == 2 and lag >= 1:
                            update_x(2 * U - 1, (u + B - 1) % B)
                        if g == 2 and feed:
                            feed_scale(U, u, G)
                        if g == 3 and feed:
                            feed_mix(U, u, G)
                        if g == 3:
                            dve.wait_ge(s["v_ready"], N + 1)
                            nc.vector.tensor_copy(vals[:, g, :, :].rearrange("p a n -> p (a n)"), bank[6]).then_inc(s["v_saved"], 1)
                        if g == 0:
                            dve.wait_ge(s["rotated_parts"], N + 1)
                            if stage[1]:
                                dve.wait_ge(s["qk_normed"], N)
                            nc.vector.tensor_tensor(rotated[:, :], rot_a[:, :], rot_b[:, :], ALU.add).then_inc(s["rotated_ready"], 1)
                        if not (g == 3 and feed):
                            norm_qk(N + 1, N if stage[1] else None)
                        if g == 0 and lag >= 2:
                            shift_for_feed((u + B - 2) % B)
                        if stage[1]:
                            shift_scores(N, g, N - 2 if stage[3] else None)
                        if g == 3 and feed:
                            norm_qk(N + 1, N)

                each_unit(dve, stack, unit)

                U = (stack + 1) * UNITS
                G = stack * DEPTH + DEPTH
                N = U * GROUPS
                sum_exponentials(N - 1, 3, N - 4)
                sum_exponentials(N, 0, N - 3)
                feed_add(U, 0, G)
                update_x(2 * U - 2, B - 2)
                dve.wait_ge(s["x_updated"], 2 * U - 2)
                shift_for_feed(B - 2)
                shift_scores(N, 0, N - 2)
                sum_exponentials(N + 1, 1, N - 2)
                update_x(2 * U - 1, B - 1)
                feed_scale(U, 0, G)
                feed_mix(U, 0, G)
                update_x(2 * U, B - 1)
                dve.wait_ge(s["x_updated"], 2 * U)
                shift_for_feed(B - 1)
                feed_add(U + 1, 1, G)
                dve.wait_ge(s["f_x"], final_before(stack) + U - 2)
                add_half(range(CHUNKS - 1))
                feed_scale(U + 1, 1, G)
                if stack == 1:
                    keep_results(range(CHUNKS - 1))
                feed_mix(U + 1, 1, G)
                feed_add(U + 2, 2, G)

            last_chunk = range(CHUNKS - 1, CHUNKS)

            def add_half(chunks):
                for c in chunks:
                    at = slice(c * CHUNK, (c + 1) * CHUNK)
                    nc.vector.scalar_tensor_tensor(out=baseT[:, at], in0=xT[:, at], scalar=0.5, in1=baseT[:, at],
                                                   op0=ALU.mult, op1=ALU.add).then_inc(s["out_summed"], 1)

            def keep_results(chunks):
                for c in chunks:
                    dve.wait_ge(s["out_turned"], c + 1)
                    nc.vector.tensor_copy(by_token[:, c * CHUNK:(c + 1) * CHUNK], bank[4 + c]).then_inc(s["out_kept"], 1)

            dve.wait_ge(s["consts_loaded"], 16 * len(values))
            nc.vector.tensor_copy(ident_bf[:, :], ident[:, :])
            nc.vector.tensor_copy(mask_bf[:, :, :].rearrange("p f k -> p (f k)"), cst["mask"][:, :])
            nc.vector.tensor_copy(causal_bf[:, :], cst["causal"][:, :])
            nc.vector.memset(eps_col[:, :], LN_EPS)
            nc.vector.memset(rnorm_col[:, :], 0.5 * LN2 * float(np.log2(SQ_SCALE)))
            nc.vector.memset(kblock[:, :, :, :], 0.0)
            nc.vector.memset(band[:, :, :, :], 0.0)
            nc.vector.memset(xs_hi[:, :].bitcast(F32), 0.0)
            nc.vector.memset(xs_lo[:, :].bitcast(F32), 0.0)
            nc.vector.memset(f_in[:, :], 0.0)
            nc.vector.memset(ones_row[:, :], 1.0).then_inc(s["consts_ready"], 1)
            dve.wait_ge(s["consts_ready"], 1)
            for c in range(CHUNKS):
                dve.wait_ge(s["x_turned"], c + 1)
                nc.vector.tensor_copy(baseT[:, c * CHUNK:(c + 1) * CHUNK], bank[4 + c]).then_inc(s["x_kept"], 1)
            ln_vector(dve, ln_sems["ln_in"], xT)
            dve.wait_ge(ln_sems["ln_in"]["scaled"], CHUNKS)
            dve.sem_inc(s["f_x"], 1)
            stack_body(0)
            dve.wait_ge(s["f_x"], final_before(0) + UNITS)
            add_half(last_chunk)

            ln_vector(dve, ln_sems["ln_mid"], xT)
            dve.wait_ge(s["m_loaded"], 16 * 8)
            pairs = "p (n two) -> p n two"
            for to, frm in ((m_w[:, 1, :], m_w[:, 0, :]), (m_brow[:, 1, :], m_bin[:, 0:128])):
                t2, f2 = to.rearrange(pairs, two=2), frm.rearrange(pairs, two=2)
                nc.vector.tensor_copy(t2[:, :, 0:1], f2[:, :, 1:2])
                nc.vector.tensor_copy(t2[:, :, 1:2], f2[:, :, 0:1])
            nc.vector.tensor_copy(m_brow[:, 0, :], m_bin[:, 0:128])
            for rows, to, frm in ((P, m_w, m_wk[:, 0:32]), (1, m_brow, m_bin[:, 128:160])):
                for rep in range(M_REP):
                    t3 = to[:, 2, :].rearrange("p (g r d) -> p g r d", r=M_REP, d=M_DIM)[:, :, rep, :]
                    s3 = to[:, 3, :].rearrange("p (g r d) -> p g r d", r=M_REP, d=M_DIM)[:, :, rep, :]
                    f3 = frm.rearrange("p (g d) -> p g d", d=M_DIM)
                    nc.vector.tensor_copy(t3, f3)
                    for a in range(2):
                        last = nc.vector.tensor_copy(s3.rearrange("p g (n two) -> p g n two", two=2)[:, :, :, a],
                                                     f3.rearrange("p g (n two) -> p g n two", two=2)[:, :, :, 1 - a])
            nc.vector.memset(m_v[:, :, :, :, M_DIM:M_DIM + 1], 1.0)
            last.then_inc(s["m_prepared"], 1)
            dve.wait_ge(s["m_bturned"], 1)
            nc.vector.tensor_copy(m_bcol[:, :], bank[3][:, 0:4]).then_inc(s["m_bsaved"], 1)
            dve.wait_ge(s["m_bsaved"], 1)

            def m_rotate(u, parity, i, name):
                dve.wait_ge(s["m_" + name], u + 1)
                for v in range(2):
                    n = 2 * i + v
                    part = nc.vector.scalar_tensor_tensor(out=m_rot[:, n * T:(n + 1) * T], in0=bank[1][:, v * T:(v + 1) * T],
                                                          scalar=m_bcol[:, n:n + 1], in1=cst["m_rotary"][:, v * T:(v + 1) * T],
                                                          op0=ALU.add, op1=ALU.mult)
                part.then_inc(s["m_" + name + "parts"], 1)
                dve.wait_ge(s["m_" + name + "parts"], u + 1)
                parts = m_rot.rearrange("p (i v t) -> p i v t", i=2, v=2)
                nc.vector.tensor_tensor(m_rope[:, parity, i, :], parts[:, i, 0, :], parts[:, i, 1, :], ALU.add).then_inc(s["m_" + name + "roped"], 1)

            def m_keys_by_head(u, parity):
                dve.wait_ge(s["m_kroped"], u + 1)
                nc.vector.tensor_tensor(m_kblock[:, parity, :, :], m_rope[:, parity, 1:2, :].broadcast_to((P, M_REP, T)),
                                        cst["own_head"][:, :].unsqueeze(2).broadcast_to((P, M_REP, T)), ALU.mult).then_inc(s["m_kblocked"], 1)

            def m_queries_by_group(u, parity):
                dve.wait_ge(s["m_qroped"], u + 1)
                nc.vector.tensor_tensor(m_qblock[:, parity, :, :], m_rope[:, parity, 0:1, :].broadcast_to((P, M_GROUPS, T)),
                                        cst["own_group"][:, :].unsqueeze(2).broadcast_to((P, M_GROUPS, T)), ALU.mult).then_inc(s["m_qblocked"], 1)

            def m_maxima(u, i):
                K = u * 2 * M_CHUNKS + i
                dve.wait_ge(s["m_scores"], K + 1)
                sc = ps_pair[1 + i % 2][:, :, :].rearrange("p a (h k) -> p (a h) k", h=2)[:, :, 0:(i // M_CHUNKS + 1) * P]
                nc.vector.tensor_reduce(m_nmax[:, i % 2, :], sc, AX_X, ALU.max, negate=True).then_inc(s["m_maxed"], 1)

            def m_outputs(u, first):
                dve.wait_ge(s["m_pv"], (u + 1) * 2 * M_CHUNKS)
                nc.vector.reciprocal(m_rec[:, :].rearrange("p (a h) -> p a h", a=2), m_out[:, :, :, M_DIM]).then_inc(s["m_recd"], 1)
                if not first:
                    dve.wait_ge(s["m_oturned"], u)
                dve.wait_ge(s["m_recd"], u + 1)
                for hf in range(2):
                    o = nc.vector.tensor_tensor(m_o[:, hf, :].rearrange("p (h d) -> p h d", d=M_DIM), m_out[:, hf, :, 0:M_DIM],
                                                m_rec[:, hf * M_HEADS:(hf + 1) * M_HEADS].unsqueeze(2).broadcast_to((P, M_HEADS, M_DIM)), ALU.mult)
                o.then_inc(s["m_osaved"], 1)

            def m_add(u):
                dve.wait_ge(s["m_y"], u + 1)
                at = baseT[:, bass.ds(u * T, T)]
                nc.vector.scalar_tensor_tensor(out=at, in0=bank[1][:, T:2 * T], scalar=m_bo[:, 0:1], in1=at,
                                               op0=ALU.add, op1=ALU.add).then_inc(s["m_x"], 1)

            def mid_unit(u, parity, first, last):
                for i in range(2 * M_CHUNKS):
                    m_maxima(u, i)
                    if i == 1 and not last:
                        m_rotate(u + 1, 1 - parity, 1, "k")
                    if i == 2 and not first:
                        m_outputs(u - 1, isinstance(u, int) and u == 1)
                    if i == 2 and not last:
                        m_keys_by_head(u + 1, 1 - parity)
                    if i == 5 and not first:
                        m_add(u - 1)
                    if i == 3 and not last:
                        m_rotate(u + 1, 1 - parity, 0, "q")
                    if i == 4 and not last:
                        m_queries_by_group(u + 1, 1 - parity)

            m_rotate(0, 0, 1, "k")
            m_keys_by_head(0, 0)
            m_rotate(0, 0, 0, "q")
            m_queries_by_group(0, 0)
            each_sequence(dve, mid_unit)
            m_outputs(B - 1, False)
            m_add(B - 1)

            ln_vector(dve, ln_sems["ln_out"], xT)
            dve.wait_ge(ln_sems["ln_out"]["scaled"], CHUNKS)
            dve.sem_inc(s["f_x"], 1)
            stack_body(1)
            dve.wait_ge(s["f_x"], final_before(1) + 2 * UNITS)
            add_half(last_chunk)
            keep_results(last_chunk)

        @block.gpsimd
        def _(pool):
            def split_weights(G, g):
                cols = slice(g * 3 * GCOLS, (g + 1) * 3 * GCOLS)
                pool.wait_ge(s["w_rounded"], G * GROUPS + g + 1)
                nc.gpsimd.tensor_tensor(w_lo[:, cols], wqkv[:, cols], w_hi[:, cols].bitcast(F32), ALU.subtract).then_inc(s["w_split"], 1)

            def split_first_weights(G):
                pool.wait_ge(s["w_1_rounded"], G + 1)
                nc.gpsimd.tensor_tensor(w1_lo[:, :], w1[:, :], w1_hi[:, :].bitcast(F32), ALU.subtract).then_inc(s["w_1_split"], 1)

            def split_shifted(n, u):
                pool.wait_ge(s["xs_ready"], n + 1)
                nc.gpsimd.tensor_tensor(xs_lo[0:64, :], xT[0:64, bass.ds(u * T, T)], xs_hi[0:64, :].bitcast(F32), ALU.subtract)
                nc.gpsimd.tensor_tensor(xs_lo[64:P, 1:T], xT[64:P, bass.ds(u * T, T - 1)], xs_hi[64:P, 1:T].bitcast(F32),
                                        ALU.subtract).then_inc(s["xs_split"], 1)

            def place_probs(N, g, summed, used):
                pool.wait_ge(s["rotated_ready"], summed)
                pool.wait_ge(s["prec_ready"], N - 1)
                if used is not None:
                    pool.wait_ge(s["pt_ready"], used)
                for j in range(P // WINDOW):
                    r = slice(j * WINDOW, (j + 1) * WINDOW)
                    to = nc.gpsimd.tensor_tensor(band[r, g % 2, :, j * WINDOW:j * WINDOW + KEYS], probs[r, g % 2, :, :],
                                                 prec[r, g % 2, :].unsqueeze(2).broadcast_to((WINDOW, 2 * GH, KEYS)), ALU.mult)
                to.then_inc(s["band_ready"], 1)

            def unit(stack, U, u, G, lag, more):
                for g in range(GROUPS):
                    N = U * GROUPS + g
                    stage = stages(g, lag)
                    weights = prepared_weights(u, g, more)
                    if stage[3]:
                        pool.wait_ge(s["band_ready"], N - 2)
                    if weights:
                        split_weights(G + weights[1], weights[0])
                    if g > 0:
                        pool.wait_ge(s["rotated_parts"], N + 1)
                        if stage[1]:
                            pool.wait_ge(s["qk_normed"], N)
                        nc.gpsimd.tensor_tensor(rotated[:, :], rot_a[:, :], rot_b[:, :], ALU.add).then_inc(s["rotated_ready"], 1)
                    if g == GROUPS - 1:
                        pool.wait_ge(s["rotated_ready"], N + 1)
                        split_shifted(U + stack + 1, (u + 1) % B)
                        pool.wait_ge(s["xs_split"], U + stack + 2)
                    if stage[2]:
                        if weights:
                            pool.wait_ge(s["w_split"], (G + weights[1]) * GROUPS + weights[0] + 1)
                        if isinstance(u, int) and u == 2 and g == 1:
                            split_first_weights(G)
                            pool.wait_ge(s["w_1_split"], G + 1)
                        place_probs(N, g, N + 1, N - 3 if stage[4] else None)

            def stack_body(stack):
                if stack == 0:
                    split_weights(0, 0)
                    split_weights(0, 1)
                    pool.wait_ge(s["w_split"], 2)
                split_shifted(stack * UNITS + stack, 0)
                pool.wait_ge(s["xs_split"], stack * UNITS + stack + 1)
                each_unit(pool, stack, lambda *args: unit(stack, *args))
                N = (stack + 1) * UNITS * GROUPS
                place_probs(N, 0, N, N - 3)
                place_probs(N + 1, 1, N, N - 2)

            pool.wait_ge(s["consts_ready"], 1)
            stack_body(0)
            stack_body(1)


_AS_THEY_ARE = ["L0_attn_x", "L0_attn_Wq", "L0_attn_bq", "L0_attn_Wk", "L0_attn_bk", "L0_attn_Wv", "L0_attn_bv", "L0_attn_Wo",
                "L0_attn_bo", "L0_ffn_Wo", "L0_ffn_W1", "L0_ffn_W2"]


def laid_out(inputs):
    arrays = {n: np.ascontiguousarray(inputs[n]) for n in _AS_THEY_ARE}
    w = np.asarray(inputs["L0_ffn_Wqkv"])
    w = w.reshape(DEPTH, DIM, 3, GROUPS, GCOLS).transpose(0, 1, 3, 2, 4)
    arrays["wqkv"] = np.ascontiguousarray(w.reshape(DEPTH, DIM, 3 * INNER))
    scales = np.stack([np.asarray(inputs[n]) for n in ("L0_ffn_q_scale", "L0_ffn_k_scale")], axis=1)
    swapped = scales.reshape(DEPTH, 2, 2, HALF)[:, :, ::-1].reshape(DEPTH, 2, DIM_HEAD)
    rows = np.stack([scales, swapped], axis=1).reshape(DEPTH, 1, 2, 2 * DIM_HEAD)
    arrays["qk_rows"] = np.ascontiguousarray(np.tile(rows, (1, P, 1, 1)))
    cols = [np.asarray(inputs[n]) for n in ("L0_ffn_ln_g", "L0_ffn_ln_b", "L0_ffn_b2")]
    b1 = np.asarray(inputs["L0_ffn_b1"])
    for part in range(2):
        for m, rows in enumerate(FFN_ROWS):
            o = part * DIM_INNER + m * P
            cols.append(np.pad(b1[:, o:o + rows], ((0, 0), (0, P - rows))))
    arrays["ffn_cols"] = np.ascontiguousarray(np.stack(cols, axis=2))
    return arrays


def kernel(**inputs):
    import concourse.bacc as _bacc
    from concourse.bass_utils import run_bass_kernel_spmd as _run

    nc = _bacc.Bacc("TRN2", target_bir_lowering=False, num_devices=1)
    arrays, io = {}, {}
    for name, a in laid_out(inputs).items():
        arrays[f"in_{name}"] = a
        io[name] = nc.dram_tensor(f"in_{name}", a.shape, mybir.dt.from_np(a.dtype), kind="ExternalInput").ap()
    io["out"] = nc.dram_tensor("out_0", (B, T, DIM), F32, kind="ExternalOutput").ap()
    build_macaron(nc, io)
    r = _run(nc, [arrays], core_ids=[0])
    return r.results[0]["out_0"]
```
